# Optimizing a Trainium2 kernel written in Bass

```python
import numpy as np
import jax
import jax.numpy as jnp

def _softmax(x, axis=-1):
    return jax.nn.softmax(x, axis=axis)

def _gelu(x):
    return jax.nn.gelu(x, approximate=True)

def _silu(x):
    return jax.nn.silu(x)

def _sigmoid(x):
    return jax.nn.sigmoid(x)

def _layernorm(x, axis=-1, eps=1e-05):
    m = jnp.mean(x, axis=axis, keepdims=True)
    v = jnp.var(x, axis=axis, keepdims=True)
    return (x - m) / jnp.sqrt(v + eps)

def _scatter_add(tgt, idx, src, axis=0):
    return tgt.at[idx].add(src)

def _segment_sum(src, seg, n):
    return jax.ops.segment_sum(src, seg, n)
kernel_name = 'mk_seq_preln_d1_jaxref_r8_1f655e'

def setup_inputs(seed: int=0):
    np.random.seed(seed)
    _w = jnp.asarray

    def _L0_attn_setup():
        import jax, jax.numpy as jnp
        import numpy as np
        B, T, D, H = (4, 256, 128, 16)
        HD = D // H
        EPS = 1e-05
        NEG = 10000000000.0
        key = jax.random.key(seed)
        k1, k2, k3 = jax.random.split(key, 3)
        return {'target': jax.random.normal(k1, (B, T, D), dtype=jnp.float32), 'w_qkv': jax.random.normal(k2, (D, 3 * D), dtype=jnp.float32) * 0.02, 'w_proj': jax.random.normal(k3, (D, D), dtype=jnp.float32) * (0.02 / np.sqrt(24.0)), 'b_proj': jnp.zeros((D,), dtype=jnp.float32), 'ln_gamma': jnp.ones((D,), dtype=jnp.float32), 'ln_beta': jnp.zeros((D,), dtype=jnp.float32)}
    _L0_attn_in = _L0_attn_setup()

    def _L0_ffn_setup():
        import jax, jax.numpy as jnp
        import numpy as np
        D_MODEL = 128
        D_HIDDEN = 512
        NUM_BANKS = 16
        NUM_SELECTED = 2
        key = jax.random.key(seed)
        ks = jax.random.split(key, 7)
        s = 0.02
        return {'tensor': jax.random.normal(ks[0], (4, 128, D_MODEL), dtype=jnp.float32), 'Wr': jax.random.normal(ks[1], (D_MODEL, NUM_BANKS), dtype=jnp.float32) * s, 'br': jnp.zeros((NUM_BANKS,), dtype=jnp.float32), 'W1': jax.random.normal(ks[2], (NUM_BANKS, D_MODEL, D_HIDDEN), dtype=jnp.float32) * s, 'b1': jnp.zeros((NUM_BANKS, D_HIDDEN), dtype=jnp.float32), 'W2': jax.random.normal(ks[3], (NUM_BANKS, D_HIDDEN, D_MODEL), dtype=jnp.float32) * s, 'b2': jnp.zeros((NUM_BANKS, D_MODEL), dtype=jnp.float32)}
    _L0_ffn_in = _L0_ffn_setup()
    _d = {'L0_attn_target': _L0_attn_in['target'], 'L0_attn_w_qkv': _L0_attn_in['w_qkv'], 'L0_attn_w_proj': _L0_attn_in['w_proj'], 'L0_attn_b_proj': _L0_attn_in['b_proj'], 'L0_attn_ln_gamma': _L0_attn_in['ln_gamma'], 'L0_attn_ln_beta': _L0_attn_in['ln_beta'], 'L0_ffn_Wr': _L0_ffn_in['Wr'], 'L0_ffn_br': _L0_ffn_in['br'], 'L0_ffn_W1': _L0_ffn_in['W1'], 'L0_ffn_b1': _L0_ffn_in['b1'], 'L0_ffn_W2': _L0_ffn_in['W2'], 'L0_ffn_b2': _L0_ffn_in['b2']}
    _x0 = _d['L0_attn_target']
    _d['L0_attn_target'] = jax.random.normal(jax.random.fold_in(jax.random.key(seed), 1), (8, 512, 128), dtype=_x0.dtype)
    del _x0
    return _d

def reference(L0_attn_target, L0_attn_w_qkv, L0_attn_w_proj, L0_attn_b_proj, L0_attn_ln_gamma, L0_attn_ln_beta, L0_ffn_Wr, L0_ffn_br, L0_ffn_W1, L0_ffn_b1, L0_ffn_W2, L0_ffn_b2):

    def _L0_attn_ref(target, w_qkv, w_proj, b_proj, ln_gamma, ln_beta):
        import jax, jax.numpy as jnp
        import numpy as np
        B, T, D, H = (4, 256, 128, 16)
        HD = D // H
        EPS = 1e-05
        NEG = 10000000000.0
        b, t, d = target.shape
        resid = target
        qkv = target @ w_qkv
        q, k, v = jnp.split(qkv, 3, axis=-1)
        q = q.reshape(b, t, H, HD).transpose(0, 2, 1, 3)
        k = k.reshape(b, t, H, HD).transpose(0, 2, 1, 3)
        v = v.reshape(b, t, H, HD).transpose(0, 2, 1, 3)
        scores = jnp.einsum('bhqd,bhkd->bhqk', q, k) * (1.0 / np.sqrt(HD))
        causal = (jnp.arange(t)[:, None] >= jnp.arange(t)[None, :]).astype(scores.dtype)
        scores = scores * causal - (1.0 - causal) * NEG
        attn = jax.nn.softmax(scores, axis=-1)
        out = jnp.einsum('bhqk,bhkd->bhqd', attn, v)
        out = out.transpose(0, 2, 1, 3).reshape(b, t, d)
        proj = out @ w_proj + b_proj
        x = proj + resid
        mu = jnp.mean(x, axis=-1, keepdims=True)
        var = jnp.var(x, axis=-1, keepdims=True)
        return (x - mu) * jax.lax.rsqrt(var + EPS) * ln_gamma + ln_beta

    def _L0_ffn_ref(tensor, Wr, br, W1, b1, W2, b2):
        import jax, jax.numpy as jnp
        import numpy as np
        D_MODEL = 128
        D_HIDDEN = 512
        NUM_BANKS = 16
        NUM_SELECTED = 2
        logits = jnp.einsum('bsd,de->bse', tensor, Wr) + br
        probs = jax.nn.softmax(logits, axis=-1)
        topv, topi = jax.lax.top_k(probs, NUM_SELECTED)
        gate = jnp.sum(jax.nn.one_hot(topi, NUM_BANKS, dtype=tensor.dtype) * topv[..., None], axis=-2)
        h = jax.nn.relu(jnp.einsum('bsd,edh->bseh', tensor, W1) + b1)
        y = jnp.einsum('bseh,ehm->bsem', h, W2) + b2
        out = jnp.einsum('bse,bsem->bsm', gate, y)
        return out
    x = L0_attn_target
    x = x + _L0_attn_ref(_layernorm(x, axis=-1), L0_attn_w_qkv, L0_attn_w_proj, L0_attn_b_proj, L0_attn_ln_gamma, L0_attn_ln_beta)
    x = x + _L0_ffn_ref(_layernorm(x, axis=-1), L0_ffn_Wr, L0_ffn_br, L0_ffn_W1, L0_ffn_b1, L0_ffn_W2, L0_ffn_b2)
    return x

_drawn_inputs = setup_inputs


def setup_inputs(seed=0):
    import zlib

    import numpy as np

    out = dict(_drawn_inputs(seed))
    spreads = {'L0_attn_b_proj': (0.0, 0.1),
     'L0_attn_ln_gamma': (1.0, 0.2),
     'L0_attn_ln_beta': (0.0, 0.1),
     'L0_ffn_br': (0.0, 0.8),
     'L0_ffn_b1': (0.0, 0.8),
     'L0_ffn_b2': (0.0, 0.8)}
    factors = {'L0_attn_w_qkv': 8.0,
     'L0_attn_w_proj': 8.0,
     'L0_ffn_Wr': 7.653,
     'L0_ffn_W1': 8.0,
     'L0_ffn_W2': 8.0}
    for name, (base, spread) in spreads.items():
        noise = np.random.default_rng([zlib.crc32(name.encode()), seed]).standard_normal(out[name].shape)
        drawn = base * np.exp(spread * noise) if base else spread * noise
        out[name] = jnp.asarray(drawn.astype(out[name].dtype))
    for name, factor in factors.items():
        out[name] = (out[name] * factor).astype(out[name].dtype)
    return out
```

```python
from contextlib import ExitStack

import concourse.bass as bass
from concourse import mybir

F32 = mybir.dt.float32
BF16 = mybir.dt.bfloat16
I32 = mybir.dt.int32
U32 = mybir.dt.uint32
ALU = mybir.AluOpType
ACT = mybir.ActivationFunctionType
AX = mybir.AxisListType

P = 128
EPS = 1e-5
MASKED = -1e30
SKIP = 1 << 20

SLOT = [
    ("S", 0), ("U", 0), ("x", 0), ("S", 1), ("PVL", 2), ("S", 2), ("U", 1), ("x", 1), ("S", 3), ("SEL", 0),
    ("PVL", 3), ("M", 0), ("S", 4), ("OE", 0), ("U", 2), ("x", 2), ("S", 5), ("U", 3), ("x", 3), ("S", 6),
    ("N", 0), ("PV", 0), ("S", 7), ("SEL", 1), ("U", 4), ("x", 4), ("S", 8), ("U", 5), ("SPLIT", 0),
    ("S", 9), ("SEL", 2), ("PV", 1), ("x", 5), ("S", 10), ("SEL", 3), ("x", 6),
]
EXTRA = {
    (0, 0): [("LOADX", 2), ("RELOAD", -1), ("STB", 1), ("T", -2)],
    (0, 3): [("LN1S", 2)],
    (0, 5): [("LN1C", 2), ("XB", -1)],
    (1, 0): [("R", -2), ("LN1N", 2)],
    (1, 1): [("TOP", -2)],
    (1, 2): [("A", -1)],
    (1, 3): [("X", 2)],
    (1, 5): [("Q", 2)],
    (1, 6): [("Q2", 2), ("PROJ", -1)],
    (2, 0): [("K", 2), ("LN2S", -1)],
    (2, 2): [("K2", 2), ("LN2C", -1)],
    (2, 3): [("STA", 2)],
    (2, 4): [("LN2N", -1)],
    (2, 5): [("X1", -1)],
    (3, 0): [("C", -2), ("LN3S", -1)],
    (3, 1): [("STORE1", -1)],
    (3, 2): [("LN3C", -1)],
    (3, 3): [("SCATTER", -2)],
    (3, 4): [("LN3N", -1)],
    (3, 5): [("V", 1)],
}


def moe_block(nc, x_in, w_qkv, w_proj, b_proj, gamma, beta, w_r, b_r, w1, b1, w2, b2, out):
    B, T, D = x_in.shape
    E, _, HID = w1.shape
    H, HD, G = 16, D // 16, 4
    HH = H // 2
    NT = T // P
    NS = H // G
    ROWS = T * B + P
    TILES = (2 * B * T + E * (P - 1)) // P
    TILES += TILES % 2
    HC = HID // P
    RW = D + 2
    KQ = 9 * HD
    MROW = 96
    SCALE = float(HD) ** -0.5
    assert D == P and NT == 4 and NS == 4 and B % 2 == 0

    routed = nc.dram_tensor("routed_rows", [E * ROWS + P, RW], F32).ap()
    results = nc.dram_tensor("result_rows", [2 * B * T, D], F32).ap()
    xn_store = nc.dram_tensor("xn_store", [B, T, D], F32).ap()

    ctx = ExitStack()
    with ctx:
        def sb(name, shape, dt=F32):
            return ctx.enter_context(nc.sbuf_tensor(name, shape, dt))

        def sem(name):
            return ctx.enter_context(nc.semaphore(name))

        ident = sb("ident", [P, P])
        identb = sb("identb", [P, P], BF16)
        maskneg = sb("maskneg", [P, 2, P], BF16)
        before = sb("before", [P, P], BF16)
        onesb = sb("onesb", [P, P], BF16)
        iota_i = sb("iota_i", [P, 64], I32)
        iota_e = sb("iota_e", [P, E])
        region = sb("region", [P, E])
        tile_no = sb("tile_no", [P, 1])
        upto = sb("upto", [P, E, E])
        res_row = sb("res_row", [P, NT])
        neg_half = sb("neg_half", [P, NT])
        w_raw = sb("w_raw", [P, 3 * D])
        wq_p = sb("wq_p", [P, D])
        wk_p = sb("wk_p", [P, D])
        wp = sb("wp", [P, D])
        wr = sb("wr", [P, E])
        brb = sb("brb", [P, E])
        gammab = sb("gammab", [P, D])
        betab = sb("betab", [P, D])
        bprojb = sb("bprojb", [P, D])
        b1T = sb("b1T", [P, E * HC])
        b1row = sb("b1row", [E * HC, P])
        w1s = sb("w1s", [P, E, HID])

        xin = [sb(f"xin{i}", [P, NT, D]) for i in range(2)]
        xn = sb("xn", [P, NT, D])
        xnT = [sb(f"xnT{i}", [P, T]) for i in range(2)]
        parts = [sb(f"parts{i}", [P, 3, T], BF16) for i in range(2)]
        resid = sb("resid", [P, T])
        qs = sb("qs", [P, 2, H, T], BF16)
        ks = sb("ks", [P, 2, H, T], BF16)
        va = [sb(f"va{i}", [P, NT, H, HD + 1]) for i in range(2)]
        nmax = [sb(f"nmax{i}", [P, NT, G]) for i in range(2)]
        nres = sb("nres", [P, NT, G])
        nsplit = [sb(f"nsplit{i}", [P, NT, 3, G], BF16) for i in range(2)]
        nmT = [sb(f"nmT{i}", [3 * G, T], BF16) for i in range(2)]
        pr = sb("pr", [P, G * (512 + 384 + 256 + 128)])
        oT = sb("oT", [P, T])
        rsum = sb("rsum", [P, NT, G])
        on = [sb(f"on{i}", [P, NT, D]) for i in range(2)]
        aT = sb("aT", [P, T])
        xr = sb("xr", [P, NT, D])
        xnr = sb("xnr", [P, NT, D])
        z = sb("z", [P, NT, D])
        x1w = sb("x1w", [P, NT, D])
        x1 = sb("x1", [P, B * NT, D])
        stats = sb("stats", [P, 3, NT, 6])
        mv = sb("mv", [P, 3, NT, 2])
        veps = sb("veps", [P, 3, NT])
        rstd = sb("rstd", [P, 3, NT])
        nmr0 = sb("nmr0", [P, 3, NT])
        nmr = sb("nmr", [P, 3, NT])

        rows = [[sb(f"rows{i}{c}", [P, NT, RW]) for c in range(2)] for i in range(2)]
        tT = sb("tT", [P, T])
        logit = sb("logit", [P, NT, E])
        lmax = sb("lmax", [P, NT])
        lsub = sb("lsub", [P, NT, E])
        pe_ = sb("pexp", [P, NT, E])
        psum_ = sb("psum_", [P, NT])
        prec = sb("prec", [P, NT])
        prob = sb("prob", [P, NT, E])
        top_v = sb("top_v", [P, NT, 8])
        top_i = sb("top_i", [P, NT, 8], U32)
        top_f = sb("top_f", [P, NT, 8])
        hot = sb("hot", [P, 2, NT, E])
        hotb = sb("hotb", [P, NT, E], BF16)
        place = sb("place", [P, NT, E])
        picked = sb("picked", [P, 2, NT, E])
        dest_f = sb("dest_f", [P, 2, NT])
        dest = [sb(f"dest{i}", [P, 2, NT], U32) for i in range(2)]
        base = sb("base", [P, E])

        cnt = sb("cnt", [P, E])
        cnt_i = sb("cnt_i", [P, E], I32)
        nt_i = sb("nt_i", [P, E], I32)
        nt_f = sb("nt_f", [P, E])
        cum3 = sb("cum3", [P, E, E])
        cum = sb("cum", [P, E])
        done = sb("done", [P, E])
        skipped = sb("skipped", [P, E])
        tv = sb("tv", [P, 6])
        table = sb("table", [1, 2, P], I32)
        pad_at = sb("pad_at", [1, E], I32)
        pad_rows = sb("pad_rows", [P, RW])
        XG = 4
        xg = [sb(f"xg{i}", [P, RW]) for i in range(XG)]
        xgT = [sb(f"xgT{i}", [P, P]) for i in range(2)]
        w1c = [parts[i][:, :, :].rearrange("p c t -> p (c t)").bitcast(F32)[:, 0:HID] for i in range(2)]
        hid = [xnT[i][:, :].rearrange("p (c s) -> p c s", c=HC) for i in range(2)]
        yb = [sb(f"yb{i}", [P, D]) for i in range(2)]
        yg = [sb(f"yg{i}", [P, D]) for i in range(2)]
        ydest = [sb(f"ydest{i}", [P, 1], U32) for i in range(2)]

        w2s = qs[:, :, :, :].rearrange("p a h t -> p (a h t)").bitcast(F32).rearrange("p (e c m) -> p e c m", e=E, c=HC)
        b2b = pr[:, 0:E * D].rearrange("p (e m) -> p e m", e=E)
        fin = ks[:, :, :, :].rearrange("p a h t -> p (a h t)").bitcast(F32).rearrange("p (n i c d) -> p n i c d", n=B, i=NT, c=2)
        OFF = [0, G * 512, G * 896, G * 1152]
        QN = [T - P * k for k in range(NT)]
        prob_of = [pr[:, OFF[k]:OFF[k] + G * QN[k]].rearrange("p (h q) -> p h q", h=G) for k in range(NT)]

        pU = ctx.enter_context(nc.psum_tensor("pU", [P, 2, 2, 512], F32))
        pS = ctx.enter_context(nc.psum_tensor("pS", [P, 2, 512], F32))
        pO = ctx.enter_context(nc.psum_tensor("pO", [P, 512], F32))
        pM = ctx.enter_context(nc.psum_tensor("pM", [P, 512], F32))
        pMb = pM[:, :].bitcast(BF16)

        s_pc = sem("const_steps")
        s_const = sem("const_made")
        s_dz = sem("stacks_zeroed")
        s_b1t = sem("b1_product")
        s_zero = sem("zeroed")
        s_w = sem("small_weights_in")
        s_w1 = sem("w1_in")
        s_w2 = sem("w2_in")
        s_wperm = sem("q_k_weights_ordered")
        s_b1 = sem("b1_turned")
        s_x = [sem(f"x_in{i}") for i in range(2)]
        s_stat = [sem(f"ln{k}_stats") for k in range(3)]
        s_mv = [sem(f"ln{k}_mean_var") for k in range(3)]
        s_coef = [sem(f"ln{k}_coef") for k in range(3)]
        s_norm = [sem(f"ln{k}_normed") for k in range(3)]
        s_xout = sem("xn_stored")
        s_re = sem("x_and_xn_back")
        s_xb = sem("biases_added")
        s_xt = sem("xn_turned")
        s_xnT = sem("xnT_ready")
        s_qk = sem("q_k_product")
        s_hi = sem("q_k_high")
        s_res = sem("q_k_residue")
        s_mid = sem("q_k_middle")
        s_lo = sem("q_k_low")
        s_st = [sem(f"stack_in{i}") for i in range(2)]
        s_vmm = sem("v_product")
        s_v = sem("v_ready")
        s_u = sem("unit_scores")
        s_red = sem("unit_maxima")
        s_spl = sem("maxima_split")
        s_mt = sem("maxima_turned")
        s_nmT = sem("maxima_rows")
        s_mr = [sem(f"maxima_in_stack{i}") for i in range(2)]
        s_s = sem("bank_scores")
        s_e = sem("bank_exp")
        s_sel = sem("masked")
        s_pv = sem("pv_done")
        s_oT = sem("o_copied")
        s_nt = sem("o_turned")
        s_rs = sem("o_reciprocals")
        s_n = sem("o_normed")
        s_at = sem("o_rows_turned")
        s_aT = sem("aT_ready")
        s_pj = sem("proj_product")
        s_z = sem("z_ready")
        s_x1 = sem("x1_steps")
        s_x1d = sem("x1_kept")
        s_row = sem("second_rows")
        s_tt = sem("t_turned")
        s_tT = sem("tT_ready")
        s_r = sem("router_product")
        s_lg = sem("router_steps")
        s_le = sem("router_exp")
        s_cp = sem("prefix_product")
        s_cs = sem("place_steps")
        s_sc = [sem(f"scattered{i}") for i in range(2)]
        LG, CS, ST = 11, 7, 16 * 18
        s_tb = sem("table_steps")
        TB_PAD, TB_COLS, TB_END = 1, 16, 17
        s_tm = sem("table_product")
        s_pad = sem("padding_stored")
        s_g = [sem(f"rows_in{i}") for i in range(XG)]
        s_gt = sem("rows_turned")
        s_gT = sem("xgT_ready")
        s_wc = sem("w1_of_tile")
        s_h = sem("hidden_product")
        s_ha = sem("hidden_act")
        s_hv = sem("hidden_act_vector")
        s_y = sem("y_product")
        s_yb = sem("y_bias")
        s_yi = sem("y_rows_known")
        s_yg = sem("y_gated")
        s_ys = [sem(f"y_stored{i}") for i in range(2)]
        s_fin = [sem(f"results_in{i}") for i in range(B)]
        s_f1 = sem("results_added")
        s_f2 = sem("x1_added")
        s_out = sem("out_stored")

        def due(n):
            return max(n, 0) if isinstance(n, int) else n

        def held(eng, n):
            if isinstance(n, int):
                return due(n)
            n = eng.to_reg(n)
            eng.wait_ge(s_const, 1)
            return n

        def steps(eng, step):
            def has(b):
                return lambda k: 0 <= b + k < B
            for b in range(-2, 2):
                step(b, b % 2, has(b))
            with eng.Fori(1, B // 2 - 1) as i:
                step(2 * i, 0, lambda k: True)
                step(2 * i + 1, 1, lambda k: True)
            for b in range(B - 2, B + 2):
                step(b, b % 2, has(b))

        def walk(has, do):
            for g in range(NS):
                for name, i in SLOT:
                    if name == "x":
                        for what, k in EXTRA.get((g, i), []):
                            if has(k):
                                do(what, k, g)
                    elif name in ("U", "SPLIT"):
                        if has(1):
                            do(name, i, g)
                    elif name == "M":
                        if has(1) if g else has(0):
                            do(name, i, g)
                    elif name in ("PVL", "OE", "N"):
                        if has(0) if g else has(-1):
                            do(name, i, g)
                    elif has(0):
                        do(name, i, g)

        block = ctx.enter_context(nc.Block())

        @block.sync
        def _(sp):
            w_cols = w_qkv
            small = [(w_raw[:, :], w_cols), (wp[:, :], w_proj), (wr[:, :], w_r),
                     (brb[:, :], b_r.partition_broadcast(P)), (gammab[:, :], gamma.partition_broadcast(P)),
                     (betab[:, :], beta.partition_broadcast(P)), (bprojb[:, :], b_proj.partition_broadcast(P)),
                     (b1row[:, :], b1.rearrange("e (c p) -> (e c) p", p=P))]
            for dst, src in small:
                sp.dma_start(dst, src).then_inc(s_w, 16)
            sp.wait_ge(s_zero, 1)

            def stack(n, q, half):
                sp.wait_ge(s_lo, held(sp, 2 * n + 2))
                sp.wait_ge(s_s, held(sp, 44 * (n - 2) + 22 * (half + 1)))
                sp.wait_ge(s_st[half], held(sp, ST * n))
                heads, lanes = slice(HH * half, HH * half + HH), slice(64 * half, 64 * half + 64)
                for i in range(3):
                    for j in range(3):
                        r = 24 * i + 8 * j
                        sp.dma_start(qs[r:r + 8, q, heads, :], parts[0][lanes, i, :]).then_inc(s_st[half], 16)
                        sp.dma_start(ks[r:r + 8, q, heads, :], parts[1][lanes, j, :]).then_inc(s_st[half], 16)

            def step(b, pb, has):
                def do(name, k, g):
                    if name == "LOADX":
                        n, q = b + k, (pb + k) % 2
                        if not isinstance(n, int) or n >= 2:
                            sp.wait_ge(s_norm[0], held(sp, n - 1))
                        sp.dma_start(xin[q][:, :, :], x_in[n].rearrange("(i p) d -> p i d", p=P)).then_inc(s_x[q], 16)
                    elif name == "X":
                        n = b + k
                        sp.wait_ge(s_norm[0], held(sp, n + 1))
                        sp.dma_start(xn_store[n].rearrange("(i p) d -> p i d", p=P), xn[:, :, :]).then_inc(s_xout, 16)
                    elif name == "RELOAD":
                        n = b + k
                        sp.wait_ge(s_xout, held(sp, 16 * (n + 1)))
                        sp.wait_ge(s_x1, held(sp, 2 * n))
                        sp.dma_start(xr[:, :, :], x_in[n].rearrange("(i p) d -> p i d", p=P)).then_inc(s_re, 16)
                        sp.dma_start(xnr[:, :, :], xn_store[n].rearrange("(i p) d -> p i d", p=P)).then_inc(s_re, 16)
                    elif name == "STA":
                        stack(b + k, pb, 0)
                    elif name == "STB":
                        stack(b + k, (pb + 1) % 2, 1)
                    elif name == "M":
                        n1 = 4 * b + (4 + g - 1)
                        q, gm = (g - 1) % 2, (g - 1) % 4
                        pq = (pb + 1) % 2 if g else pb
                        sp.wait_ge(s_nmT, held(sp, n1 + 1))
                        if not isinstance(b, int) or n1 >= 2:
                            sp.wait_ge(s_mr[q], held(sp, 8 * (n1 - q)))
                        sp.dma_start(qs[MROW:MROW + 3, pq, G * gm:G * gm + G, :], nmT[q][:, :]).then_inc(s_mr[q], 16)
                    elif name == "STORE1":
                        n = b + k
                        sp.wait_ge(s_x1, held(sp, 2 * n + 2))
                        sp.dma_start(x1[:, 4 * n:4 * n + 4, :] if isinstance(n, int) else x1[:, bass.ds(4 * n, 4), :],
                                     x1w[:, :, :]).then_inc(s_x1d, 16)
                walk(has, do)

            steps(sp, step)

            sp.wait_ge(s_s, 11 * NS * B)
            for q in range(2):
                sp.wait_ge(s_mr[q], held(sp, 16 * NS * B // 2))
            for e in range(0, E, 4):
                sp.dma_start(w2s[:, e:e + 4, :, :].rearrange("p e c m -> p (e c) m"),
                             w2[e:e + 4].rearrange("e (c p) m -> p (e c) m", p=P)).then_inc(s_w2, 16)
            sp.wait_ge(s_pv, 4 * NS * B)
            sp.dma_start(b2b, b2.rearrange("e m -> (e m)").partition_broadcast(P).rearrange("p (e m) -> p e m", e=E))\
                .then_inc(s_w2, 16)

            sp.dma_start(routed[E * ROWS:E * ROWS + P, :], pad_rows[:, :]).then_inc(s_pad, 16)
            sp.wait_ge(s_tb, TB_PAD)
            for e in range(E):
                at = sp.value_load(pad_at[0:1, e:e + 1], min_val=0, max_val=(e + 1) * ROWS - P)
                sp.dma_start(routed[bass.ds(at, P), :], pad_rows[:, :]).then_inc(s_pad, 16)
            for q in range(2):
                sp.wait_ge(s_sc[q], held(sp, 16 * 2 * NT * B // 2))
            sp.wait_ge(s_pad, held(sp, 16 * (E + 1)))
            sp.wait_ge(s_tb, TB_END)

            def load_rows(t, q):
                if not isinstance(t, int) or t >= XG:
                    sp.wait_ge(s_yg, held(sp, t - XG + 1))
                    sp.wait_ge(s_yi, held(sp, t - XG + 1))
                at = sp.value_load(table[0:1, 1, t:t + 1] if isinstance(t, int) else table[0:1, 1, bass.ds(t, 1)],
                                   min_val=0, max_val=E * ROWS)
                sp.dma_start(xg[q][:, :], routed[bass.ds(at, P), :]).then_inc(s_g[q], 16)

            for t in range(XG):
                load_rows(t, t)
            with sp.Fori(XG, TILES, XG) as t:
                for q in range(XG):
                    load_rows(t + q, q)

            for q in range(2):
                sp.wait_ge(s_ys[q], held(sp, 16 * TILES // 2))
            for n in range(B):
                sp.dma_start(fin[:, n].rearrange("p i c d -> p i (c d)"),
                             results.rearrange("(n i p c) d -> n p i (c d)", i=NT, p=P, c=2)[n]).then_inc(s_fin[n], 16)
            for n in range(B):
                sp.wait_ge(s_f2, held(sp, n + 1))
                sp.dma_start(out[n].rearrange("(i p) d -> p i d", p=P), x1[:, NT * n:NT * n + NT, :]).then_inc(s_out, 16)
            sp.wait_ge(s_out, 16 * B)

        @block.gpsimd
        def _(pool):
            pool.memset(ident[:, :], 0.0).then_inc(s_pc, 1)
            pool.memset(maskneg[:, :, :], 0.0).then_inc(s_pc, 1)
            pool.memset(before[:, :], 1.0).then_inc(s_pc, 1)
            pool.memset(onesb[:, :], 1.0).then_inc(s_pc, 1)
            pool.memset(neg_half[:, :], -0.5).then_inc(s_pc, 1)
            pool.memset(upto[:, :, :], 1.0).then_inc(s_pc, 1)
            pool.iota(iota_i[:, 0:E], pattern=[[1, E]], base=0, channel_multiplier=0).then_inc(s_pc, 1)
            pool.iota(iota_i[:, E:2 * E], pattern=[[ROWS, E]], base=0, channel_multiplier=0).then_inc(s_pc, 1)
            pool.iota(iota_i[:, 2 * E:2 * E + NT], pattern=[[2 * P, NT]], base=0, channel_multiplier=2).then_inc(s_pc, 1)
            pool.iota(iota_i[:, 3 * E:3 * E + 1], pattern=[[0, 1]], base=0, channel_multiplier=1).then_inc(s_pc, 1)
            pool.memset(pad_rows[:, 0:D], 0.0).then_inc(s_pc, 1)
            pool.memset(pad_rows[:, D:D + 1], float(SKIP)).then_inc(s_pc, 1)
            pool.memset(pad_rows[:, D + 1:D + 2], 0.0).then_inc(s_pc, 1)
            pool.wait_ge(s_pc, 13)
            pool.affine_select(out=ident[:, :], in_=ident[:, :], compare_op=ALU.not_equal, fill=1.0, base=0,
                               pattern=[[-1, P]], channel_multiplier=1).then_inc(s_pc, 1)
            pool.affine_select(out=maskneg[:, :, :], in_=maskneg[:, :, :], compare_op=ALU.is_ge, fill=MASKED, base=0,
                               pattern=[[0, 2], [-1, P]], channel_multiplier=1).then_inc(s_pc, 1)
            pool.affine_select(out=before[:, :], in_=before[:, :], compare_op=ALU.is_ge, fill=0.0, base=-1,
                               pattern=[[1, P]], channel_multiplier=-1).then_inc(s_pc, 1)
            pool.affine_select(out=upto[:, :, :], in_=upto[:, :, :], compare_op=ALU.is_ge, fill=0.0, base=0,
                               pattern=[[1, E], [-1, E]], channel_multiplier=0).then_inc(s_pc, 1)
            pool.tensor_copy(iota_e[:, :], iota_i[:, 0:E]).then_inc(s_pc, 1)
            pool.tensor_copy(region[:, :], iota_i[:, E:2 * E]).then_inc(s_pc, 1)
            pool.tensor_copy(base[:, :], iota_i[:, E:2 * E]).then_inc(s_pc, 1)
            pool.tensor_copy(res_row[:, :], iota_i[:, 2 * E:2 * E + NT]).then_inc(s_pc, 1)
            pool.tensor_copy(tile_no[:, :], iota_i[:, 3 * E:3 * E + 1]).then_inc(s_pc, 1)
            pool.wait_ge(s_pc, 22)
            pool.tensor_copy(identb[:, :], ident[:, :]).then_inc(s_const, 1)
            pool.wait_ge(s_const, 1)

            def step(b, pb, has):
                def do(name, k, g):
                    if name == "SPLIT":
                        n1, q = 4 * b + (4 + g), g % 2
                        pool.wait_ge(s_red, held(pool, 6 * n1 + 6))
                        pool.wait_ge(s_mt, held(pool, n1 - 1))
                        pool.tensor_copy(nsplit[q][:, :, 0, :], nmax[q][:, :, :]).then_inc(s_spl, 1)
                        pool.wait_ge(s_spl, held(pool, 4 * n1 + 1))
                        pool.tensor_tensor(nres[:, :, :], nmax[q][:, :, :], nsplit[q][:, :, 0, :], ALU.subtract).then_inc(s_spl, 1)
                        pool.wait_ge(s_spl, held(pool, 4 * n1 + 2))
                        pool.tensor_copy(nsplit[q][:, :, 1, :], nres[:, :, :]).then_inc(s_spl, 1)
                        pool.wait_ge(s_spl, held(pool, 4 * n1 + 3))
                        pool.tensor_tensor(nsplit[q][:, :, 2, :], nres[:, :, :], nsplit[q][:, :, 1, :], ALU.subtract).then_inc(s_spl, 1)
                    elif name == "SEL":
                        n = 4 * b + g
                        pool.wait_ge(s_e, held(pool, 11 * n + [4, 8, 10, 11][k]))
                        diag = prob_of[k][:, :, 0:P]
                        pool.affine_select(out=diag, in_=diag, compare_op=ALU.is_ge, fill=0.0, base=0,
                                           pattern=[[0, G], [1, P]], channel_multiplier=-1).then_inc(s_sel, 1)
                    elif name in ("Q2", "K2"):
                        n, c = b + k, int(name == "K2")
                        pool.wait_ge(s_mid, held(pool, 2 * n + c + 1))
                        pool.tensor_tensor(parts[c][:, 2, :], resid[:, :], parts[c][:, 1, :], ALU.subtract).then_inc(s_lo, 1)
                    elif name in ("LN1C", "LN2C", "LN3C"):
                        n, j = b + k, int(name[2]) - 1
                        pool.wait_ge(s_mv[j], held(pool, n + 1))
                        pool.wait_ge(s_norm[j], held(pool, n))
                        pool.tensor_scalar(veps[:, j, :], mv[:, j, :, 1], EPS, None, ALU.add).then_inc(s_coef[j], 1)
                        pool.wait_ge(s_coef[j], held(pool, 4 * n + 1))
                        pool.tensor_tensor(rstd[:, j, :], veps[:, j, :], neg_half[:, :], ALU.pow).then_inc(s_coef[j], 1)
                        pool.wait_ge(s_coef[j], held(pool, 4 * n + 2))
                        pool.tensor_tensor(nmr0[:, j, :], mv[:, j, :, 0], rstd[:, j, :], ALU.mult).then_inc(s_coef[j], 1)
                        pool.wait_ge(s_coef[j], held(pool, 4 * n + 3))
                        pool.tensor_scalar(nmr[:, j, :], nmr0[:, j, :], -1.0, None, ALU.mult).then_inc(s_coef[j], 1)
                    elif name == "XB":
                        n = b + k
                        pool.wait_ge(s_re, held(pool, 32 * n + 32))
                        pool.tensor_tensor(xnr[:, :, :], xnr[:, :, :], bprojb[:, None, :].to_broadcast([P, NT, D]), ALU.add).then_inc(s_xb, 1)
                        pool.tensor_tensor(xr[:, :, :], xr[:, :, :], betab[:, None, :].to_broadcast([P, NT, D]), ALU.add).then_inc(s_xb, 1)
                    elif name == "X1":
                        n = b + k
                        pool.wait_ge(s_norm[1], held(pool, n + 1))
                        pool.tensor_tensor(z[:, :, :], z[:, :, :], gammab[:, None, :].to_broadcast([P, NT, D]), ALU.mult).then_inc(s_x1, 1)
                        pool.wait_ge(s_x1, held(pool, 2 * n + 1))
                        pool.wait_ge(s_xb, held(pool, 2 * n + 2))
                        pool.wait_ge(s_norm[2], held(pool, n))
                        pool.wait_ge(s_x1d, held(pool, 16 * n))
                        pool.tensor_tensor(x1w[:, :, :], z[:, :, :], xr[:, :, :], ALU.add).then_inc(s_x1, 1)
                    elif name == "SCATTER":
                        n, q = b + k, pb
                        pool.wait_ge(s_cs, held(pool, CS * n + 6))
                        pool.wait_ge(s_row, held(pool, n + 1))
                        for i in range(NT):
                            for c in range(2):
                                pool.indirect_dma_start(
                                    routed[:, :], bass.IndirectOffsetOnAxis(ap=dest[q][:, c, i:i + 1], axis=0),
                                    rows[q][c][:, i, :], None).then_inc(s_sc[q], 16)
                walk(has, do)

            steps(pool, step)

            def store(t, q):
                pool.wait_ge(s_yg, held(pool, t + 1))
                pool.wait_ge(s_yi, held(pool, t + 1))
                pool.indirect_dma_start(results[:, :], bass.IndirectOffsetOnAxis(ap=ydest[q][:, 0:1], axis=0), yg[q][:, :], None,
                                        bounds_check=2 * B * T - 1, oob_is_err=False).then_inc(s_ys[q], 16)
            with pool.Fori(0, TILES, 2) as t:
                store(t, 0)
                store(t + 1, 1)

        @block.scalar
        def _(act):
            for e in range(0, E, 4):
                act.dma_start(w1s[:, e:e + 4, :], w1[e:e + 4].rearrange("e p h -> p e h")).then_inc(s_w1, 16)

            def norm(j, n, dst, src):
                act.wait_ge(s_coef[j], 4 * n + 4)
                for i in range(NT):
                    last = act.activation(dst[:, i, :], src[:, i, :], ACT.Identity, bias=nmr[:, j, i:i + 1], scale=rstd[:, j, i:i + 1])
                last.then_inc(s_norm[j], 1)

            def step(b, pb, has):
                def do(name, k, g):
                    n = b + k if isinstance(k, int) else None
                    if name == "S":
                        slot, i = 4 * b + g, k
                        kb, h = ([(0, j) for j in range(4)] + [(1, j) for j in range(4)] + [(2, 0), (2, 2), (3, 0)])[i]
                        nh = [1, 1, 2, 4][kb]
                        if h == 0:
                            act.wait_ge(s_pv, due(4 * slot - 3 + kb))
                        act.wait_ge(s_s, 11 * slot + i + 1)
                        act.activation(prob_of[kb][:, h:h + nh, :],
                                       pS[:, (g + i) % 2, 0:nh * QN[kb]].rearrange("p (h q) -> p h q", h=nh),
                                       ACT.Exp, scale=SCALE).then_inc(s_e, 1)
                    elif name == "OE":
                        slot = 4 * b + (g - 1)
                        act.wait_ge(s_pv, 4 * slot + 4)
                        act.wait_ge(s_nt, due(slot))
                        act.copy(oT[:, :], pO[:, :]).then_inc(s_oT, 1)
                    elif name == "M":
                        n1, q = 4 * b + (4 + g - 1), (g - 1) % 2
                        act.wait_ge(s_mt, n1 + 1)
                        act.wait_ge(s_mr[q], due(8 * (n1 - q)))
                        act.copy(nmT[q][:, :], pMb[0:3 * G, 0:T]).then_inc(s_nmT, 1)
                    elif name == "X":
                        act.wait_ge(s_xt, n + 1)
                        act.wait_ge(s_vmm, due(n - 1))
                        act.copy(xnT[pb][:, :], pM[:, :]).then_inc(s_xnT, 1)
                    elif name in ("Q", "K"):
                        c = int(name == "K")
                        act.wait_ge(s_qk, 2 * n + c + 1)
                        for half in range(2):
                            act.wait_ge(s_st[half], due(ST * n))
                        act.copy(parts[c][:, 0, :], pM[:, :]).then_inc(s_hi, 1)
                    elif name in ("Q2", "K2"):
                        c = int(name == "K2")
                        act.wait_ge(s_res, 2 * n + c + 1)
                        act.copy(parts[c][:, 1, :], resid[:, :]).then_inc(s_mid, 1)
                    elif name == "V":
                        q = (pb + 1) % 2
                        act.wait_ge(s_vmm, n + 1)
                        act.wait_ge(s_pv, due(16 * (n - 1)))
                        act.copy(va[q][:, :, :, 0:HD], pM[:, :].rearrange("p (i h d) -> p i h d", i=NT, h=H)).then_inc(s_v, 1)
                    elif name == "LN1N":
                        act.wait_ge(s_xt, due(n))
                        act.wait_ge(s_xout, due(16 * n))
                        norm(0, n, xn, xin[pb])
                    elif name == "LN2N":
                        norm(1, n, z, z)
                    elif name == "LN3N":
                        q = (pb + 1) % 2
                        act.wait_ge(s_sc[q], due(64 * (n - q)))
                        norm(2, n, rows[q][0][:, :, 0:D], x1w)
                        act.wait_ge(s_norm[2], n + 1)
                        act.copy(rows[q][1][:, :, 0:D], rows[q][0][:, :, 0:D]).then_inc(s_row, 1)
                    elif name == "A":
                        act.wait_ge(s_at, n + 1)
                        act.wait_ge(s_pj, due(n))
                        act.copy(aT[:, :], pM[:, :]).then_inc(s_aT, 1)
                    elif name == "T":
                        act.wait_ge(s_tt, n + 1)
                        act.wait_ge(s_r, due(n))
                        act.copy(tT[:, :], pM[:, :]).then_inc(s_tT, 1)
                    elif name == "TOP":
                        act.wait_ge(s_lg, LG * n + 3)
                        act.activation(pe_[:, :, :], lsub[:, :, :], ACT.Exp).then_inc(s_le, 1)
                walk(has, do)

            steps(act, step)

            act.wait_ge(s_b1, 1)

            def tile(t, q):
                e = act.value_load(table[0:1, 0, t:t + 1] if isinstance(t, int) else table[0:1, 0, bass.ds(t, 1)], min_val=0, max_val=E - 1)
                act.wait_ge(s_h, t + 1)
                if not isinstance(t, int) or t >= 2:
                    act.wait_ge(s_y, due(t - 1))
                for c in range(2):
                    last = act.activation(hid[q % 2][:, c, :], pU[:, q % 2, 0, c * P:(c + 1) * P], ACT.Relu,
                                          bias=b1T[:, bass.ds(e * HC + c, 1)])
                last.then_inc(s_ha, 1)

            def gate(t, q):
                act.wait_ge(s_yb, t + 1)
                if not isinstance(t, int) or t >= 2:
                    act.wait_ge(s_ys[q % 2], due(8 * (t - q % 2)))
                act.activation(yg[q % 2][:, :], yb[q % 2][:, :], ACT.Identity, scale=xg[q][:, D + 1:D + 2]).then_inc(s_yg, 1)

            act.wait_ge(s_tb, TB_END)
            tile(0, 0)
            for t in range(1, XG):
                tile(t, t)
                gate(t - 1, t - 1)
            with act.Fori(XG, TILES, XG) as t:
                for q in range(XG):
                    tile(t + q, q)
                    gate(t + (q - 1), (q - 1) % XG)
            gate(TILES - 1, XG - 1)

        @block.tensor
        def _(pe):
            last_use = [(s_const, 1)]

            def last_left(s, n):
                before_, last_use[0] = last_use[0], (s, n)
                return before_

            pe.wait_ge(s_const, 1)
            pe.wait_ge(s_w, 16 * 8)
            pe.wait_ge(*last_left(s_b1, 1))
            pe.transpose(pM[:, 0:E * HC], b1row[:, :], ident[0:E * HC, 0:E * HC]).then_inc(s_b1t, 1)
            pe.wait_ge(s_zero, 1)
            pe.wait_ge(s_wperm, 2)

            def turn(src, s):
                for i in range(NT):
                    last = pe.transpose(pM[:, i * P:(i + 1) * P], src(i), ident[:, :])
                last.then_inc(s, 1)

            def step(b, pb, has):
                if has(0):
                    last_use[0] = (s_v, b + 1)

                def pv(slot, j, gm, kb, pvp):
                    pe.wait_ge(s_sel, 4 * slot + kb + 1)
                    if kb == 0:
                        pe.wait_ge(s_oT, due(slot))
                    for h in range(G):
                        last = pe.matmul(pO[32 * h:32 * h + HD + 1, kb * P:T], va[pvp][:, kb, G * gm + h, :], prob_of[kb][:, h, :],
                                         start=(kb == 0), stop=(kb == NT - 1), skip_group_check=True)
                    last.then_inc(s_pv, 1)

                def do(name, k, g):
                    n = b + k
                    if name == "S":
                        slot, i = 4 * b + g, k
                        if i == 0:
                            pe.wait_ge(s_mr[g % 2], due(8 * (slot - g % 2) + 16))
                        pe.wait_ge(s_e, due(11 * slot + i - 1))
                        kb, h = ([(0, j) for j in range(4)] + [(1, j) for j in range(4)] + [(2, 0), (2, 2), (3, 0)])[i]
                        nh = [1, 1, 2, 4][kb]
                        for j in range(nh):
                            last = pe.matmul(pS[:, (g + i) % 2, j * QN[kb]:(j + 1) * QN[kb]],
                                             ks[:, pb, G * g + h + j, kb * P:(kb + 1) * P],
                                             qs[:, pb, G * g + h + j, kb * P:T], start=True, stop=True)
                        last.then_inc(s_s, 1)
                    elif name == "U":
                        u, slot = k, 4 * b + (4 + g)
                        q, p1 = u % 2, (pb + 1) % 2
                        if u == 0:
                            pe.wait_ge(s_st[g // 2], ST * b + 2 * ST)
                        pe.wait_ge(s_red, due(6 * slot + u - 1))
                        pair, kind = u // 3, u % 3

                        def scores(dst, h, qt, start):
                            pe.matmul(dst, qs[0:MROW, p1, h, qt * P:(qt + 1) * P], ks[0:MROW, p1, h, 0:(qt + 1) * P],
                                      start=start, stop=False, skip_group_check=True)

                        def mask(dst, m):
                            return pe.matmul(dst, identb[:, :], maskneg[:, 0:m, :], start=False, stop=True, skip_group_check=True)

                        for j in range(2):
                            h = G * g + 2 * pair + j
                            if kind == 0:
                                scores(pU[:, q, j, :], h, 3, True)
                                last = mask(pU[:, q, j, 3 * P:4 * P], 1)
                            elif kind == 1:
                                scores(pU[:, q, j, 0:3 * P], h, 2, True)
                                scores(pU[:, q, j, 3 * P:4 * P], h, 0, False)
                                last = mask(pU[:, q, j, 2 * P:4 * P], 2)
                            else:
                                scores(pU[:, q, 0, 2 * j * P:(2 * j + 2) * P], h, 1, j == 0)
                                last = mask(pU[:, q, 0, (2 * j + 1) * P:(2 * j + 2) * P], 1)
                        last.then_inc(s_u, 1)
                    elif name == "PV":
                        if k == 0 and g == 0:
                            pe.wait_ge(s_v, b + 1)
                        pv(4 * b + g, None, g, k, pb)
                    elif name == "PVL":
                        pv(4 * b + (g - 1), None, (g - 1) % 4, k, pb if g else (pb + 1) % 2)
                    elif name == "M":
                        n1, q = 4 * b + (4 + g - 1), (g - 1) % 2
                        pe.wait_ge(s_spl, 4 * n1 + 4)
                        pe.wait_ge(*last_left(s_nmT, n1 + 1))
                        for i in range(NT):
                            last = pe.transpose(pMb[0:3 * G, i * P:(i + 1) * P], nsplit[q][:, i, :, :].rearrange("p c h -> p (c h)"), identb[:, :])
                        last.then_inc(s_mt, 1)
                    elif name == "N":
                        slot = 4 * b + (g - 1)
                        pe.wait_ge(s_oT, slot + 1)
                        pe.wait_ge(*last_left(s_n, slot + 1))
                        turn(lambda i: oT[:, i * P:(i + 1) * P], s_nt)
                    elif name == "X":
                        pe.wait_ge(s_norm[0], n + 1)
                        pe.wait_ge(*last_left(s_xnT, n + 1))
                        turn(lambda i: xn[:, i, :], s_xt)
                    elif name in ("Q", "K"):
                        c = int(name == "K")
                        pe.wait_ge(s_xnT, n + 1)
                        pe.wait_ge(*last_left(s_res, 2 * n + c + 1))
                        pe.matmul(pM[:, :], (wk_p if c else wq_p)[:, :], xnT[pb][:, :], start=True, stop=True).then_inc(s_qk, 1)
                    elif name == "V":
                        pe.wait_ge(*last_left(s_v, n + 1))
                        for i in range(NT):
                            last = pe.matmul(pM[:, i * P:(i + 1) * P], xnT[(pb + 1) % 2][:, i * P:(i + 1) * P], w_raw[:, 2 * D:3 * D], start=True, stop=True)
                        last.then_inc(s_vmm, 1)
                    elif name == "A":
                        q = (pb + 1) % 2
                        pe.wait_ge(s_n, 4 * n + 4)
                        pe.wait_ge(*last_left(s_aT, n + 1))
                        turn(lambda i: on[q][:, i, :], s_at)
                    elif name == "PROJ":
                        pe.wait_ge(s_aT, n + 1)
                        pe.wait_ge(*last_left(s_z, n + 1))
                        for i in range(NT):
                            last = pe.matmul(pM[:, i * P:(i + 1) * P], aT[:, i * P:(i + 1) * P], wp[:, :], start=True, stop=True)
                        last.then_inc(s_pj, 1)
                    elif name == "T":
                        pe.wait_ge(s_norm[2], n + 1)
                        pe.wait_ge(*last_left(s_tT, n + 1))
                        turn(lambda i: rows[pb][0][:, i, 0:D], s_tt)
                    elif name == "R":
                        pe.wait_ge(s_tT, n + 1)
                        pe.wait_ge(*last_left(s_lg, LG * n + 1))
                        for i in range(NT):
                            last = pe.matmul(pM[:, i * E:(i + 1) * E], tT[:, i * P:(i + 1) * P], wr[:, :], start=True, stop=True)
                        last.then_inc(s_r, 1)
                    elif name == "C":
                        pe.wait_ge(s_lg, LG * n + 11)
                        pe.wait_ge(*last_left(s_cs, CS * n + 2))
                        for i in range(NT):
                            pe.matmul(pM[:, i * E:(i + 1) * E], before[:, :], hotb[:, i, :], start=(i == 0), stop=False, skip_group_check=True)
                            for j in range(i):
                                pe.matmul(pM[:, i * E:(i + 1) * E], onesb[:, :], hotb[:, j, :], start=False, stop=False, skip_group_check=True)
                        for j in range(NT):
                            last = pe.matmul(pM[:, NT * E:(NT + 1) * E], onesb[:, :], hotb[:, j, :], start=False, stop=(j == NT - 1), skip_group_check=True)
                        last.then_inc(s_cp, 1)
                walk(has, do)

            steps(pe, step)

            pe.wait_ge(s_tb, TB_COLS)
            pe.wait_ge(*last_use[0])
            for j in range(2):
                last = pe.matmul(pM[0:1, j * P:(j + 1) * P], tv[:, 4 + j:5 + j], ident[:, :], start=True, stop=True)
            last.then_inc(s_tm, 1)
            pe.wait_ge(s_tb, TB_END)
            pe.wait_ge(s_w1, 16 * 4)
            pe.wait_ge(s_w2, 16 * 5)

            def expert(t):
                return pe.value_load(table[0:1, 0, t:t + 1] if isinstance(t, int) else table[0:1, 0, bass.ds(t, 1)], min_val=0, max_val=E - 1)

            def turn_rows(t, q):
                pe.wait_ge(s_g[q], due(4 * (t - q) + 16))
                pe.wait_ge(s_gT, due(t))
                pe.transpose(pM[:, 0:P], xg[q][:, 0:D], ident[:, :]).then_inc(s_gt, 1)

            def first(t, q):
                pe.wait_ge(s_gT, t + 1)
                pe.wait_ge(s_wc, t + 1)
                if not isinstance(t, int) or t >= 2:
                    pe.wait_ge(s_ha, due(t - 1))
                    pe.wait_ge(s_hv, due(t - 1))
                for c in range(HC):
                    last = pe.matmul(pU[:, q % 2, c // 2, (c % 2) * P:(c % 2 + 1) * P], w1c[q % 2][:, c * P:(c + 1) * P],
                                     xgT[q % 2][:, :], start=True, stop=True)
                last.then_inc(s_h, 1)

            def second(t, q):
                e = expert(t)
                pe.wait_ge(s_ha, t + 1)
                pe.wait_ge(s_hv, t + 1)
                if not isinstance(t, int) or t >= 2:
                    pe.wait_ge(s_yb, due(t - 1))
                for c in range(HC):
                    last = pe.matmul(pS[:, q % 2, 0:D], hid[q % 2][:, c, :], w2s[:, bass.ds(e, 1), c, :].rearrange("p e m -> p (e m)"), start=(c == 0), stop=(c == HC - 1))
                last.then_inc(s_y, 1)

            turn_rows(0, 0)
            first(0, 0)
            turn_rows(1, 1)
            for t in range(XG):
                turn_rows(t + 2, (t + 2) % XG)
                first(t + 1, (t + 1) % XG)
                second(t, t)
            with pe.Fori(XG, TILES - XG, XG) as t:
                for q in range(XG):
                    turn_rows(t + (q + 2), (q + 2) % XG)
                    first(t + (q + 1), (q + 1) % XG)
                    second(t + q, q)
            for t in range(TILES - XG, TILES):
                if t + 2 < TILES:
                    turn_rows(t + 2, (t + 2) % XG)
                if t + 1 < TILES:
                    first(t + 1, (t + 1) % XG)
                second(t, t % XG)

        @block.vector
        def _(dve):
            dve.memset(pO[:, :], 0.0)
            for tile_ in va:
                dve.memset(tile_[:, :, :, HD:HD + 1], 1.0)
            for stack in (qs, ks):
                dve.memset(stack[64:P, :, :, :].rearrange("p a h t -> p (a h t)").bitcast(F32), 0.0).then_inc(s_dz, 1)
            dve.wait_ge(s_dz, 2)
            dve.memset(ks[MROW:MROW + 3, :, :, :].rearrange("p a h t -> p (a h t)"), 1.0).then_inc(s_zero, 1)
            dve.wait_ge(s_w, 16 * 8)
            for j, w in enumerate((wq_p, wk_p)):
                dve.tensor_copy(w[:, :].rearrange("p (g d h) -> p g d h", g=2, d=HD),
                                w_raw[:, j * D:(j + 1) * D].rearrange("p (g h d) -> p g d h", g=2, h=HH)).then_inc(s_wperm, 1)
            dve.wait_ge(s_b1t, 1)
            dve.tensor_copy(b1T[:, :], pM[:, 0:E * HC]).then_inc(s_b1, 1)
            dve.wait_ge(s_const, 1)

            def step(b, pb, has):
                def do(name, k, g):
                    n = b + k
                    if name == "U":
                        u, slot, q = k, 4 * b + (4 + g), g % 2
                        if u == 0:
                            dve.wait_ge(s_spl, due(4 * slot - 4))
                        dve.wait_ge(s_u, 6 * slot + u + 1)
                        pair, kind = u // 3, u % 3
                        hs = slice(2 * pair, 2 * pair + 2)
                        if kind == 0:
                            last = dve.tensor_reduce(nmax[q][:, 3, hs], pU[:, u % 2, :, :], AX.X, ALU.max, negate=True)
                        elif kind == 1:
                            dve.tensor_reduce(nmax[q][:, 2, hs], pU[:, u % 2, :, 0:3 * P], AX.X, ALU.max, negate=True)
                            last = dve.tensor_reduce(nmax[q][:, 0, hs], pU[:, u % 2, :, 3 * P:4 * P], AX.X, ALU.max, negate=True)
                        else:
                            last = dve.tensor_reduce(nmax[q][:, 1, hs], pU[:, u % 2, 0, :].rearrange("p (h k) -> p h k", h=2), AX.X, ALU.max, negate=True)
                        last.then_inc(s_red, 1)
                    elif name == "N":
                        slot, gm, q = 4 * b + (g - 1), (g - 1) % 4, pb if g else (pb + 1) % 2
                        o4 = pM[:, :].rearrange("p (i h c) -> p i h c", i=NT, h=G)
                        dve.wait_ge(s_nt, slot + 1)
                        dve.reciprocal(rsum[:, :, :], o4[:, :, :, HD]).then_inc(s_rs, 1)
                        dve.wait_ge(s_rs, slot + 1)
                        if gm == 0:
                            dve.wait_ge(s_at, due((b if g else b - 1) - 1))
                        dve.tensor_tensor(on[q][:, :, 32 * gm:32 * gm + 32].rearrange("p i (h d) -> p i h d", h=G), o4[:, :, :, 0:HD],
                                          rsum[:, :, :, None].to_broadcast([P, NT, G, HD]), ALU.mult).then_inc(s_n, 1)
                    elif name in ("Q", "K"):
                        c = int(name == "K")
                        dve.wait_ge(s_hi, 2 * n + c + 1)
                        dve.wait_ge(s_lo, 2 * n + c)
                        dve.tensor_tensor(resid[:, :], pM[:, :], parts[c][:, 0, :], ALU.subtract).then_inc(s_res, 1)
                    elif name in ("LN1S", "LN2S", "LN3S"):
                        j = int(name[2]) - 1
                        if j == 0:
                            src = xin[pb]
                            dve.wait_ge(s_x[pb], due(8 * (n - pb) + 16))
                        elif j == 1:
                            src = z
                            dve.wait_ge(s_z, n + 1)
                        else:
                            src = x1w
                            dve.wait_ge(s_x1, 2 * n + 2)
                        dve.wait_ge(s_mv[j], due(n))
                        for i in range(NT):
                            last = dve.bn_stats(stats[:, j, i, :], src[:, i, :])
                        last.then_inc(s_stat[j], 1)
                        dve.wait_ge(s_coef[j], held(dve, 4 * n))
                        dve.wait_ge(s_stat[j], held(dve, n + 1))
                        for i in range(NT):
                            last = dve.bn_aggr(mv[:, j, i, :], stats[:, j, i, :])
                        last.then_inc(s_mv[j], 1)
                    elif name == "PROJ":
                        dve.wait_ge(s_pj, n + 1)
                        dve.wait_ge(s_xb, 2 * n + 1)
                        dve.wait_ge(s_x1, due(2 * n))
                        dve.tensor_tensor(z[:, :, :], pM[:, :].rearrange("p (i d) -> p i d", i=NT), xnr[:, :, :], ALU.add).then_inc(s_z, 1)
                    elif name == "R":
                        a = LG * n
                        dve.wait_ge(s_r, n + 1)
                        dve.wait_ge(s_cs, due(CS * n))
                        dve.tensor_tensor(logit[:, :, :], pM[:, 0:NT * E].rearrange("p (i e) -> p i e", i=NT),
                                          brb[:, None, :].to_broadcast([P, NT, E]), ALU.add).then_inc(s_lg, 1)
                        dve.wait_ge(s_lg, a + 1)
                        dve.tensor_reduce(lmax[:, :], logit[:, :, :], AX.X, ALU.max, negate=True).then_inc(s_lg, 1)
                        dve.wait_ge(s_lg, a + 2)
                        dve.tensor_tensor(lsub[:, :, :], logit[:, :, :], lmax[:, :, None].to_broadcast([P, NT, E]), ALU.add).then_inc(s_lg, 1)
                    elif name == "TOP":
                        a = LG * n
                        dve.wait_ge(s_le, n + 1)
                        dve.tensor_reduce(psum_[:, :], pe_[:, :, :], AX.X, ALU.add).then_inc(s_lg, 1)
                        dve.wait_ge(s_lg, a + 4)
                        dve.reciprocal(prec[:, :], psum_[:, :]).then_inc(s_lg, 1)
                        dve.wait_ge(s_lg, a + 5)
                        dve.tensor_tensor(prob[:, :, :], pe_[:, :, :], prec[:, :, None].to_broadcast([P, NT, E]), ALU.mult).then_inc(s_lg, 1)
                        dve.wait_ge(s_lg, held(dve, a + 6))
                        for i in range(NT):
                            last = dve.max(top_v[:, i, :], prob[:, i, :])
                        last.then_inc(s_lg, 1)
                        dve.wait_ge(s_lg, held(dve, a + 7))
                        for i in range(NT):
                            last = dve.max_index(top_i[:, i, :], top_v[:, i, :], prob[:, i, :])
                        last.then_inc(s_lg, 1)
                        dve.wait_ge(s_lg, a + 8)
                        dve.tensor_copy(top_f[:, :, :], top_i[:, :, :]).then_inc(s_lg, 1)
                        dve.wait_ge(s_lg, a + 9)
                        for c in range(2):
                            last = dve.tensor_tensor(hot[:, c, :, :], iota_e[:, None, :].to_broadcast([P, NT, E]),
                                                     top_f[:, :, c:c + 1].to_broadcast([P, NT, E]), ALU.is_equal)
                        last.then_inc(s_lg, 1)
                        dve.wait_ge(s_lg, a + 10)
                        dve.wait_ge(s_cp, due(n))
                        dve.tensor_tensor(hotb[:, :, :], hot[:, 0, :, :], hot[:, 1, :, :], ALU.add).then_inc(s_lg, 1)
                    elif name == "C":
                        a, q = CS * n, pb
                        dve.wait_ge(s_cp, n + 1)
                        dve.wait_ge(s_cs, due(a))
                        dve.tensor_tensor(place[:, :, :], pM[:, 0:NT * E].rearrange("p (i e) -> p i e", i=NT),
                                          base[:, None, :].to_broadcast([P, NT, E]), ALU.add).then_inc(s_cs, 1)
                        dve.wait_ge(s_cs, a + 1)
                        dve.tensor_tensor(base[:, :], pM[:, NT * E:(NT + 1) * E], base[:, :], ALU.add).then_inc(s_cs, 1)
                        dve.wait_ge(s_cs, a + 2)
                        for c in range(2):
                            last = dve.tensor_tensor(picked[:, c, :, :], place[:, :, :], hot[:, c, :, :], ALU.mult)
                        last.then_inc(s_cs, 1)
                        dve.wait_ge(s_cs, a + 3)
                        dve.tensor_reduce(dest_f[:, :, :], picked[:, :, :, :], AX.X, ALU.add).then_inc(s_cs, 1)
                        dve.wait_ge(s_cs, a + 4)
                        dve.wait_ge(s_sc[q], due(64 * (n - q)))
                        dve.tensor_copy(dest[q][:, :, :], dest_f[:, :, :]).then_inc(s_cs, 1)
                        for c in range(2):
                            dve.tensor_copy(rows[q][c][:, :, D + 1], top_v[:, :, c])
                            last = dve.tensor_scalar(rows[q][c][:, :, D], res_row[:, :], float(c), None, ALU.add)
                        last.then_inc(s_cs, 1)
                        dve.wait_ge(s_cs, a + 6)
                        dve.tensor_scalar(res_row[:, :], res_row[:, :], float(2 * T), None, ALU.add).then_inc(s_cs, 1)
                walk(has, do)

            steps(dve, step)

            dve.wait_ge(s_cs, CS * B)
            link = [0]

            def chain(ins):
                link[0] += 1
                ins.then_inc(s_tb, 1)
                dve.wait_ge(s_tb, link[0])

            chain(dve.tensor_copy(pad_at[:, :], base[0:1, :]))
            assert link[0] == TB_PAD
            chain(dve.tensor_tensor(cnt[:, :], base[:, :], region[:, :], ALU.subtract))
            chain(dve.tensor_scalar(cnt_i[:, :], cnt[:, :], float(P - 1), None, ALU.add))
            chain(dve.tensor_scalar(nt_i[:, :], cnt_i[:, :], 7, None, ALU.arith_shift_right))
            chain(dve.tensor_copy(nt_f[:, :], nt_i[:, :]))
            chain(dve.tensor_tensor(cum3[:, :, :], upto[:, :, :], nt_f[:, None, :].to_broadcast([P, E, E]), ALU.mult))
            chain(dve.tensor_reduce(cum[:, :], cum3[:, :, :], AX.X, ALU.add))
            chain(dve.tensor_scalar(done[:, :], cum[:, :], tile_no[:, 0:1], None, ALU.is_le))
            chain(dve.tensor_reduce(tv[:, 0:1], done[:, :], AX.X, ALU.add))
            chain(dve.tensor_tensor(skipped[:, :], done[:, :], nt_f[:, :], ALU.mult))
            chain(dve.tensor_reduce(tv[:, 1:2], skipped[:, :], AX.X, ALU.add))
            chain(dve.tensor_tensor(tv[:, 2:3], tile_no[:, :], tv[:, 1:2], ALU.subtract))
            chain(dve.tensor_scalar(tv[:, 3:4], tv[:, 0:1], float(E), float(P), ALU.is_lt, ALU.mult))
            chain(dve.tensor_tensor(tv[:, 2:3], tv[:, 2:3], tv[:, 3:4], ALU.mult))
            chain(dve.tensor_scalar(tv[:, 4:5], tv[:, 0:1], float(E - 1), None, ALU.min))
            chain(dve.scalar_tensor_tensor(out=tv[:, 5:6], in0=tv[:, 0:1], scalar=float(ROWS), in1=tv[:, 2:3], op0=ALU.mult, op1=ALU.add))
            assert link[0] == TB_COLS
            dve.wait_ge(s_tm, 1)
            chain(dve.tensor_copy(table[:, :, :], pM[0:1, 0:2 * P].rearrange("p (j t) -> p j t", j=2)))
            assert link[0] == TB_END
            dve.wait_ge(s_w2, 16 * 5)
            dve.wait_ge(s_w1, 16 * 4)

            def expert(t):
                return dve.value_load(table[0:1, 0, t:t + 1] if isinstance(t, int) else table[0:1, 0, bass.ds(t, 1)], min_val=0, max_val=E - 1)

            def rows_T(t, q):
                dve.wait_ge(s_gt, t + 1)
                if not isinstance(t, int) or t >= 2:
                    dve.wait_ge(s_h, due(t - 1))
                dve.tensor_copy(xgT[q % 2][:, :], pM[:, 0:P]).then_inc(s_gT, 1)
                dve.tensor_copy(w1c[q % 2][:, :], w1s[:, bass.ds(expert(t), 1), :].rearrange("p e h -> p (e h)")).then_inc(s_wc, 1)

            def act_half(t, q, e):
                dve.wait_ge(s_h, t + 1)
                if not isinstance(t, int) or t >= 2:
                    dve.wait_ge(s_y, due(t - 1))
                for c in range(2, HC):
                    last = dve.tensor_scalar(hid[q % 2][:, c, :], pU[:, q % 2, 1, (c - 2) * P:(c - 1) * P],
                                             b1T[:, bass.ds(e * HC + c, 1)], 0.0, ALU.add, ALU.max)
                last.then_inc(s_hv, 1)

            def bias(t, q, e):
                if not isinstance(t, int) or t >= 2:
                    dve.wait_ge(s_ys[q % 2], due(8 * (t - q % 2)))
                dve.tensor_copy(ydest[q % 2][:, :], xg[q][:, D:D + 1]).then_inc(s_yi, 1)
                dve.wait_ge(s_y, t + 1)
                if not isinstance(t, int) or t >= 2:
                    dve.wait_ge(s_yg, due(t - 1))
                dve.tensor_tensor(yb[q % 2][:, :], pS[:, q % 2, 0:D], b2b[:, bass.ds(e, 1), :].rearrange("p e m -> p (e m)"), ALU.add).then_inc(s_yb, 1)

            rows_T(0, 0)
            rows_T(1, 1)
            act_half(0, 0, expert(0))
            for t in range(XG):
                rows_T(t + 2, (t + 2) % XG)
                act_half(t + 1, (t + 1) % XG, expert(t + 1))
                bias(t, t, expert(t))
            with dve.Fori(XG, TILES - XG, XG) as t:
                for q in range(XG):
                    rows_T(t + (q + 2), (q + 2) % XG)
                    act_half(t + (q + 1), (q + 1) % XG, expert(t + (q + 1)))
                    bias(t + q, q, expert(t + q))
            for t in range(TILES - XG, TILES):
                if t + 2 < TILES:
                    rows_T(t + 2, (t + 2) % XG)
                if t + 1 < TILES:
                    act_half(t + 1, (t + 1) % XG, expert(t + 1))
                bias(t, t % XG, expert(t))

            for n in range(B):
                dve.wait_ge(s_fin[n], 16)
                dve.tensor_tensor(fin[:, n, :, 0, :], fin[:, n, :, 0, :], fin[:, n, :, 1, :], ALU.add).then_inc(s_f1, 1)
                dve.wait_ge(s_f1, n + 1)
                dve.wait_ge(s_x1d, 16 * B)
                dve.tensor_tensor(x1[:, NT * n:NT * n + NT, :], x1[:, NT * n:NT * n + NT, :], fin[:, n, :, 0, :], ALU.add).then_inc(s_f2, 1)


_INS = ["L0_attn_target", "L0_attn_w_qkv", "L0_attn_w_proj", "L0_attn_b_proj", "L0_attn_ln_gamma", "L0_attn_ln_beta",
        "L0_ffn_Wr", "L0_ffn_br", "L0_ffn_W1", "L0_ffn_b1", "L0_ffn_W2", "L0_ffn_b2"]


def kernel(**inputs):
    import numpy as np
    import concourse.bacc as bacc
    from concourse.bass_utils import run_bass_kernel_spmd

    nc = bacc.Bacc("TRN2", target_bir_lowering=False, num_devices=1)
    arrays, args = {}, []
    for name in _INS:
        a = np.ascontiguousarray(inputs[name])
        arrays[name] = a
        args.append(nc.dram_tensor(name, a.shape, mybir.dt.from_np(a.dtype), kind="ExternalInput").ap())
    shape = inputs["L0_attn_target"].shape
    args.append(nc.dram_tensor("out", shape, F32, kind="ExternalOutput").ap())
    moe_block(nc, *args)
    return run_bass_kernel_spmd(nc, [arrays], core_ids=[0]).results[0]["out"]
```

```python
from contextlib import ExitStack

import numpy as np

import concourse.bass as bass
from concourse import mybir

F32 = mybir.dt.float32
BF16 = mybir.dt.bfloat16
I32 = mybir.dt.int32
U32 = mybir.dt.uint32
ALU = mybir.AluOpType
ACT = mybir.ActivationFunctionType
AX = mybir.AxisListType

P = 128
EPS = 1e-5
MASKED = -1e30
ONES_PAIR = float(np.array([0x3F803F80], np.uint32).view(np.float32)[0])
SKIP = 1 << 20

SLOT = [
    ("PVL", 1), ("S", 0), ("U", 0), ("S", 1), ("x", 0), ("S", 2), ("U", 1), ("S", 3), ("x", 1), ("SEL", 0),
    ("PVL", 2), ("M", 0), ("PVL", 3), ("U", 2), ("OE", 0), ("S", 4), ("x", 2), ("S", 5), ("x", 3), ("U", 3), ("N", 0),
    ("S", 6), ("U", 4), ("S", 7), ("SEL", 1), ("x", 4), ("PV", 0), ("S", 8), ("S", 9), ("U", 5), ("x", 5), ("SEL", 2),
    ("S", 10), ("SPLIT", 0), ("x", 6), ("SEL", 3),
]
EXTRA = {
    (0, 0): [("T", -2), ("LOADX", 2)],
    (0, 1): [("XB0", -1), ("LN1S0", 2), ("STB", 1)],
    (0, 2): [("COPY", -2), ("W10", 0), ("LN1S1", 2)],
    (0, 3): [("R", -2)],
    (0, 4): [("TOP", -2)],
    (0, 5): [("A", -1), ("XB1", -1)],
    (1, 0): [("PROJ", -1), ("LN1C", 2)],
    (1, 2): [("W11", 0), ("C", -2), ("W12", 0), ("SCATTER0", -2)],
    (1, 3): [("LN1N0", 2)],
    (1, 4): [("LN1N1", 2)],
    (1, 5): [("SCATTER1", -2), ("X", 2), ("LN2S0", -1)],
    (1, 6): [("LN2S1", -1)],
    (2, 0): [("LN2C", -1), ("Q", 2)],
    (2, 1): [("SCATTER2", -2), ("Q2", 2)],
    (2, 2): [("LN2N0", -1)],
    (2, 3): [("SCATTER3", -2), ("LN2N1", -1), ("X1A", -1)],
    (2, 4): [("K", 2), ("QOUT", 2), ("SCATTER4", -2)],
    (2, 5): [("X1B", -1), ("K2", 2)],
    (3, 0): [("KOUT", 2), ("LN3S0", -1), ("SCATTER5", -2)],
    (3, 1): [("LN3S1", -1), ("SCATTER6", -2), ("STA", 2)],
    (3, 2): [("LN3C", -1)],
    (3, 3): [("SCATTER7", -2), ("RELOAD", 0)],
    (3, 4): [("W13", 0)],
    (3, 5): [("LN3N0", -1), ("LN3N1", -1)],
    (3, 6): [("STORE1", -1), ("LEFT", -2), ("V", 1)],
}


def moe_block(nc, x_in, w_qkv, w_proj, b_proj, gamma, beta, w_r, b_r, w1, b1, w2, b2, out):
    B, T, D = x_in.shape
    E, _, HID = w1.shape
    H, HD, G = 16, D // 16, 4
    HH = H // 2
    NT = T // P
    NS = H // G
    ROWS = T * B + P
    TILES = (2 * B * T + E * (P - 1)) // P
    TILES += TILES % 2
    HC = HID // P
    RW = D + 2
    KQ = 9 * HD
    MROW = 96
    SCALE = float(HD) ** -0.5
    assert D == P and NT == 4 and NS == 4 and B % 2 == 0

    routed = nc.dram_tensor("routed_rows", [E * ROWS + P, RW], F32).ap()
    results = nc.dram_tensor("result_rows", [2 * B * T, D], F32).ap()
    xn_store = nc.dram_tensor("xn_store", [B, T, D], F32).ap()
    q_parts = nc.dram_tensor("q_parts", [2, 3, 2, HD, HH * T], BF16).ap()
    k_parts = nc.dram_tensor("k_parts", [2, 2, 3, HD, HH * T], BF16).ap()

    ctx = ExitStack()
    with ctx:
        def sb(name, shape, dt=F32):
            return ctx.enter_context(nc.sbuf_tensor(name, shape, dt))

        def sem(name):
            return ctx.enter_context(nc.semaphore(name))

        ident = sb("ident", [P, P])
        identb = sb("identb", [P, P], BF16)
        maskneg = sb("maskneg", [P, 2, P], BF16)
        before = sb("before", [P, P], BF16)
        onesb = sb("onesb", [P, P], BF16)
        iota_i = sb("iota_i", [P, 64], I32)
        iota_e = sb("iota_e", [P, E])
        region = sb("region", [P, E])
        tile_no = sb("tile_no", [P, 1])
        upto = sb("upto", [P, E, E])
        res_row = sb("res_row", [P, NT])
        neg_half = sb("neg_half", [P, NT])
        w_raw = sb("w_raw", [P, 3 * D])
        wq_p = sb("wq_p", [P, D])
        wk_p = sb("wk_p", [P, D])
        wp = sb("wp", [P, D])
        wr = sb("wr", [P, E])
        brb = sb("brb", [P, E])
        gammab = sb("gammab", [P, D])
        betab = sb("betab", [P, D])
        bprojb = sb("bprojb", [P, D])
        b1row = sb("b1row", [E * HC, P])
        w1s = sb("w1s", [P, E, HID + HC])

        ones_pair = sb("ones_pair", [P, 1])

        xin = [sb(f"xin{i}", [P, NT, D]) for i in range(2)]
        xn = sb("xn", [P, NT, D])
        xnT = [sb(f"xnT{i}", [P, T]) for i in range(2)]
        parts = [sb(f"parts{i}", [P, 3, T], BF16) for i in range(2)]
        resid = sb("resid", [P, T])
        qs = sb("qs", [P, 2, H, T], BF16)
        ks = sb("ks", [P, 2, H, T], BF16)
        va = [sb(f"va{i}", [P, NT, H, HD + 1]) for i in range(2)]
        nmax = [sb(f"nmax{i}", [P, NT, G]) for i in range(2)]
        nres = sb("nres", [P, NT, G])
        nsplit = [sb(f"nsplit{i}", [P, NT, 3, G], BF16) for i in range(2)]
        nmT = [sb(f"nmT{i}", [3 * G, T], BF16) for i in range(2)]
        pr = sb("pr", [P, G * (512 + 384 + 256 + 128)])
        oT = sb("oT", [P, T])
        rsum = sb("rsum", [P, NT, G])
        on = [sb(f"on{i}", [P, NT, D]) for i in range(2)]
        aT = sb("aT", [P, T])
        xr = sb("xr", [P, NT, D])
        xnr = sb("xnr", [P, NT, D])
        z = sb("z", [P, NT, D])
        x1w = sb("x1w", [P, NT, D])
        x1 = sb("x1", [P, B * NT, D])
        stats = sb("stats", [P, 3, NT, 6])
        mv = sb("mv", [P, 3, NT, 2])
        veps = sb("veps", [P, 3, NT])
        rstd = sb("rstd", [P, 3, NT])
        nmr0 = sb("nmr0", [P, 3, NT])
        nmr = sb("nmr", [P, 3, NT])

        rows = [[sb(f"rows{i}{c}", [P, NT, RW]) for c in range(2)] for i in range(2)]
        tT = sb("tT", [P, T])
        logit = sb("logit", [P, NT, E])
        lmax = sb("lmax", [P, NT])
        lsub = sb("lsub", [P, NT, E])
        pe_ = sb("pexp", [P, NT, E])
        psum_ = sb("psum_", [P, NT])
        prec = sb("prec", [P, NT])
        prob = sb("prob", [P, NT, E])
        top_v = sb("top_v", [P, NT, 8])
        top_i = sb("top_i", [P, NT, 8], U32)
        top_f = sb("top_f", [P, NT, 8])
        hot = sb("hot", [P, 2, NT, E])
        hotb = sb("hotb", [P, NT, E], BF16)
        place = sb("place", [P, NT, E])
        picked = sb("picked", [P, 2, NT, E])
        dest_f = sb("dest_f", [P, 2, NT])
        dest = [sb(f"dest{i}", [P, 2, NT], U32) for i in range(2)]
        base = sb("base", [P, E])

        cnt = sb("cnt", [P, E])
        cnt_i = sb("cnt_i", [P, E], I32)
        nt_i = sb("nt_i", [P, E], I32)
        nt_f = sb("nt_f", [P, E])
        cum3 = sb("cum3", [P, E, E])
        cum = sb("cum", [P, E])
        done = sb("done", [P, E])
        skipped = sb("skipped", [P, E])
        tv = sb("tv", [P, 6])
        table_f = sb("table_f", [1, 2, P])
        table = sb("table", [1, 2, P], I32)
        pad_at = sb("pad_at", [1, E], I32)
        pad_rows = sb("pad_rows", [P, RW])
        XG = 4
        xg = [sb(f"xg{i}", [P, RW]) for i in range(XG)]
        xgT = [sb(f"xgT{i}", [P, P]) for i in range(2)]
        w1c = ([parts[i][:, :, :].rearrange("p c t -> p (c t)").bitcast(F32)[:, 0:HID + HC] for i in range(2)]
               + [rows[i][0][:, :, :].rearrange("p i r -> p (i r)")[:, 0:HID + HC] for i in range(2)])
        b2c = [buf[:, 0, :] for buf in (xr, xnr, z)] + [resid[:, 0:D]]
        hid = [xnT[i][:, :].rearrange("p (c s) -> p c s", c=HC) for i in range(2)]
        yb = [sb(f"yb{i}", [P, D]) for i in range(2)]
        yg = [sb(f"yg{i}", [P, D]) for i in range(2)]
        ydest = [sb(f"ydest{i}", [P, 1], U32) for i in range(XG)]
        ygate = [sb(f"ygate{i}", [P, 1]) for i in range(XG)]

        def hidden(c, q):
            return pU[:, q % 2, 1, 0:P] if c == HC - 1 else pU[:, q % 2, 0, c * P:(c + 1) * P]

        w2s = qs[:, :, :, :].rearrange("p a h t -> p (a h t)").bitcast(F32).rearrange("p (e c m) -> p e c m", e=E, c=HC)
        b2b = pr[:, 0:E * D].rearrange("p (e m) -> p e m", e=E)
        fin = ks[:, :, :, :].rearrange("p a h t -> p (a h t)").bitcast(F32).rearrange("p (n i c d) -> p n i c d", n=B, i=NT, c=2)
        OFF = [0, G * 512, G * 896, G * 1152]
        QN = [T - P * k for k in range(NT)]
        prob_of = [pr[:, OFF[k]:OFF[k] + G * QN[k]].rearrange("p (h q) -> p h q", h=G) for k in range(NT)]

        pU = ctx.enter_context(nc.psum_tensor("pU", [P, 2, 2, 512], F32))
        pS = ctx.enter_context(nc.psum_tensor("pS", [P, 2, 512], F32))
        pO = ctx.enter_context(nc.psum_tensor("pO", [P, 512], F32))
        pM = ctx.enter_context(nc.psum_tensor("pM", [P, 512], F32))
        pMb = pM[:, :].bitcast(BF16)

        s_pc = sem("const_steps")
        s_const = sem("const_made")
        s_one = sem("ones_pair_set")
        s_zk = sem("k_stacks_zeroed")
        s_ok = sem("k_stacks_ones")
        s_zq = sem("q_stacks_padded")
        s_b1t = sem("b1_product")
        s_zero = sem("zeroed")
        s_w = sem("small_weights_in")
        s_w1 = sem("w1_in")
        s_w2 = sem("w2_in")
        s_wperm = sem("q_k_weights_ordered")
        s_b1 = sem("b1_turned")
        s_x = [sem(f"x_in{i}") for i in range(2)]
        s_stat = [sem(f"ln{k}_stats") for k in range(3)]
        s_mv = [sem(f"ln{k}_mean_var") for k in range(3)]
        s_coef = [sem(f"ln{k}_coef") for k in range(3)]
        s_norm = [sem(f"ln{k}_normed") for k in range(3)]
        s_xout = sem("xn_stored")
        s_re = sem("x_and_xn_back")
        s_xb = sem("biases_added")
        s_xt = sem("xn_turned")
        s_xnT = sem("xnT_ready")
        s_qk = sem("q_k_product")
        s_hi = sem("q_k_high")
        s_res = sem("q_k_residue")
        s_mid = sem("q_k_middle")
        s_lo = sem("q_k_low")
        s_qout = sem("q_parts_out")
        s_kout = sem("k_parts_out")
        s_st = [sem(f"stack_in{i}") for i in range(2)]
        s_vmm = sem("v_product")
        s_v = sem("v_ready")
        s_u = sem("unit_scores")
        s_red = sem("unit_maxima")
        s_spl = sem("maxima_split")
        s_mt = sem("maxima_turned")
        s_nmT = sem("maxima_rows")
        s_mr = [sem(f"maxima_in_stack{i}") for i in range(2)]
        s_s = sem("bank_scores")
        s_e = sem("bank_exp")
        s_sel = sem("masked")
        s_pv = sem("pv_done")
        s_oT = sem("o_copied")
        s_nt = sem("o_turned")
        s_rs = sem("o_reciprocals")
        s_n = sem("o_normed")
        s_at = sem("o_rows_turned")
        s_aT = sem("aT_ready")
        s_pj = sem("proj_product")
        s_z = sem("z_ready")
        s_x1 = sem("x1_steps")
        s_x1d = sem("x1_kept")
        s_row = sem("second_rows")
        s_tt = sem("t_turned")
        s_tT = sem("tT_ready")
        s_r = sem("router_product")
        s_lg = sem("router_steps")
        s_le = sem("router_exp")
        s_cp = sem("prefix_product")
        s_cs = sem("place_steps")
        s_sc = [sem(f"scattered{i}") for i in range(2)]
        LG, CS, ST = 11, 7, 16 * 4
        s_tb = sem("table_steps")
        TB_PAD, TB_COLS, TB_END = 1, 16, 20
        s_tm = sem("table_product")
        s_pad = sem("padding_stored")
        s_g = [sem(f"rows_in{i}") for i in range(XG)]
        s_gt = sem("rows_turned")
        s_gT = sem("xgT_ready")
        s_wc = sem("w1_of_tile")
        s_bc = sem("b2_of_tile")
        s_h = sem("hidden_product")
        s_ha = sem("hidden_act")
        s_hv = sem("hidden_act_vector")
        s_y = sem("y_product")
        s_yb = sem("y_bias")
        s_yi = sem("y_rows_known")
        s_yg = sem("y_gated")
        s_ys = [sem(f"y_stored{i}") for i in range(2)]
        s_fin = [sem(f"results_in{i}") for i in range(B)]
        s_f1 = sem("results_added")
        s_f2 = sem("x1_added")
        s_out = sem("out_stored")

        def due(n):
            return max(n, 0) if isinstance(n, int) else n

        def held(eng, n):
            if isinstance(n, int):
                return due(n)
            n = eng.to_reg(n)
            eng.wait_ge(s_const, 1)
            return n

        def steps(eng, step):
            def has(b):
                return lambda k: 0 <= b + k < B
            for b in range(-2, 2):
                step(b, b % 2, has(b))
            with eng.Fori(1, B // 2 - 1) as i:
                step(2 * i, 0, lambda k: True)
                step(2 * i + 1, 1, lambda k: True)
            for b in range(B - 2, B + 2):
                step(b, b % 2, has(b))

        def walk(has, do):
            for g in range(NS):
                for name, i in SLOT:
                    if name == "x":
                        for what, k in EXTRA.get((g, i), []):
                            if has(k):
                                do(what, k, g)
                    elif name in ("U", "SPLIT"):
                        if has(1):
                            do(name, i, g)
                    elif name == "M":
                        if has(1) if g else has(0):
                            do(name, i, g)
                    elif name in ("PVL", "OE", "N"):
                        if has(0) if g else has(-1):
                            do(name, i, g)
                    elif has(0):
                        do(name, i, g)

        block = ctx.enter_context(nc.Block())

        @block.sync
        def _(sp):
            small = [(w_raw[:, :], w_qkv), (wp[:, :], w_proj), (wr[:, :], w_r),
                     (brb[:, :], b_r.partition_broadcast(P)), (gammab[:, :], gamma.partition_broadcast(P)),
                     (betab[:, :], beta.partition_broadcast(P)), (bprojb[:, :], b_proj.partition_broadcast(P)),
                     (b1row[:, :], b1.rearrange("e (c p) -> (e c) p", p=P))]
            for n in range(2):
                sp.dma_start(xin[n][:, :, :], x_in[n].rearrange("(i p) d -> p i d", p=P)).then_inc(s_x[n], 16)
            for dst, src in small:
                sp.dma_start(dst, src).then_inc(s_w, 16)

            def stack(n, q, half):
                sp.wait_ge(s_qout, held(sp, 16 * n + 16))
                sp.wait_ge(s_kout, held(sp, 32 * n + 32))
                sp.wait_ge(s_s, held(sp, 44 * (n - 2) + 22 * (half + 1)))
                sp.wait_ge(s_st[half], held(sp, ST * n))
                if isinstance(n, int) and n < 2:
                    sp.wait_ge(s_zk, n + 1)
                    sp.wait_ge(s_zq, n + 1)
                heads = slice(HH * half, HH * half + HH)
                for i in range(3):
                    sp.dma_start(qs[3 * HD * i:3 * HD * (i + 1), q, heads, :],
                                 q_parts[q, i, half][None, :, :].to_broadcast([3, HD, HH * T])).then_inc(s_st[half], 16)
                sp.dma_start(ks[0:KQ, q, heads, :],
                             k_parts[q, half].rearrange("j d n -> (j d) n")[None, :, :].to_broadcast([3, 3 * HD, HH * T]))\
                    .then_inc(s_st[half], 16)

            def second_weights():
                sp.wait_ge(s_s, 11 * NS * B)
                for q in range(2):
                    sp.wait_ge(s_mr[q], 16 * NS * B // 2)
                for e in range(0, E, 4):
                    sp.dma_start(w2s[:, e:e + 4, :, :].rearrange("p e c m -> p (e c) m"),
                                 w2[e:e + 4].rearrange("e (c p) m -> p (e c) m", p=P)).then_inc(s_w2, 16)

            def step(b, pb, has):
                if isinstance(b, int) and b == B:
                    second_weights()

                def do(name, k, g):
                    if name == "LOADX":
                        n, q = b + k, (pb + k) % 2
                        if isinstance(n, int) and n < 2:
                            return
                        sp.wait_ge(s_norm[0], held(sp, n - 1))
                        sp.dma_start(xin[q][:, :, :], x_in[n].rearrange("(i p) d -> p i d", p=P)).then_inc(s_x[q], 16)
                    elif name == "X":
                        n = b + k
                        sp.wait_ge(s_norm[0], held(sp, n + 1))
                        sp.dma_start(xn_store[n].rearrange("(i p) d -> p i d", p=P), xn[:, :, :]).then_inc(s_xout, 16)
                    elif name == "RELOAD":
                        n = b + k
                        sp.wait_ge(s_xout, held(sp, 16 * (n + 1)))
                        sp.wait_ge(s_x1, held(sp, 2 * n))
                        sp.dma_start(xr[:, :, :], x_in[n].rearrange("(i p) d -> p i d", p=P)).then_inc(s_re, 16)
                        sp.dma_start(xnr[:, :, :], xn_store[n].rearrange("(i p) d -> p i d", p=P)).then_inc(s_re, 16)
                    elif name[0:2] == "W1" and isinstance(b, int) and b == B - 2:
                        e = 4 * int(name[2])
                        sp.dma_start(w1s[:, e:e + 4, 0:HID], w1[e:e + 4].rearrange("e p h -> p e h")).then_inc(s_w1, 16)
                    elif name == "QOUT":
                        n = b + k
                        sp.wait_ge(s_lo, held(sp, 2 * n + 1))
                        sp.wait_ge(s_st[1], held(sp, ST * (n - 1)))
                        sp.dma_start(q_parts[pb].rearrange("i g d (h t) -> (g d h) i t", t=T), parts[0][:, :, :]).then_inc(s_qout, 16)
                    elif name == "KOUT":
                        n = b + k
                        sp.wait_ge(s_lo, held(sp, 2 * n + 2))
                        for half in range(2):
                            sp.dma_start(k_parts[pb, half].rearrange("j d (h t) -> (d h) j t", t=T),
                                         parts[1][64 * half:64 * half + 64, :, :]).then_inc(s_kout, 16)
                    elif name == "STA":
                        stack(b + k, pb, 0)
                    elif name == "STB":
                        stack(b + k, (pb + 1) % 2, 1)
                    elif name == "M":
                        n1 = 4 * b + (4 + g - 1)
                        q, gm = (g - 1) % 2, (g - 1) % 4
                        pq = (pb + 1) % 2 if g else pb
                        sp.wait_ge(s_nmT, held(sp, n1 + 1))
                        if not isinstance(b, int) or n1 >= 2:
                            sp.wait_ge(s_mr[q], held(sp, 8 * (n1 - q)))
                        sp.dma_start(qs[MROW:MROW + 3, pq, G * gm:G * gm + G, :], nmT[q][:, :]).then_inc(s_mr[q], 16)
                    elif name == "STORE1":
                        n = b + k
                        sp.wait_ge(s_x1, held(sp, 2 * n + 2))
                        sp.dma_start(x1[:, 4 * n:4 * n + 4, :] if isinstance(n, int) else x1[:, bass.ds(4 * n, 4), :],
                                     x1w[:, :, :]).then_inc(s_x1d, 16)
                walk(has, do)

            steps(sp, step)

            sp.wait_ge(s_pv, 4 * NS * B)
            sp.dma_start(b2b, b2.rearrange("e m -> (e m)").partition_broadcast(P).rearrange("p (e m) -> p e m", e=E))\
                .then_inc(s_w2, 16)

            sp.dma_start(routed[E * ROWS:E * ROWS + P, :], pad_rows[:, :]).then_inc(s_pad, 16)
            sp.wait_ge(s_tb, TB_PAD)
            for e in range(0, E, 2):
                at = sp.value_load(pad_at[0:1, e:e + 1], min_val=0, max_val=(e + 1) * ROWS - P)
                sp.dma_start(routed[bass.ds(at, P), :], pad_rows[:, :]).then_inc(s_pad, 16)
            for q in range(2):
                sp.wait_ge(s_sc[q], held(sp, 16 * 2 * NT * B // 2))
            sp.wait_ge(s_pad, held(sp, 16 * (E + 1)))
            sp.wait_ge(s_tb, TB_END)

            def load_rows(t, q):
                if not isinstance(t, int) or t >= XG:
                    sp.wait_ge(s_gt, held(sp, t - XG + 1))
                    sp.wait_ge(s_yi, held(sp, t - XG + 1))
                at = sp.value_load(table[0:1, 1, t:t + 1] if isinstance(t, int) else table[0:1, 1, bass.ds(t, 1)],
                                   min_val=0, max_val=E * ROWS)
                sp.dma_start(xg[q][:, :], routed[bass.ds(at, P), :]).then_inc(s_g[q], 16)

            for t in range(XG):
                load_rows(t, t)
            with sp.Fori(XG, TILES, XG) as t:
                for q in range(XG):
                    load_rows(t + q, q)

            for q in range(2):
                sp.wait_ge(s_ys[q], held(sp, 16 * TILES // 2))
            for n in range(B):
                sp.dma_start(fin[:, n].rearrange("p i c d -> p i (c d)"),
                             results.rearrange("(n i p c) d -> n p i (c d)", i=NT, p=P, c=2)[n]).then_inc(s_fin[n], 16)
            for n in range(B):
                sp.wait_ge(s_f2, held(sp, n + 1))
                sp.dma_start(out[n].rearrange("(i p) d -> p i d", p=P), x1[:, NT * n:NT * n + NT, :]).then_inc(s_out, 16)
            sp.wait_ge(s_out, 16 * B)

        @block.gpsimd
        def _(pool):
            pool.memset(ident[:, :], 0.0).then_inc(s_pc, 1)
            pool.memset(maskneg[:, :, :], 0.0).then_inc(s_pc, 1)
            pool.memset(before[:, :], 1.0).then_inc(s_pc, 1)
            pool.memset(onesb[:, :], 1.0).then_inc(s_pc, 1)
            pool.memset(neg_half[:, :], -0.5).then_inc(s_pc, 1)
            pool.memset(upto[:, :, :], 1.0).then_inc(s_pc, 1)
            pool.iota(iota_i[:, 0:E], pattern=[[1, E]], base=0, channel_multiplier=0).then_inc(s_pc, 1)
            pool.iota(iota_i[:, E:2 * E], pattern=[[ROWS, E]], base=0, channel_multiplier=0).then_inc(s_pc, 1)
            pool.iota(iota_i[:, 2 * E:2 * E + NT], pattern=[[2 * P, NT]], base=0, channel_multiplier=2).then_inc(s_pc, 1)
            pool.iota(iota_i[:, 3 * E:3 * E + 1], pattern=[[0, 1]], base=0, channel_multiplier=1).then_inc(s_pc, 1)
            pool.memset(pad_rows[:, 0:D], 0.0).then_inc(s_pc, 1)
            pool.memset(pad_rows[:, D:D + 1], float(SKIP)).then_inc(s_pc, 1)
            pool.memset(pad_rows[:, D + 1:D + 2], 0.0).then_inc(s_pc, 1)
            pool.wait_ge(s_pc, 13)
            pool.affine_select(out=ident[:, :], in_=ident[:, :], compare_op=ALU.not_equal, fill=1.0, base=0,
                               pattern=[[-1, P]], channel_multiplier=1).then_inc(s_pc, 1)
            pool.affine_select(out=maskneg[:, :, :], in_=maskneg[:, :, :], compare_op=ALU.is_ge, fill=MASKED, base=0,
                               pattern=[[0, 2], [-1, P]], channel_multiplier=1).then_inc(s_pc, 1)
            pool.affine_select(out=before[:, :], in_=before[:, :], compare_op=ALU.is_ge, fill=0.0, base=-1,
                               pattern=[[1, P]], channel_multiplier=-1).then_inc(s_pc, 1)
            pool.affine_select(out=upto[:, :, :], in_=upto[:, :, :], compare_op=ALU.is_ge, fill=0.0, base=0,
                               pattern=[[1, E], [-1, E]], channel_multiplier=0).then_inc(s_pc, 1)
            pool.tensor_copy(iota_e[:, :], iota_i[:, 0:E]).then_inc(s_pc, 1)
            pool.tensor_copy(region[:, :], iota_i[:, E:2 * E]).then_inc(s_pc, 1)
            pool.tensor_copy(base[:, :], iota_i[:, E:2 * E]).then_inc(s_pc, 1)
            pool.tensor_copy(res_row[:, :], iota_i[:, 2 * E:2 * E + NT]).then_inc(s_pc, 1)
            pool.tensor_copy(tile_no[:, :], iota_i[:, 3 * E:3 * E + 1]).then_inc(s_pc, 1)
            pool.wait_ge(s_pc, 22)
            pool.tensor_copy(identb[:, :], ident[:, :]).then_inc(s_const, 1)
            pool.wait_ge(s_const, 1)

            def step(b, pb, has):
                def do(name, k, g):
                    if name == "SPLIT":
                        n1, q = 4 * b + (4 + g), g % 2
                        pool.wait_ge(s_red, held(pool, 6 * n1 + 6))
                        pool.wait_ge(s_mt, held(pool, n1 - 1))
                        pool.tensor_copy(nsplit[q][:, :, 0, :], nmax[q][:, :, :]).then_inc(s_spl, 1)
                        pool.wait_ge(s_spl, held(pool, 4 * n1 + 1))
                        pool.tensor_tensor(nres[:, :, :], nmax[q][:, :, :], nsplit[q][:, :, 0, :], ALU.subtract).then_inc(s_spl, 1)
                        pool.wait_ge(s_spl, held(pool, 4 * n1 + 2))
                        pool.tensor_copy(nsplit[q][:, :, 1, :], nres[:, :, :]).then_inc(s_spl, 1)
                        pool.wait_ge(s_spl, held(pool, 4 * n1 + 3))
                        pool.tensor_tensor(nsplit[q][:, :, 2, :], nres[:, :, :], nsplit[q][:, :, 1, :], ALU.subtract).then_inc(s_spl, 1)
                    elif name == "SEL":
                        n = 4 * b + g
                        pool.wait_ge(s_e, held(pool, 11 * n + [4, 8, 10, 11][k]))
                        diag = prob_of[k][:, :, 0:P]
                        pool.affine_select(out=diag, in_=diag, compare_op=ALU.is_ge, fill=0.0, base=0,
                                           pattern=[[0, G], [1, P]], channel_multiplier=-1).then_inc(s_sel, 1)
                    elif name in ("Q2", "K2"):
                        n, c = b + k, int(name == "K2")
                        pool.wait_ge(s_mid, held(pool, 2 * n + c + 1))
                        pool.tensor_tensor(parts[c][:, 2, :], resid[:, :], parts[c][:, 1, :], ALU.subtract).then_inc(s_lo, 1)
                    elif name in ("LN1C", "LN2C", "LN3C"):
                        n, j = b + k, int(name[2]) - 1
                        pool.wait_ge(s_mv[j], held(pool, n + 1))
                        pool.wait_ge(s_norm[j], held(pool, n))
                        pool.tensor_scalar(veps[:, j, :], mv[:, j, :, 1], EPS, None, ALU.add).then_inc(s_coef[j], 1)
                        pool.wait_ge(s_coef[j], held(pool, 4 * n + 1))
                        pool.tensor_tensor(rstd[:, j, :], veps[:, j, :], neg_half[:, :], ALU.pow).then_inc(s_coef[j], 1)
                        pool.wait_ge(s_coef[j], held(pool, 4 * n + 2))
                        pool.tensor_tensor(nmr0[:, j, :], mv[:, j, :, 0], rstd[:, j, :], ALU.mult).then_inc(s_coef[j], 1)
                        pool.wait_ge(s_coef[j], held(pool, 4 * n + 3))
                        pool.tensor_scalar(nmr[:, j, :], nmr0[:, j, :], -1.0, None, ALU.mult).then_inc(s_coef[j], 1)
                        if j == 0 and isinstance(n, int) and n == 0:
                            pool.wait_ge(s_coef[j], 4)
                            for q in range(2):
                                pool.memset(qs[64:P, q, :, :].rearrange("p h t -> p (h t)").bitcast(F32), 0.0).then_inc(s_zq, 1)
                                pool.wait_ge(s_zq, q + 1)
                    elif name == "XB0":
                        n = b + k
                        pool.wait_ge(s_re, held(pool, 32 * n + 32))
                        pool.tensor_tensor(xnr[:, :, :], xnr[:, :, :], bprojb[:, None, :].to_broadcast([P, NT, D]), ALU.add).then_inc(s_xb, 1)
                    elif name == "XB1":
                        n = b + k
                        pool.tensor_tensor(xr[:, :, :], xr[:, :, :], betab[:, None, :].to_broadcast([P, NT, D]), ALU.add).then_inc(s_xb, 1)
                    elif name == "X1A":
                        n = b + k
                        pool.wait_ge(s_norm[1], held(pool, n + 1))
                        pool.tensor_tensor(z[:, :, :], z[:, :, :], gammab[:, None, :].to_broadcast([P, NT, D]), ALU.mult).then_inc(s_x1, 1)
                    elif name == "X1B":
                        n = b + k
                        pool.wait_ge(s_x1, held(pool, 2 * n + 1))
                        pool.wait_ge(s_xb, held(pool, 2 * n + 2))
                        pool.wait_ge(s_norm[2], held(pool, n))
                        pool.wait_ge(s_x1d, held(pool, 16 * n))
                        pool.tensor_tensor(x1w[:, :, :], z[:, :, :], xr[:, :, :], ALU.add).then_inc(s_x1, 1)
                    elif name.startswith("SCATTER"):
                        n, q = b + k, pb
                        pool.wait_ge(s_cs, held(pool, CS * n + 6))
                        pool.wait_ge(s_row, held(pool, n + 1))
                        i, c = divmod(int(name[-1]), 2)
                        pool.indirect_dma_start(
                            routed[:, :], bass.IndirectOffsetOnAxis(ap=dest[q][:, c, i:i + 1], axis=0),
                            rows[q][c][:, i, :], None).then_inc(s_sc[q], 16)
                    elif name == "LEFT":
                        n = b + k
                        pool.wait_ge(s_sc[pb], held(pool, 64 * (n - pb) + 128))
                walk(has, do)

            steps(pool, step)

            def store(t, q):
                pool.wait_ge(s_yg, held(pool, t + 1))
                pool.indirect_dma_start(results[:, :], bass.IndirectOffsetOnAxis(ap=ydest[q][:, 0:1], axis=0), yg[q % 2][:, :], None,
                                        bounds_check=2 * B * T - 1, oob_is_err=False).then_inc(s_ys[q % 2], 16)
            with pool.Fori(0, TILES, XG) as t:
                for q in range(XG):
                    store(t + q, q)

        @block.scalar
        def _(act):

            act.wait_ge(s_one, 1)
            for q in range(2):
                act.copy(ks[MROW:P, q, :, :].rearrange("p h t -> p (h t)").bitcast(F32),
                         ones_pair[MROW:P, 0:1].to_broadcast([P - MROW, H * T // 2])).then_inc(s_ok, 1)

            def norm(j, n, dst, src, half):
                act.wait_ge(s_coef[j], 4 * n + 4)
                for i in range(2 * half, 2 * half + 2):
                    last = act.activation(dst[:, i, :], src[:, i, :], ACT.Identity, bias=nmr[:, j, i:i + 1], scale=rstd[:, j, i:i + 1])
                if half:
                    last.then_inc(s_norm[j], 1)

            def step(b, pb, has):
                def do(name, k, g):
                    n = b + k if isinstance(k, int) else None
                    if name == "S":
                        slot, i = 4 * b + g, k
                        kb, h = ([(0, j) for j in range(4)] + [(1, j) for j in range(4)] + [(2, 0), (2, 2), (3, 0)])[i]
                        nh = [1, 1, 2, 4][kb]
                        if h == 0:
                            act.wait_ge(s_pv, due(4 * slot - 3 + kb))
                        act.wait_ge(s_s, 11 * slot + i + 1)
                        act.activation(prob_of[kb][:, h:h + nh, :],
                                       pS[:, (g + i) % 2, 0:nh * QN[kb]].rearrange("p (h q) -> p h q", h=nh),
                                       ACT.Exp, scale=SCALE).then_inc(s_e, 1)
                    elif name == "OE":
                        slot = 4 * b + (g - 1)
                        act.wait_ge(s_pv, 4 * slot + 4)
                        act.wait_ge(s_nt, due(slot))
                        act.copy(oT[:, :], pO[:, :]).then_inc(s_oT, 1)
                    elif name == "M":
                        n1, q = 4 * b + (4 + g - 1), (g - 1) % 2
                        act.wait_ge(s_mt, n1 + 1)
                        act.wait_ge(s_mr[q], due(8 * (n1 - q)))
                        act.copy(nmT[q][:, :], pMb[0:3 * G, 0:T]).then_inc(s_nmT, 1)
                    elif name == "X":
                        act.wait_ge(s_xt, n + 1)
                        act.wait_ge(s_vmm, due(n - 1))
                        act.copy(xnT[pb][:, :], pM[:, :]).then_inc(s_xnT, 1)
                    elif name in ("Q", "K"):
                        c = int(name == "K")
                        act.wait_ge(s_qk, 2 * n + c + 1)
                        parts_out, each = [(s_qout, 16), (s_kout, 32)][c]
                        act.wait_ge(parts_out, due(each * n))
                        act.copy(parts[c][:, 0, :], pM[:, :]).then_inc(s_hi, 1)
                    elif name in ("Q2", "K2"):
                        c = int(name == "K2")
                        act.wait_ge(s_res, 2 * n + c + 1)
                        act.copy(parts[c][:, 1, :], resid[:, :]).then_inc(s_mid, 1)
                    elif name == "V":
                        q = (pb + 1) % 2
                        act.wait_ge(s_vmm, n + 1)
                        act.wait_ge(s_pv, due(16 * (n - 1)))
                        act.copy(va[q][:, :, :, 0:HD], pM[:, :].rearrange("p (i h d) -> p i h d", i=NT, h=H)).then_inc(s_v, 1)
                    elif name in ("LN1N0", "LN1N1"):
                        act.wait_ge(s_xt, due(n))
                        act.wait_ge(s_xout, due(16 * n))
                        norm(0, n, xn, xin[pb], int(name[4]))
                    elif name in ("LN2N0", "LN2N1"):
                        norm(1, n, z, z, int(name[4]))
                    elif name in ("LN3N0", "LN3N1"):
                        q = (pb + 1) % 2
                        if isinstance(n, int):
                            act.wait_ge(s_sc[q], due(64 * (n - q)))
                        norm(2, n, rows[q][0][:, :, 0:D], x1w, int(name[4]))
                    elif name == "COPY":
                        q = pb
                        act.wait_ge(s_norm[2], n + 1)
                        act.copy(rows[q][1][:, :, 0:D], rows[q][0][:, :, 0:D]).then_inc(s_row, 1)
                    elif name == "A":
                        act.wait_ge(s_at, n + 1)
                        act.wait_ge(s_pj, due(n))
                        act.copy(aT[:, :], pM[:, :]).then_inc(s_aT, 1)
                    elif name == "T":
                        act.wait_ge(s_tt, n + 1)
                        act.copy(tT[:, :], pM[:, :]).then_inc(s_tT, 1)
                    elif name == "TOP":
                        act.wait_ge(s_lg, LG * n + 3)
                        act.activation(pe_[:, :, :], lsub[:, :, :], ACT.Exp).then_inc(s_le, 1)
                walk(has, do)

            steps(act, step)

            act.wait_ge(s_tb, TB_PAD)
            for e in range(1, E, 2):
                at = act.value_load(pad_at[0:1, e:e + 1], min_val=0, max_val=(e + 1) * ROWS - P)
                act.dma_start(routed[bass.ds(at, P), :], pad_rows[:, :]).then_inc(s_pad, 16)
            act.wait_ge(s_b1, 1)

            def tile(t, q):
                act.wait_ge(s_h, t + 1)
                if not isinstance(t, int) or t >= 2:
                    act.wait_ge(s_y, due(t - 1))
                for c in range(HC - 1):
                    last = act.activation(hid[q % 2][:, c, :], hidden(c, q), ACT.Relu,
                                          bias=w1c[q][:, HID + c:HID + c + 1])
                last.then_inc(s_ha, 1)

            def gate(t, q):
                act.wait_ge(s_yb, t + 1)
                if not isinstance(t, int) or t >= 2:
                    act.wait_ge(s_ys[q % 2], due(8 * (t - q % 2)))
                act.activation(yg[q % 2][:, :], yb[q % 2][:, :], ACT.Identity, scale=ygate[q][:, :]).then_inc(s_yg, 1)

            act.wait_ge(s_tb, TB_END)
            tile(0, 0)
            for t in range(1, XG):
                tile(t, t)
                gate(t - 1, t - 1)
            with act.Fori(XG, TILES, XG) as t:
                for q in range(XG):
                    tile(t + q, q)
                    gate(t + (q - 1), (q - 1) % XG)
            gate(TILES - 1, XG - 1)

        @block.tensor
        def _(pe):
            last_use = [(s_const, 1)]

            def last_left(s, n):
                before_, last_use[0] = last_use[0], (s, n)
                return before_

            pe.wait_ge(s_const, 1)
            pe.wait_ge(s_w, 16 * 8)
            pe.wait_ge(*last_left(s_b1, 1))
            pe.transpose(pM[:, 0:E * HC], b1row[:, :], ident[0:E * HC, 0:E * HC]).then_inc(s_b1t, 1)
            pe.wait_ge(s_zero, 1)
            pe.wait_ge(s_wperm, 2)

            def turn(src, s):
                for i in range(NT):
                    last = pe.transpose(pM[:, i * P:(i + 1) * P], src(i), ident[:, :])
                last.then_inc(s, 1)

            def step(b, pb, has):
                if has(0):
                    last_use[0] = (s_v, b + 1)

                def pv(slot, j, gm, kb, pvp):
                    pe.wait_ge(s_sel, 4 * slot + kb + 1)
                    if kb == 0:
                        pe.wait_ge(s_oT, due(slot))
                    for h in range(G):
                        last = pe.matmul(pO[32 * h:32 * h + HD + 1, kb * P:T], va[pvp][:, kb, G * gm + h, :], prob_of[kb][:, h, :],
                                         start=(kb == 0), stop=(kb == NT - 1), skip_group_check=True)
                    last.then_inc(s_pv, 1)

                def do(name, k, g):
                    n = b + k
                    if name == "S":
                        slot, i = 4 * b + g, k
                        if i == 0:
                            if g == 0 and isinstance(b, int) and b < 2:
                                pe.wait_ge(s_ok, b + 1)
                            pe.wait_ge(s_mr[g % 2], due(8 * (slot - g % 2) + 16))
                        pe.wait_ge(s_e, due(11 * slot + i - 1))
                        kb, h = ([(0, j) for j in range(4)] + [(1, j) for j in range(4)] + [(2, 0), (2, 2), (3, 0)])[i]
                        nh = [1, 1, 2, 4][kb]
                        for j in range(nh):
                            last = pe.matmul(pS[:, (g + i) % 2, j * QN[kb]:(j + 1) * QN[kb]],
                                             ks[:, pb, G * g + h + j, kb * P:(kb + 1) * P],
                                             qs[:, pb, G * g + h + j, kb * P:T], start=True, stop=True)
                        last.then_inc(s_s, 1)
                    elif name == "U":
                        u, slot = k, 4 * b + (4 + g)
                        q, p1 = u % 2, (pb + 1) % 2
                        if u == 0:
                            pe.wait_ge(s_st[g // 2], ST * b + 2 * ST)
                        pe.wait_ge(s_red, due(6 * slot + u - 1))
                        pair, kind = u // 3, u % 3

                        def scores(dst, h, qt, start):
                            pe.matmul(dst, qs[0:MROW, p1, h, qt * P:(qt + 1) * P], ks[0:MROW, p1, h, 0:(qt + 1) * P],
                                      start=start, stop=False, skip_group_check=True)

                        def mask(dst, m):
                            return pe.matmul(dst, identb[:, :], maskneg[:, 0:m, :], start=False, stop=True, skip_group_check=True)

                        for j in range(2):
                            h = G * g + 2 * pair + j
                            if kind == 0:
                                scores(pU[:, q, j, :], h, 3, True)
                                last = mask(pU[:, q, j, 3 * P:4 * P], 1)
                            elif kind == 1:
                                scores(pU[:, q, j, 0:3 * P], h, 2, True)
                                scores(pU[:, q, j, 3 * P:4 * P], h, 0, False)
                                last = mask(pU[:, q, j, 2 * P:4 * P], 2)
                            else:
                                scores(pU[:, q, 0, 2 * j * P:(2 * j + 2) * P], h, 1, j == 0)
                                last = mask(pU[:, q, 0, (2 * j + 1) * P:(2 * j + 2) * P], 1)
                        last.then_inc(s_u, 1)
                    elif name == "PV":
                        if k == 0 and g == 0:
                            pe.wait_ge(s_v, b + 1)
                        pv(4 * b + g, None, g, k, pb)
                    elif name == "PVL":
                        pv(4 * b + (g - 1), None, (g - 1) % 4, k, pb if g else (pb + 1) % 2)
                    elif name == "M":
                        n1, q = 4 * b + (4 + g - 1), (g - 1) % 2
                        pe.wait_ge(s_spl, 4 * n1 + 4)
                        pe.wait_ge(*last_left(s_nmT, n1 + 1))
                        for i in range(NT):
                            last = pe.transpose(pMb[0:3 * G, i * P:(i + 1) * P], nsplit[q][:, i, :, :].rearrange("p c h -> p (c h)"), identb[:, :])
                        last.then_inc(s_mt, 1)
                    elif name == "N":
                        slot = 4 * b + (g - 1)
                        pe.wait_ge(s_oT, slot + 1)
                        pe.wait_ge(*last_left(s_n, slot + 1))
                        turn(lambda i: oT[:, i * P:(i + 1) * P], s_nt)
                    elif name == "X":
                        pe.wait_ge(s_norm[0], n + 1)
                        pe.wait_ge(*last_left(s_xnT, n + 1))
                        turn(lambda i: xn[:, i, :], s_xt)
                    elif name in ("Q", "K"):
                        c = int(name == "K")
                        pe.wait_ge(s_xnT, n + 1)
                        pe.wait_ge(*last_left(s_res, 2 * n + c + 1))
                        pe.matmul(pM[:, :], (wk_p if c else wq_p)[:, :], xnT[pb][:, :], start=True, stop=True).then_inc(s_qk, 1)
                    elif name == "V":
                        pe.wait_ge(*last_left(s_v, n + 1))
                        for i in range(NT):
                            last = pe.matmul(pM[:, i * P:(i + 1) * P], xnT[(pb + 1) % 2][:, i * P:(i + 1) * P], w_raw[:, 2 * D:3 * D], start=True, stop=True)
                        last.then_inc(s_vmm, 1)
                    elif name == "A":
                        q = (pb + 1) % 2
                        pe.wait_ge(s_n, 4 * n + 4)
                        pe.wait_ge(*last_left(s_aT, n + 1))
                        turn(lambda i: on[q][:, i, :], s_at)
                    elif name == "PROJ":
                        pe.wait_ge(s_aT, n + 1)
                        pe.wait_ge(*last_left(s_z, n + 1))
                        for i in range(NT):
                            last = pe.matmul(pM[:, i * P:(i + 1) * P], aT[:, i * P:(i + 1) * P], wp[:, :], start=True, stop=True)
                        last.then_inc(s_pj, 1)
                    elif name == "T":
                        pe.wait_ge(s_norm[2], n + 1)
                        pe.wait_ge(*last_left(s_tT, n + 1))
                        turn(lambda i: rows[pb][0][:, i, 0:D], s_tt)
                    elif name == "R":
                        pe.wait_ge(s_tT, n + 1)
                        pe.wait_ge(*last_left(s_lg, LG * n + 1))
                        for i in range(NT):
                            last = pe.matmul(pM[:, i * E:(i + 1) * E], tT[:, i * P:(i + 1) * P], wr[:, :], start=True, stop=True)
                        last.then_inc(s_r, 1)
                    elif name == "C":
                        pe.wait_ge(s_lg, LG * n + 11)
                        pe.wait_ge(*last_left(s_cs, CS * n + 2))
                        for i in range(NT):
                            pe.matmul(pM[:, i * E:(i + 1) * E], before[:, :], hotb[:, i, :], start=(i == 0), stop=False, skip_group_check=True)
                            for j in range(i):
                                pe.matmul(pM[:, i * E:(i + 1) * E], onesb[:, :], hotb[:, j, :], start=False, stop=False, skip_group_check=True)
                        for j in range(NT):
                            last = pe.matmul(pM[:, NT * E:(NT + 1) * E], onesb[:, :], hotb[:, j, :], start=False, stop=(j == NT - 1), skip_group_check=True)
                        last.then_inc(s_cp, 1)
                walk(has, do)

            steps(pe, step)

            pe.wait_ge(s_tb, TB_COLS)
            pe.wait_ge(*last_use[0])
            for j in range(2):
                last = pe.matmul(pM[0:1, j * P:(j + 1) * P], tv[:, 4 + j:5 + j], ident[:, :], start=True, stop=True)
            last.then_inc(s_tm, 1)
            pe.wait_ge(s_tb, TB_END)
            pe.wait_ge(s_w1, 16 * 4)
            pe.wait_ge(s_w2, 16 * 5)

            def experts(t):
                word = pe.value_load(table[0:1, 0, t:t + 1] if isinstance(t, int) else table[0:1, 0, bass.ds(t, 1)],
                                     min_val=0, max_val=E ** 4 - 1)
                return [(word // E ** j) % E for j in range(XG)]

            def turn_rows(t, q):
                pe.wait_ge(s_g[q], due(4 * (t - q) + 16))
                pe.wait_ge(s_gT, due(t))
                pe.transpose(pM[:, 0:P], xg[q][:, 0:D], ident[:, :]).then_inc(s_gt, 1)

            def first(t, q):
                pe.wait_ge(s_gT, t + 1)
                pe.wait_ge(s_wc, t + 1)
                if not isinstance(t, int) or t >= 2:
                    pe.wait_ge(s_ha, due(t - 1))
                    pe.wait_ge(s_hv, due(t - 1))
                for c in range(HC):
                    last = pe.matmul(hidden(c, q), w1c[q][:, c * P:(c + 1) * P],
                                     xgT[q % 2][:, :], start=True, stop=True)
                last.then_inc(s_h, 1)

            def second(t, q, e):
                pe.wait_ge(s_ha, t + 1)
                pe.wait_ge(s_hv, t + 1)
                if not isinstance(t, int) or t >= 2:
                    pe.wait_ge(s_yb, due(t - 1))
                for c in range(HC):
                    last = pe.matmul(pS[:, q % 2, 0:D], hid[q % 2][:, c, :], w2s[:, bass.ds(e, 1), c, :].rearrange("p e m -> p (e m)"), start=(c == 0), stop=(c == HC - 1))
                last.then_inc(s_y, 1)

            turn_rows(0, 0)
            first(0, 0)
            turn_rows(1, 1)
            e = experts(0)
            for t in range(XG):
                turn_rows(t + 2, (t + 2) % XG)
                first(t + 1, (t + 1) % XG)
                second(t, t, e[t])
            with pe.Fori(XG, TILES - XG, XG) as t:
                e = experts(t)
                for q in range(XG):
                    turn_rows(t + (q + 2), (q + 2) % XG)
                    first(t + (q + 1), (q + 1) % XG)
                    second(t + q, q, e[q])
            e = experts(TILES - XG)
            for t in range(TILES - XG, TILES):
                if t + 2 < TILES:
                    turn_rows(t + 2, (t + 2) % XG)
                if t + 1 < TILES:
                    first(t + 1, (t + 1) % XG)
                second(t, t % XG, e[t % XG])

        @block.vector
        def _(dve):
            dve.memset(ones_pair[:, :], ONES_PAIR).then_inc(s_one, 1)
            for tile_ in va:
                dve.memset(tile_[:, :, :, HD:HD + 1], 1.0)
            dve.memset(pO[:, :], 0.0).then_inc(s_zero, 1)
            dve.memset(ks[64:MROW, 0, :, :].rearrange("p h t -> p (h t)").bitcast(F32), 0.0).then_inc(s_zk, 1)
            dve.wait_ge(s_w, 16 * 8)
            for j, w in enumerate((wq_p, wk_p)):
                dve.tensor_copy(w[:, :].rearrange("p (g d h) -> p g d h", g=2, d=HD),
                                w_raw[:, j * D:(j + 1) * D].rearrange("p (g h d) -> p g d h", g=2, h=HH)).then_inc(s_wperm, 1)
            dve.wait_ge(s_b1t, 1)
            dve.tensor_copy(w1s[:, :, HID:HID + HC], pM[:, 0:E * HC].rearrange("p (e c) -> p e c", e=E)).then_inc(s_b1, 1)
            dve.wait_ge(s_const, 1)


            def step(b, pb, has):
                def do(name, k, g):
                    n = b + k
                    if name == "U":
                        u, slot, q = k, 4 * b + (4 + g), g % 2
                        if u == 0:
                            dve.wait_ge(s_spl, due(4 * slot - 4))
                        dve.wait_ge(s_u, 6 * slot + u + 1)
                        pair, kind = u // 3, u % 3
                        hs = slice(2 * pair, 2 * pair + 2)
                        if kind == 0:
                            last = dve.tensor_reduce(nmax[q][:, 3, hs], pU[:, u % 2, :, :], AX.X, ALU.max, negate=True)
                        elif kind == 1:
                            dve.tensor_reduce(nmax[q][:, 2, hs], pU[:, u % 2, :, 0:3 * P], AX.X, ALU.max, negate=True)
                            last = dve.tensor_reduce(nmax[q][:, 0, hs], pU[:, u % 2, :, 3 * P:4 * P], AX.X, ALU.max, negate=True)
                        else:
                            last = dve.tensor_reduce(nmax[q][:, 1, hs], pU[:, u % 2, 0, :].rearrange("p (h k) -> p h k", h=2), AX.X, ALU.max, negate=True)
                        last.then_inc(s_red, 1)
                    elif name == "N":
                        slot, gm, q = 4 * b + (g - 1), (g - 1) % 4, pb if g else (pb + 1) % 2
                        o4 = pM[:, :].rearrange("p (i h c) -> p i h c", i=NT, h=G)
                        dve.wait_ge(s_nt, slot + 1)
                        dve.reciprocal(rsum[:, :, :], o4[:, :, :, HD]).then_inc(s_rs, 1)
                        dve.wait_ge(s_rs, slot + 1)
                        if gm == 0:
                            dve.wait_ge(s_at, due((b if g else b - 1) - 1))
                        dve.tensor_tensor(on[q][:, :, 32 * gm:32 * gm + 32].rearrange("p i (h d) -> p i h d", h=G), o4[:, :, :, 0:HD],
                                          rsum[:, :, :, None].to_broadcast([P, NT, G, HD]), ALU.mult).then_inc(s_n, 1)
                    elif name in ("Q", "K"):
                        c = int(name == "K")
                        dve.wait_ge(s_hi, 2 * n + c + 1)
                        dve.wait_ge(s_lo, 2 * n + c)
                        dve.tensor_tensor(resid[:, :], pM[:, :], parts[c][:, 0, :], ALU.subtract).then_inc(s_res, 1)
                    elif name in ("LN1S0", "LN1S1", "LN2S0", "LN2S1", "LN3S0", "LN3S1"):
                        j, half = int(name[2]) - 1, int(name[4])
                        if j == 0:
                            src = xin[pb]
                            dve.wait_ge(s_x[pb], due(8 * (n - pb) + 16))
                        elif j == 1:
                            src = z
                            dve.wait_ge(s_z, n + 1)
                        else:
                            src = x1w
                            dve.wait_ge(s_x1, 2 * n + 2)
                        for i in range(2 * half, 2 * half + 2):
                            last = dve.bn_stats(stats[:, j, i, :], src[:, i, :])
                        if not half:
                            return
                        last.then_inc(s_stat[j], 1)
                        dve.wait_ge(s_coef[j], held(dve, 4 * n))
                        dve.wait_ge(s_stat[j], held(dve, n + 1))
                        for i in range(NT):
                            last = dve.bn_aggr(mv[:, j, i, :], stats[:, j, i, :])
                        last.then_inc(s_mv[j], 1)
                        if j == 0 and isinstance(n, int) and n == 0:
                            dve.memset(ks[64:MROW, 1, :, :].rearrange("p h t -> p (h t)").bitcast(F32), 0.0).then_inc(s_zk, 1)
                    elif name == "PROJ":
                        dve.wait_ge(s_pj, n + 1)
                        dve.wait_ge(s_xb, 2 * n + 1)
                        dve.wait_ge(s_x1, due(2 * n))
                        dve.tensor_tensor(z[:, :, :], pM[:, :].rearrange("p (i d) -> p i d", i=NT), xnr[:, :, :], ALU.add).then_inc(s_z, 1)
                    elif name == "R":
                        a = LG * n
                        dve.wait_ge(s_r, n + 1)
                        dve.tensor_tensor(logit[:, :, :], pM[:, 0:NT * E].rearrange("p (i e) -> p i e", i=NT),
                                          brb[:, None, :].to_broadcast([P, NT, E]), ALU.add).then_inc(s_lg, 1)
                        dve.wait_ge(s_lg, a + 1)
                        dve.tensor_reduce(lmax[:, :], logit[:, :, :], AX.X, ALU.max, negate=True).then_inc(s_lg, 1)
                        dve.wait_ge(s_lg, a + 2)
                        dve.tensor_tensor(lsub[:, :, :], logit[:, :, :], lmax[:, :, None].to_broadcast([P, NT, E]), ALU.add).then_inc(s_lg, 1)
                    elif name == "TOP":
                        a = LG * n
                        dve.wait_ge(s_le, n + 1)
                        dve.tensor_reduce(psum_[:, :], pe_[:, :, :], AX.X, ALU.add).then_inc(s_lg, 1)
                        dve.wait_ge(s_lg, a + 4)
                        dve.reciprocal(prec[:, :], psum_[:, :]).then_inc(s_lg, 1)
                        dve.wait_ge(s_lg, a + 5)
                        dve.tensor_tensor(prob[:, :, :], pe_[:, :, :], prec[:, :, None].to_broadcast([P, NT, E]), ALU.mult).then_inc(s_lg, 1)
                        dve.wait_ge(s_lg, held(dve, a + 6))
                        for i in range(NT):
                            last = dve.max(top_v[:, i, :], prob[:, i, :])
                        last.then_inc(s_lg, 1)
                        dve.wait_ge(s_lg, held(dve, a + 7))
                        for i in range(NT):
                            last = dve.max_index(top_i[:, i, :], top_v[:, i, :], prob[:, i, :])
                        last.then_inc(s_lg, 1)
                        dve.wait_ge(s_lg, a + 8)
                        dve.tensor_copy(top_f[:, :, :], top_i[:, :, :]).then_inc(s_lg, 1)
                        dve.wait_ge(s_lg, a + 9)
                        for c in range(2):
                            last = dve.tensor_tensor(hot[:, c, :, :], iota_e[:, None, :].to_broadcast([P, NT, E]),
                                                     top_f[:, :, c:c + 1].to_broadcast([P, NT, E]), ALU.is_equal)
                        last.then_inc(s_lg, 1)
                        dve.wait_ge(s_lg, a + 10)
                        dve.tensor_tensor(hotb[:, :, :], hot[:, 0, :, :], hot[:, 1, :, :], ALU.add).then_inc(s_lg, 1)
                    elif name == "C":
                        a, q = CS * n, pb
                        dve.wait_ge(s_cp, n + 1)
                        dve.tensor_tensor(place[:, :, :], pM[:, 0:NT * E].rearrange("p (i e) -> p i e", i=NT),
                                          base[:, None, :].to_broadcast([P, NT, E]), ALU.add).then_inc(s_cs, 1)
                        dve.wait_ge(s_cs, a + 1)
                        dve.tensor_tensor(base[:, :], pM[:, NT * E:(NT + 1) * E], base[:, :], ALU.add).then_inc(s_cs, 1)
                        dve.wait_ge(s_cs, a + 2)
                        for c in range(2):
                            last = dve.tensor_tensor(picked[:, c, :, :], place[:, :, :], hot[:, c, :, :], ALU.mult)
                        last.then_inc(s_cs, 1)
                        dve.wait_ge(s_cs, a + 3)
                        dve.tensor_reduce(dest_f[:, :, :], picked[:, :, :, :], AX.X, ALU.add).then_inc(s_cs, 1)
                        dve.wait_ge(s_cs, a + 4)
                        if isinstance(n, int):
                            dve.wait_ge(s_sc[q], due(64 * (n - q)))
                        dve.tensor_copy(dest[q][:, :, :], dest_f[:, :, :]).then_inc(s_cs, 1)
                        for c in range(2):
                            dve.tensor_copy(rows[q][c][:, :, D + 1], top_v[:, :, c])
                            last = dve.tensor_scalar(rows[q][c][:, :, D], res_row[:, :], float(c), None, ALU.add)
                        last.then_inc(s_cs, 1)
                        dve.wait_ge(s_cs, a + 6)
                        dve.tensor_scalar(res_row[:, :], res_row[:, :], float(2 * T), None, ALU.add).then_inc(s_cs, 1)
                        dve.wait_ge(s_cs, a + 7)
                walk(has, do)

            steps(dve, step)

            dve.wait_ge(s_cs, CS * B)
            link = [0]

            def chain(ins):
                link[0] += 1
                ins.then_inc(s_tb, 1)
                dve.wait_ge(s_tb, link[0])

            chain(dve.tensor_copy(pad_at[:, :], base[0:1, :]))
            assert link[0] == TB_PAD
            chain(dve.tensor_tensor(cnt[:, :], base[:, :], region[:, :], ALU.subtract))
            chain(dve.tensor_scalar(cnt_i[:, :], cnt[:, :], float(P - 1), None, ALU.add))
            chain(dve.tensor_scalar(nt_i[:, :], cnt_i[:, :], 7, None, ALU.arith_shift_right))
            chain(dve.tensor_copy(nt_f[:, :], nt_i[:, :]))
            chain(dve.tensor_tensor(cum3[:, :, :], upto[:, :, :], nt_f[:, None, :].to_broadcast([P, E, E]), ALU.mult))
            chain(dve.tensor_reduce(cum[:, :], cum3[:, :, :], AX.X, ALU.add))
            chain(dve.tensor_scalar(done[:, :], cum[:, :], tile_no[:, 0:1], None, ALU.is_le))
            chain(dve.tensor_reduce(tv[:, 0:1], done[:, :], AX.X, ALU.add))
            chain(dve.tensor_tensor(skipped[:, :], done[:, :], nt_f[:, :], ALU.mult))
            chain(dve.tensor_reduce(tv[:, 1:2], skipped[:, :], AX.X, ALU.add))
            chain(dve.tensor_tensor(tv[:, 2:3], tile_no[:, :], tv[:, 1:2], ALU.subtract))
            chain(dve.tensor_scalar(tv[:, 3:4], tv[:, 0:1], float(E), float(P), ALU.is_lt, ALU.mult))
            chain(dve.tensor_tensor(tv[:, 2:3], tv[:, 2:3], tv[:, 3:4], ALU.mult))
            chain(dve.tensor_scalar(tv[:, 4:5], tv[:, 0:1], float(E - 1), None, ALU.min))
            chain(dve.scalar_tensor_tensor(out=tv[:, 5:6], in0=tv[:, 0:1], scalar=float(ROWS), in1=tv[:, 2:3], op0=ALU.mult, op1=ALU.add))
            assert link[0] == TB_COLS
            dve.wait_ge(s_tm, 1)
            chain(dve.tensor_copy(table_f[:, :, :], pM[0:1, 0:2 * P].rearrange("p (j t) -> p j t", j=2)))
            for d in (1, 2):
                n = P - d
                chain(dve.scalar_tensor_tensor(out=table_f[:, 0, 0:n], in0=table_f[:, 0, d:P], scalar=float(E ** d),
                                               in1=table_f[:, 0, 0:n], op0=ALU.mult, op1=ALU.add))
            chain(dve.tensor_copy(table[:, :, :], table_f[:, :, :]))
            assert link[0] == TB_END
            dve.wait_ge(s_w2, 16 * 5)
            dve.wait_ge(s_w1, 16 * 4)

            def experts(t):
                word = dve.value_load(table[0:1, 0, t:t + 1] if isinstance(t, int) else table[0:1, 0, bass.ds(t, 1)],
                                      min_val=0, max_val=E ** 4 - 1)
                return [(word // E ** j) % E for j in range(XG)]

            def rows_T(t, q, e):
                dve.wait_ge(s_gt, t + 1)
                if not isinstance(t, int) or t >= 2:
                    dve.wait_ge(s_h, due(t - 1))
                dve.tensor_copy(xgT[q % 2][:, :], pM[:, 0:P]).then_inc(s_gT, 1)
                if not isinstance(t, int) or t >= XG:
                    dve.wait_ge(s_ha, due(t - XG + 1))
                    dve.wait_ge(s_hv, due(t - XG + 1))
                    dve.wait_ge(s_yb, due(t - XG + 1))
                dve.tensor_copy(w1c[q][:, :], w1s[:, bass.ds(e, 1), :].rearrange("p e h -> p (e h)")).then_inc(s_wc, 1)
                if not isinstance(t, int) or t >= XG:
                    dve.wait_ge(s_ys[q % 2], due(8 * (t - XG - q % 2) + 16))
                    dve.wait_ge(s_yg, due(t - XG + 1))
                dve.tensor_copy(ydest[q][:, :], xg[q][:, D:D + 1])
                dve.tensor_copy(ygate[q][:, :], xg[q][:, D + 1:D + 2]).then_inc(s_yi, 1)
                dve.tensor_copy(b2c[q], b2b[:, bass.ds(e, 1), :].rearrange("p e m -> p (e m)")).then_inc(s_bc, 1)

            def act_last(t, q):
                dve.wait_ge(s_h, t + 1)
                if not isinstance(t, int) or t >= 2:
                    dve.wait_ge(s_y, due(t - 1))
                c = HC - 1
                dve.tensor_scalar(hid[q % 2][:, c, :], hidden(c, q),
                                  w1c[q][:, HID + c:HID + c + 1], 0.0, ALU.add, ALU.max).then_inc(s_hv, 1)

            def bias(t, q):
                dve.wait_ge(s_y, t + 1)
                dve.wait_ge(s_bc, t + 1)
                if not isinstance(t, int) or t >= 2:
                    dve.wait_ge(s_yg, due(t - 1))
                dve.tensor_tensor(yb[q % 2][:, :], pS[:, q % 2, 0:D], b2c[q], ALU.add).then_inc(s_yb, 1)

            e = experts(0)
            rows_T(0, 0, e[0])
            rows_T(1, 1, e[1])
            act_last(0, 0)
            e = experts(2)
            for t in range(XG):
                rows_T(t + 2, (t + 2) % XG, e[t])
                act_last(t + 1, (t + 1) % XG)
                bias(t, t)
            with dve.Fori(XG, TILES - XG, XG) as t:
                e = experts(t + 2)
                for q in range(XG):
                    rows_T(t + (q + 2), (q + 2) % XG, e[q])
                    act_last(t + (q + 1), (q + 1) % XG)
                    bias(t + q, q)
            e = experts(TILES - XG + 2)
            for t in range(TILES - XG, TILES):
                if t + 2 < TILES:
                    rows_T(t + 2, (t + 2) % XG, e[t % XG])
                if t + 1 < TILES:
                    act_last(t + 1, (t + 1) % XG)
                bias(t, t % XG)

            for n in range(B):
                dve.wait_ge(s_fin[n], 16)
                dve.tensor_tensor(fin[:, n, :, 0, :], fin[:, n, :, 0, :], fin[:, n, :, 1, :], ALU.add).then_inc(s_f1, 1)
                dve.wait_ge(s_f1, n + 1)
                dve.wait_ge(s_x1d, 16 * B)
                dve.tensor_tensor(x1[:, NT * n:NT * n + NT, :], x1[:, NT * n:NT * n + NT, :], fin[:, n, :, 0, :], ALU.add).then_inc(s_f2, 1)


_INS = ["L0_attn_target", "L0_attn_w_qkv", "L0_attn_w_proj", "L0_attn_b_proj", "L0_attn_ln_gamma", "L0_attn_ln_beta",
        "L0_ffn_Wr", "L0_ffn_br", "L0_ffn_W1", "L0_ffn_b1", "L0_ffn_W2", "L0_ffn_b2"]


def kernel(**inputs):
    import numpy as np
    import concourse.bacc as bacc
    from concourse.bass_utils import run_bass_kernel_spmd

    nc = bacc.Bacc("TRN2", target_bir_lowering=False, num_devices=1)
    arrays, args = {}, []
    for name in _INS:
        a = np.ascontiguousarray(inputs[name])
        arrays[name] = a
        args.append(nc.dram_tensor(name, a.shape, mybir.dt.from_np(a.dtype), kind="ExternalInput").ap())
    shape = inputs["L0_attn_target"].shape
    args.append(nc.dram_tensor("out", shape, F32, kind="ExternalOutput").ap())
    moe_block(nc, *args)
    return run_bass_kernel_spmd(nc, [arrays], core_ids=[0]).results[0]["out"]
```

```python
from contextlib import ExitStack

import numpy as np

import concourse.bass as bass
from concourse import mybir

F32 = mybir.dt.float32
BF16 = mybir.dt.bfloat16
I32 = mybir.dt.int32
U32 = mybir.dt.uint32
ALU = mybir.AluOpType
ACT = mybir.ActivationFunctionType
AX = mybir.AxisListType

P = 128
EPS = 1e-5
MASKED = -1e30
ONES_PAIR = float(np.array([0x3F803F80], np.uint32).view(np.float32)[0])
SKIP = 1 << 20

SLOT = [
    ("S", 0), ("PVL", 1), ("S", 1), ("U", 0), ("x", 0), ("S", 2), ("U", 1), ("S", 3), ("x", 1), ("PVL", 2),
    ("SEL", 0), ("M", 0), ("S", 4), ("PVL", 3), ("U", 2), ("OE", 0), ("x", 2), ("x", 3), ("S", 5), ("S", 6), ("U", 3),
    ("N", 0), ("S", 7), ("SEL", 1), ("S", 8), ("x", 4), ("U", 4), ("S", 9), ("PV", 0), ("U", 5), ("SEL", 2), ("x", 5),
    ("S", 10), ("SPLIT", 0), ("SEL", 3), ("x", 6),
]
EXTRA = {
    (0, 0): [("LOADX", 2), ("T", -2)],
    (0, 1): [("W10", 0), ("LN1S0", 2)],
    (0, 2): [("LN1S1", 2), ("W12", 0)],
    (0, 3): [("XB0", -1), ("R", -2)],
    (0, 4): [("STB", 1)],
    (0, 5): [("XB1", -1), ("TOP", -2), ("LN1C", 2)],
    (0, 6): [("A", -1), ("W13", 0)],
    (1, 0): [("PROJ", -1), ("LN1N0", 2)],
    (1, 2): [("C", -2), ("SCATTER0", -2), ("COPY", -2)],
    (1, 3): [("SCATTER1", -2)],
    (1, 4): [("LN1N1", 2)],
    (1, 5): [("LN2S0", -1), ("LN2S1", -1)],
    (1, 6): [("LN2C", -1), ("SCATTER2", -2), ("X", 2)],
    (2, 0): [("Q", 2)],
    (2, 1): [("Q2", 2), ("SCATTER3", -2)],
    (2, 2): [("LN2N0", -1), ("K", 2)],
    (2, 3): [("LN2N1", -1), ("X1A", -1)],
    (2, 4): [("X1B", -1), ("K2", 2), ("QOUT", 2)],
    (2, 5): [("LN3S0", -1)],
    (2, 6): [("LN3S1", -1)],
    (3, 0): [("KOUT", 2), ("SCATTER4", -2), ("SCATTER5", -2), ("STA", 2)],
    (3, 1): [("RELOAD", 0)],
    (3, 2): [("W11", 0), ("LN3C", -1), ("STORE1", -1)],
    (3, 3): [("SCATTER6", -2)],
    (3, 4): [("SCATTER7", -2)],
    (3, 5): [("LN3N0", -1), ("LN3N1", -1)],
    (3, 6): [("V", 1), ("LEFT", -2)],
}
DRAIN = [
    ("PVL", 1), ("T", -2), ("XB0", -1), ("PVL", 2), ("PVL", 3), ("OE", 0), ("R", -2), ("XB1", -1), ("N", 0),
    ("TOP", -2), ("A", -1), ("C", -2), ("SCATTER0", -2), ("COPY", -2), ("SCATTER1", -2), ("PROJ", -1), ("LN2S0", -1),
    ("LN2S1", -1), ("LN2C", -1), ("SCATTER2", -2), ("LN2N0", -1), ("LN2N1", -1), ("SCATTER3", -2), ("X1A", -1),
    ("X1B", -1), ("SCATTER4", -2), ("LN3S0", -1), ("LN3S1", -1), ("LN3C", -1), ("SCATTER5", -2), ("SCATTER6", -2),
    ("SCATTER7", -2), ("STORE1", -1), ("LN3N0", -1), ("LN3N1", -1), ("T", -1), ("COPY", -1), ("R", -1), ("TOP", -1),
    ("C", -1), ("SCATTER0", -1), ("SCATTER1", -1), ("SCATTER2", -1), ("SCATTER3", -1), ("SCATTER4", -1),
    ("SCATTER5", -1), ("SCATTER6", -1), ("SCATTER7", -1),
]


def moe_block(nc, x_in, w_qkv, w_proj, b_proj, gamma, beta, w_r, b_r, w1, b1, w2, b2, out):
    B, T, D = x_in.shape
    E, _, HID = w1.shape
    H, HD, G = 16, D // 16, 4
    HH = H // 2
    NT = T // P
    NS = H // G
    ROWS = T * B + P
    TILES = (2 * B * T + E * (P - 1)) // P
    TILES += TILES % 2
    HC = HID // P
    RW = D + 2
    KQ = 9 * HD
    MROW = 96
    POOL_ADDS = range(0, B, 3)
    SCALE = float(HD) ** -0.5
    assert D == P and NT == 4 and NS == 4 and B % 2 == 0

    routed = nc.dram_tensor("routed_rows", [E * ROWS + P, RW], F32).ap()
    results = nc.dram_tensor("result_rows", [2 * B * T, D], F32).ap()
    xn_store = nc.dram_tensor("xn_store", [B, T, D], F32).ap()
    q_parts = nc.dram_tensor("q_parts", [2, 3, 2, HD, HH * T], BF16).ap()
    k_parts = nc.dram_tensor("k_parts", [2, 2, 3, HD, HH * T], BF16).ap()

    ctx = ExitStack()
    with ctx:
        def sb(name, shape, dt=F32):
            return ctx.enter_context(nc.sbuf_tensor(name, shape, dt))

        def sem(name):
            return ctx.enter_context(nc.semaphore(name))

        ident = sb("ident", [P, P])
        identb = sb("identb", [P, P], BF16)
        maskneg = sb("maskneg", [P, 2, P], BF16)
        before = sb("before", [P, P], BF16)
        onesb = sb("onesb", [P, P], BF16)
        iota_i = sb("iota_i", [P, 64], I32)
        iota_e = sb("iota_e", [P, E])
        region = sb("region", [P, E])
        tile_no = sb("tile_no", [P, 1])
        upto = sb("upto", [P, E, E])
        res_row = sb("res_row", [P, NT])
        neg_half = sb("neg_half", [P, NT])
        w_raw = sb("w_raw", [P, 3 * D])
        wq_p = sb("wq_p", [P, D])
        wk_p = sb("wk_p", [P, D])
        wp = sb("wp", [P, D])
        wr = sb("wr", [P, E])
        brb = sb("brb", [P, E])
        gammab = sb("gammab", [P, D])
        betab = sb("betab", [P, D])
        bprojb = sb("bprojb", [P, D])
        b1row = sb("b1row", [E * HC, P])
        w1s = sb("w1s", [P, E, HID + HC])

        ones_pair = sb("ones_pair", [P, 1])

        xin = [sb(f"xin{i}", [P, NT, D]) for i in range(2)]
        xn = sb("xn", [P, NT, D])
        xnT = [sb(f"xnT{i}", [P, T]) for i in range(2)]
        parts = [sb(f"parts{i}", [P, 3, T], BF16) for i in range(2)]
        resid = sb("resid", [P, T])
        qs = sb("qs", [P, 2, H, T], BF16)
        ks = sb("ks", [P, 2, H, T], BF16)
        va = [sb(f"va{i}", [P, NT, H, HD + 1]) for i in range(2)]
        nmax = [sb(f"nmax{i}", [P, G, NT]) for i in range(2)]
        nres = sb("nres", [P, G, NT])
        nsplit = [sb(f"nsplit{i}", [P, 3, G, NT], BF16) for i in range(2)]
        nmT = [sb(f"nmT{i}", [3 * G * NT, P], BF16) for i in range(2)]
        pr = sb("pr", [P, G * (512 + 384 + 256 + 128)])
        oT = sb("oT", [P, T])
        rsum = sb("rsum", [P, NT, G])
        on = [sb(f"on{i}", [P, NT, D]) for i in range(2)]
        aT = sb("aT", [P, T])
        xr = sb("xr", [P, NT, D])
        xnr = sb("xnr", [P, NT, D])
        z = sb("z", [P, NT, D])
        x1w = sb("x1w", [P, NT, D])
        x1 = sb("x1", [P, B * NT, D])
        stats = sb("stats", [P, 3, NT, 6])
        mv = sb("mv", [P, 3, NT, 2])
        veps = sb("veps", [P, 3, NT])
        rstd = sb("rstd", [P, 3, NT])
        nmr0 = sb("nmr0", [P, 3, NT])
        nmr = sb("nmr", [P, 3, NT])

        rows = [[sb(f"rows{i}{c}", [P, NT, RW]) for c in range(2)] for i in range(2)]
        tT = sb("tT", [P, T])
        logit = sb("logit", [P, NT, E])
        lmax = sb("lmax", [P, NT])
        lsub = sb("lsub", [P, NT, E])
        pexp = sb("pexp", [P, NT, E])
        prob_sum = sb("prob_sum", [P, NT])
        prec = sb("prec", [P, NT])
        prob = sb("prob", [P, NT, E])
        top_v = sb("top_v", [P, NT, 8])
        top_i = sb("top_i", [P, NT, 8], U32)
        top_f = sb("top_f", [P, NT, 8])
        hot = sb("hot", [P, 2, NT, E])
        hotb = sb("hotb", [P, NT, E], BF16)
        place = sb("place", [P, NT, E])
        picked = sb("picked", [P, 2, NT, E])
        dest_f = sb("dest_f", [P, 2, NT])
        dest = [sb(f"dest{i}", [P, 2, NT], U32) for i in range(2)]
        base = sb("base", [P, E])

        cnt = sb("cnt", [P, E])
        cnt_i = sb("cnt_i", [P, E], I32)
        nt_i = sb("nt_i", [P, E], I32)
        nt_f = sb("nt_f", [P, E])
        cum3 = sb("cum3", [P, E, E])
        cum = sb("cum", [P, E])
        done = sb("done", [P, E])
        skipped = sb("skipped", [P, E])
        tv = sb("tv", [P, 6])
        table_f = sb("table_f", [1, 2, P])
        table = sb("table", [1, 2, P], I32)
        pad_at = sb("pad_at", [1, E], I32)
        pad_rows = sb("pad_rows", [P, RW])
        XG = 4
        xg = [sb(f"xg{i}", [P, RW]) for i in range(XG)]
        xgT = [sb(f"xgT{i}", [P, P]) for i in range(2)]
        w1c = ([parts[i][:, :, :].rearrange("p c t -> p (c t)").bitcast(F32)[:, 0:HID + HC] for i in range(2)]
               + [rows[i][0][:, :, :].rearrange("p i r -> p (i r)")[:, 0:HID + HC] for i in range(2)])
        b2c = [buf[:, 0, :] for buf in (xr, xnr, z)] + [resid[:, 0:D]]
        hid = [xnT[i][:, :].rearrange("p (c s) -> p c s", c=HC) for i in range(2)]
        yb = [sb(f"yb{i}", [P, D]) for i in range(2)]
        yg = [sb(f"yg{i}", [P, D]) for i in range(2)]
        ydest = [sb(f"ydest{i}", [P, 1], U32) for i in range(XG)]
        ygate = [sb(f"ygate{i}", [P, 1]) for i in range(XG)]

        def hidden(c, q):
            return pU[:, q % 2, c // 2, (c % 2) * P:(c % 2 + 1) * P]

        w2s = qs[:, :, :, :].rearrange("p a h t -> p (a h t)").bitcast(F32).rearrange("p (e c m) -> p e c m", e=E, c=HC)
        b2b = pr[:, 0:E * D].rearrange("p (e m) -> p e m", e=E)
        fin = ks[:, :, :, :].rearrange("p a h t -> p (a h t)").bitcast(F32).rearrange("p (n i c d) -> p n i c d", n=B, i=NT, c=2)
        OFF = [0, G * 512, G * 896, G * 1152]
        QN = [T - P * k for k in range(NT)]
        prob_of = [pr[:, OFF[k]:OFF[k] + G * QN[k]].rearrange("p (h q) -> p h q", h=G) for k in range(NT)]

        pU = ctx.enter_context(nc.psum_tensor("pU", [P, 2, 2, 512], F32))
        pS = ctx.enter_context(nc.psum_tensor("pS", [P, 2, 512], F32))
        pO = ctx.enter_context(nc.psum_tensor("pO", [P, 512], F32))
        pM = ctx.enter_context(nc.psum_tensor("pM", [P, 512], F32))
        pMb = pM[:, :].bitcast(BF16)

        s_pc = sem("const_steps")
        s_const = sem("const_made")
        s_one = sem("ones_pair_set")
        s_zk = sem("k_stacks_zeroed")
        s_ok = sem("k_stacks_ones")
        s_zq = sem("q_stacks_padded")
        s_b1t = sem("b1_product")
        s_zero = sem("zeroed")
        s_w = sem("small_weights_in")
        s_w1 = sem("w1_in")
        s_w2 = sem("w2_in")
        s_wperm = sem("q_k_weights_ordered")
        s_b1 = sem("b1_turned")
        s_x = [sem(f"x_in{i}") for i in range(2)]
        s_stat = [sem(f"ln{k}_stats") for k in range(3)]
        s_mv = [sem(f"ln{k}_mean_var") for k in range(3)]
        s_coef = [sem(f"ln{k}_coef") for k in range(3)]
        s_norm = [sem(f"ln{k}_normed") for k in range(3)]
        s_xout = sem("xn_stored")
        s_re = sem("x_and_xn_back")
        s_xb = sem("biases_added")
        s_xt = sem("xn_turned")
        s_xnT = sem("xnT_ready")
        s_qk = sem("q_k_product")
        s_hi = sem("q_k_high")
        s_res = sem("q_k_residue")
        s_mid = sem("q_k_middle")
        s_lo = sem("q_k_low")
        s_qout = sem("q_parts_out")
        s_kout = sem("k_parts_out")
        s_st = [sem(f"stack_in{i}") for i in range(2)]
        s_vmm = sem("v_product")
        s_v = sem("v_ready")
        s_u = sem("unit_scores")
        s_red = sem("unit_maxima")
        s_spl = sem("maxima_split")
        s_mt = sem("maxima_turned")
        s_nmT = sem("maxima_rows")
        s_mr = [sem(f"maxima_in_stack{i}") for i in range(2)]
        s_s = sem("bank_scores")
        s_e = sem("bank_exp")
        s_sel = sem("masked")
        s_pv = sem("pv_done")
        s_oT = sem("o_copied")
        s_nt = sem("o_turned")
        s_rs = sem("o_reciprocals")
        s_n = sem("o_normed")
        s_at = sem("o_rows_turned")
        s_aT = sem("aT_ready")
        s_pj = sem("proj_product")
        s_z = sem("z_ready")
        s_x1 = sem("x1_steps")
        s_x1d = sem("x1_kept")
        s_row = sem("second_rows")
        s_tt = sem("t_turned")
        s_tT = sem("tT_ready")
        s_r = sem("router_product")
        s_lg = sem("router_steps")
        s_le = sem("router_exp")
        s_cp = sem("prefix_product")
        s_cs = sem("place_steps")
        s_sc = [sem(f"scattered{i}") for i in range(2)]
        LG, CS, ST = 11, 7, 16 * 4
        s_tb = sem("table_steps")
        TB_PAD, TB_COLS, TB_END = 1, 16, 20
        s_tm = sem("table_product")
        s_pad = sem("padding_stored")
        s_g = [sem(f"rows_in{i}") for i in range(XG)]
        s_gt = sem("rows_turned")
        s_gT = sem("xgT_ready")
        s_wc = sem("w1_of_tile")
        s_bc = sem("b2_of_tile")
        s_h = sem("hidden_product")
        s_ha = sem("hidden_act")
        s_hv = sem("hidden_act_vector")
        s_y = sem("y_product")
        s_yb = sem("y_bias")
        s_yi = sem("y_rows_known")
        s_yg = sem("y_gated")
        s_ys = [sem(f"y_stored{i}") for i in range(2)]
        s_fin = [sem(f"results_in{i}") for i in range(B)]
        s_f1 = [sem(f"results_added{i}") for i in range(B)]
        s_f2 = [sem(f"x1_added{i}") for i in range(B)]
        s_out = sem("out_stored")

        def due(n):
            return max(n, 0) if isinstance(n, int) else n

        def held(eng, n):
            if isinstance(n, int):
                return due(n)
            n = eng.to_reg(n)
            eng.wait_ge(s_const, 1)
            return n

        def steps(eng, step):
            def has(b):
                return lambda k: 0 <= b + k < B
            for b in range(-2, 2):
                step(b, b % 2, has(b))
            with eng.Fori(1, B // 2 - 1) as i:
                step(2 * i, 0, lambda k: True)
                step(2 * i + 1, 1, lambda k: True)
            for b in range(B - 2, B):
                step(b, b % 2, has(b))
            step(B, 0, None)

        def walk(has, do):
            if has is None:
                for name, i in DRAIN:
                    do(name, i, 0)
                return
            for g in range(NS):
                for name, i in SLOT:
                    if name == "x":
                        for what, k in EXTRA.get((g, i), []):
                            if has(k):
                                do(what, k, g)
                    elif name in ("U", "SPLIT"):
                        if has(1):
                            do(name, i, g)
                    elif name == "M":
                        if has(1) if g else has(0):
                            do(name, i, g)
                    elif name in ("PVL", "OE", "N"):
                        if has(0) if g else has(-1):
                            do(name, i, g)
                    elif has(0):
                        do(name, i, g)

        block = ctx.enter_context(nc.Block())

        @block.sync
        def _(sp):
            small = [(w_raw[:, :], w_qkv), (wp[:, :], w_proj), (wr[:, :], w_r),
                     (brb[:, :], b_r.partition_broadcast(P)), (gammab[:, :], gamma.partition_broadcast(P)),
                     (betab[:, :], beta.partition_broadcast(P)), (bprojb[:, :], b_proj.partition_broadcast(P)),
                     (b1row[:, :], b1.rearrange("e (c p) -> (e c) p", p=P))]
            for n in range(2):
                sp.dma_start(xin[n][:, :, :], x_in[n].rearrange("(i p) d -> p i d", p=P)).then_inc(s_x[n], 16)
            for dst, src in small:
                sp.dma_start(dst, src).then_inc(s_w, 16)

            def stack(n, q, half):
                sp.wait_ge(s_qout, held(sp, 16 * n + 16))
                sp.wait_ge(s_kout, held(sp, 32 * n + 32))
                sp.wait_ge(s_s, held(sp, 44 * (n - 2) + 22 * (half + 1)))
                sp.wait_ge(s_st[half], held(sp, ST * n))
                if isinstance(n, int) and n < 2:
                    sp.wait_ge(s_zk, n + 1)
                    sp.wait_ge(s_zq, n + 1)
                heads = slice(HH * half, HH * half + HH)
                for i in range(3):
                    sp.dma_start(qs[3 * HD * i:3 * HD * (i + 1), q, heads, :],
                                 q_parts[q, i, half][None, :, :].to_broadcast([3, HD, HH * T])).then_inc(s_st[half], 16)
                sp.dma_start(ks[0:KQ, q, heads, :],
                             k_parts[q, half].rearrange("j d n -> (j d) n")[None, :, :].to_broadcast([3, 3 * HD, HH * T]))\
                    .then_inc(s_st[half], 16)

            def second_weights():
                sp.wait_ge(s_s, 11 * NS * B)
                for q in range(2):
                    sp.wait_ge(s_mr[q], 16 * NS * B // 2)
                for e in range(0, E, 4):
                    sp.dma_start(w2s[:, e:e + 4, :, :].rearrange("p e c m -> p (e c) m"),
                                 w2[e:e + 4].rearrange("e (c p) m -> p (e c) m", p=P)).then_inc(s_w2, 16)

            def step(b, pb, has):
                if isinstance(b, int) and b == B:
                    second_weights()

                def do(name, k, g):
                    if name == "LOADX":
                        n, q = b + k, (pb + k) % 2
                        if isinstance(n, int) and n < 2:
                            return
                        sp.wait_ge(s_norm[0], held(sp, n - 1))
                        sp.dma_start(xin[q][:, :, :], x_in[n].rearrange("(i p) d -> p i d", p=P)).then_inc(s_x[q], 16)
                    elif name == "X":
                        n = b + k
                        sp.wait_ge(s_norm[0], held(sp, n + 1))
                        sp.dma_start(xn_store[n].rearrange("(i p) d -> p i d", p=P), xn[:, :, :]).then_inc(s_xout, 16)
                    elif name == "RELOAD":
                        n = b + k
                        sp.wait_ge(s_xout, held(sp, 16 * (n + 1)))
                        sp.wait_ge(s_x1, held(sp, 2 * n))
                        sp.dma_start(xr[:, :, :], x_in[n].rearrange("(i p) d -> p i d", p=P)).then_inc(s_re, 16)
                        sp.dma_start(xnr[:, :, :], xn_store[n].rearrange("(i p) d -> p i d", p=P)).then_inc(s_re, 16)
                    elif name[0:2] == "W1" and isinstance(b, int) and b == B - 2:
                        e = 4 * int(name[2])
                        sp.dma_start(w1s[:, e:e + 4, 0:HID], w1[e:e + 4].rearrange("e p h -> p e h")).then_inc(s_w1, 16)
                    elif name == "QOUT":
                        n = b + k
                        sp.wait_ge(s_lo, held(sp, 2 * n + 1))
                        sp.wait_ge(s_st[1], held(sp, ST * (n - 1)))
                        sp.dma_start(q_parts[pb].rearrange("i g d (h t) -> (g d h) i t", t=T), parts[0][:, :, :]).then_inc(s_qout, 16)
                    elif name == "KOUT":
                        n = b + k
                        sp.wait_ge(s_lo, held(sp, 2 * n + 2))
                        for half in range(2):
                            sp.dma_start(k_parts[pb, half].rearrange("j d (h t) -> (d h) j t", t=T),
                                         parts[1][64 * half:64 * half + 64, :, :]).then_inc(s_kout, 16)
                    elif name == "STA":
                        stack(b + k, pb, 0)
                    elif name == "STB":
                        stack(b + k, (pb + 1) % 2, 1)
                    elif name == "M":
                        n1 = 4 * b + (4 + g - 1)
                        q, gm = (g - 1) % 2, (g - 1) % 4
                        pq = (pb + 1) % 2 if g else pb
                        sp.wait_ge(s_nmT, held(sp, n1 + 1))
                        if not isinstance(b, int) or n1 >= 2:
                            sp.wait_ge(s_mr[q], held(sp, 8 * (n1 - q)))
                        sp.dma_start(qs[MROW:MROW + 3, pq, G * gm:G * gm + G, :], nmT[q][:, :]).then_inc(s_mr[q], 16)
                    elif name == "STORE1":
                        n = b + k
                        sp.wait_ge(s_x1, held(sp, 2 * n + 2))
                        sp.dma_start(x1[:, 4 * n:4 * n + 4, :] if isinstance(n, int) else x1[:, bass.ds(4 * n, 4), :],
                                     x1w[:, :, :]).then_inc(s_x1d, 16)
                walk(has, do)

            steps(sp, step)

            sp.wait_ge(s_pv, 4 * NS * B)
            sp.dma_start(b2b, b2.rearrange("e m -> (e m)").partition_broadcast(P).rearrange("p (e m) -> p e m", e=E))\
                .then_inc(s_w2, 16)

            sp.dma_start(routed[E * ROWS:E * ROWS + P, :], pad_rows[:, :]).then_inc(s_pad, 16)
            sp.wait_ge(s_tb, TB_PAD)
            for e in range(0, E, 2):
                at = sp.value_load(pad_at[0:1, e:e + 1], min_val=0, max_val=(e + 1) * ROWS - P)
                sp.dma_start(routed[bass.ds(at, P), :], pad_rows[:, :]).then_inc(s_pad, 16)
            sp.wait_ge(s_tb, TB_END)

            def first_row(t):
                return sp.value_load(table[0:1, 1, t:t + 1] if isinstance(t, int) else table[0:1, 1, bass.ds(t, 1)],
                                     min_val=0, max_val=E * ROWS)

            start = [first_row(t) for t in range(XG)]
            for q in range(2):
                sp.wait_ge(s_sc[q], held(sp, 16 * 2 * NT * B // 2))
            sp.wait_ge(s_pad, held(sp, 16 * (E + 1)))
            for t in range(XG):
                sp.dma_start(xg[t][:, :], routed[bass.ds(start[t], P), :]).then_inc(s_g[t], 16)
            with sp.Fori(XG, TILES, XG) as t:
                for q in range(XG):
                    at = first_row(t + q)
                    sp.wait_ge(s_gt, held(sp, t + (q - XG + 1)))
                    sp.wait_ge(s_yi, held(sp, t + (q - XG + 1)))
                    sp.dma_start(xg[q][:, :], routed[bass.ds(at, P), :]).then_inc(s_g[q], 16)

            for q in range(2):
                sp.wait_ge(s_ys[q], held(sp, 16 * TILES // 2))
            for n in range(B):
                sp.dma_start(fin[:, n].rearrange("p i c d -> p i (c d)"),
                             results.rearrange("(n i p c) d -> n p i (c d)", i=NT, p=P, c=2)[n]).then_inc(s_fin[n], 16)
            for n in range(B):
                sp.wait_ge(s_f2[n], 1)
                sp.dma_start(out[n].rearrange("(i p) d -> p i d", p=P), x1[:, NT * n:NT * n + NT, :]).then_inc(s_out, 16)
            sp.wait_ge(s_out, 16 * B)

        @block.gpsimd
        def _(pool):
            pool.memset(ident[:, :], 0.0).then_inc(s_pc, 1)
            pool.memset(maskneg[:, :, :], 0.0).then_inc(s_pc, 1)
            pool.memset(before[:, :], 1.0).then_inc(s_pc, 1)
            pool.memset(onesb[:, :], 1.0).then_inc(s_pc, 1)
            pool.memset(neg_half[:, :], -0.5).then_inc(s_pc, 1)
            pool.memset(upto[:, :, :], 1.0).then_inc(s_pc, 1)
            pool.iota(iota_i[:, 0:E], pattern=[[1, E]], base=0, channel_multiplier=0).then_inc(s_pc, 1)
            pool.iota(iota_i[:, E:2 * E], pattern=[[ROWS, E]], base=0, channel_multiplier=0).then_inc(s_pc, 1)
            pool.iota(iota_i[:, 2 * E:2 * E + NT], pattern=[[2 * P, NT]], base=0, channel_multiplier=2).then_inc(s_pc, 1)
            pool.iota(iota_i[:, 3 * E:3 * E + 1], pattern=[[0, 1]], base=0, channel_multiplier=1).then_inc(s_pc, 1)
            pool.memset(pad_rows[:, 0:D], 0.0).then_inc(s_pc, 1)
            pool.memset(pad_rows[:, D:D + 1], float(SKIP)).then_inc(s_pc, 1)
            pool.memset(pad_rows[:, D + 1:D + 2], 0.0).then_inc(s_pc, 1)
            pool.wait_ge(s_pc, 13)
            pool.affine_select(out=ident[:, :], in_=ident[:, :], compare_op=ALU.not_equal, fill=1.0, base=0,
                               pattern=[[-1, P]], channel_multiplier=1).then_inc(s_pc, 1)
            pool.affine_select(out=maskneg[:, :, :], in_=maskneg[:, :, :], compare_op=ALU.is_ge, fill=MASKED, base=0,
                               pattern=[[0, 2], [-1, P]], channel_multiplier=1).then_inc(s_pc, 1)
            pool.affine_select(out=before[:, :], in_=before[:, :], compare_op=ALU.is_ge, fill=0.0, base=-1,
                               pattern=[[1, P]], channel_multiplier=-1).then_inc(s_pc, 1)
            pool.affine_select(out=upto[:, :, :], in_=upto[:, :, :], compare_op=ALU.is_ge, fill=0.0, base=0,
                               pattern=[[1, E], [-1, E]], channel_multiplier=0).then_inc(s_pc, 1)
            pool.tensor_copy(iota_e[:, :], iota_i[:, 0:E]).then_inc(s_pc, 1)
            pool.tensor_copy(region[:, :], iota_i[:, E:2 * E]).then_inc(s_pc, 1)
            pool.tensor_copy(base[:, :], iota_i[:, E:2 * E]).then_inc(s_pc, 1)
            pool.tensor_copy(res_row[:, :], iota_i[:, 2 * E:2 * E + NT]).then_inc(s_pc, 1)
            pool.tensor_copy(tile_no[:, :], iota_i[:, 3 * E:3 * E + 1]).then_inc(s_pc, 1)
            pool.wait_ge(s_pc, 22)
            pool.tensor_copy(identb[:, :], ident[:, :]).then_inc(s_const, 1)
            pool.wait_ge(s_const, 1)

            def step(b, pb, has):
                def do(name, k, g):
                    if name == "SPLIT":
                        n1, q = 4 * b + (4 + g), g % 2
                        pool.wait_ge(s_red, held(pool, 6 * n1 + 6))
                        pool.wait_ge(s_mt, held(pool, n1 - 1))
                        pool.tensor_copy(nsplit[q][:, 0, :, :], nmax[q][:, :, :]).then_inc(s_spl, 1)
                        pool.wait_ge(s_spl, held(pool, 4 * n1 + 1))
                        pool.tensor_tensor(nres[:, :, :], nmax[q][:, :, :], nsplit[q][:, 0, :, :], ALU.subtract).then_inc(s_spl, 1)
                        pool.wait_ge(s_spl, held(pool, 4 * n1 + 2))
                        pool.tensor_copy(nsplit[q][:, 1, :, :], nres[:, :, :]).then_inc(s_spl, 1)
                        pool.wait_ge(s_spl, held(pool, 4 * n1 + 3))
                        pool.tensor_tensor(nsplit[q][:, 2, :, :], nres[:, :, :], nsplit[q][:, 1, :, :], ALU.subtract).then_inc(s_spl, 1)
                    elif name == "SEL":
                        n = 4 * b + g
                        pool.wait_ge(s_e, held(pool, 11 * n + [4, 8, 10, 11][k]))
                        diag = prob_of[k][:, :, 0:P]
                        pool.affine_select(out=diag, in_=diag, compare_op=ALU.is_ge, fill=0.0, base=0,
                                           pattern=[[0, G], [1, P]], channel_multiplier=-1).then_inc(s_sel, 1)
                    elif name in ("Q2", "K2"):
                        n, c = b + k, int(name == "K2")
                        pool.wait_ge(s_mid, held(pool, 2 * n + c + 1))
                        pool.tensor_tensor(parts[c][:, 2, :], resid[:, :], parts[c][:, 1, :], ALU.subtract).then_inc(s_lo, 1)
                    elif name in ("LN1C", "LN2C", "LN3C"):
                        n, j = b + k, int(name[2]) - 1
                        pool.wait_ge(s_mv[j], held(pool, n + 1))
                        pool.wait_ge(s_norm[j], held(pool, n))
                        pool.tensor_scalar(veps[:, j, :], mv[:, j, :, 1], EPS, None, ALU.add).then_inc(s_coef[j], 1)
                        pool.wait_ge(s_coef[j], held(pool, 4 * n + 1))
                        pool.tensor_tensor(rstd[:, j, :], veps[:, j, :], neg_half[:, :], ALU.pow).then_inc(s_coef[j], 1)
                        pool.wait_ge(s_coef[j], held(pool, 4 * n + 2))
                        pool.tensor_tensor(nmr0[:, j, :], mv[:, j, :, 0], rstd[:, j, :], ALU.mult).then_inc(s_coef[j], 1)
                        pool.wait_ge(s_coef[j], held(pool, 4 * n + 3))
                        pool.tensor_scalar(nmr[:, j, :], nmr0[:, j, :], -1.0, None, ALU.mult).then_inc(s_coef[j], 1)
                        if j == 0 and isinstance(n, int) and n == 0:
                            pool.wait_ge(s_coef[j], 4)
                            for q in range(2):
                                pool.memset(qs[64:P, q, :, :].rearrange("p h t -> p (h t)").bitcast(F32), 0.0).then_inc(s_zq, 1)
                                pool.wait_ge(s_zq, q + 1)
                    elif name == "XB0":
                        n = b + k
                        pool.wait_ge(s_re, held(pool, 32 * n + 32))
                        pool.tensor_tensor(xnr[:, :, :], xnr[:, :, :], bprojb[:, None, :].to_broadcast([P, NT, D]), ALU.add).then_inc(s_xb, 1)
                    elif name == "XB1":
                        n = b + k
                        pool.tensor_tensor(xr[:, :, :], xr[:, :, :], betab[:, None, :].to_broadcast([P, NT, D]), ALU.add).then_inc(s_xb, 1)
                    elif name in ("X1A", "X1B") and isinstance(b, int) and b + k == B - 1:
                        pass
                    elif name == "X1A":
                        n = b + k
                        pool.wait_ge(s_norm[1], held(pool, n + 1))
                        pool.tensor_tensor(z[:, :, :], z[:, :, :], gammab[:, None, :].to_broadcast([P, NT, D]), ALU.mult).then_inc(s_x1, 1)
                    elif name == "X1B":
                        n = b + k
                        pool.wait_ge(s_x1, held(pool, 2 * n + 1))
                        pool.wait_ge(s_xb, held(pool, 2 * n + 2))
                        pool.wait_ge(s_norm[2], held(pool, n))
                        pool.wait_ge(s_x1d, held(pool, 16 * n))
                        pool.tensor_tensor(x1w[:, :, :], z[:, :, :], xr[:, :, :], ALU.add).then_inc(s_x1, 1)
                    elif name.startswith("SCATTER"):
                        n, q = b + k, (pb + k) % 2
                        pool.wait_ge(s_cs, held(pool, CS * n + 6))
                        pool.wait_ge(s_row, held(pool, n + 1))
                        i, c = divmod(int(name[-1]), 2)
                        pool.indirect_dma_start(
                            routed[:, :], bass.IndirectOffsetOnAxis(ap=dest[q][:, c, i:i + 1], axis=0),
                            rows[q][c][:, i, :], None).then_inc(s_sc[q], 16)
                    elif name == "LEFT":
                        n = b + k
                        pool.wait_ge(s_sc[pb], held(pool, 64 * (n - pb) + 128))
                walk(has, do)

            steps(pool, step)

            def store(t, q):
                pool.wait_ge(s_yg, held(pool, t + 1))
                pool.indirect_dma_start(results[:, :], bass.IndirectOffsetOnAxis(ap=ydest[q][:, 0:1], axis=0), yg[q % 2][:, :], None,
                                        bounds_check=2 * B * T - 1, oob_is_err=False).then_inc(s_ys[q % 2], 16)
            with pool.Fori(0, TILES, XG) as t:
                for q in range(XG):
                    store(t + q, q)

            for n in POOL_ADDS:
                pool.wait_ge(s_fin[n], 16)
                pool.tensor_tensor(fin[:, n, :, 0, :], fin[:, n, :, 0, :], fin[:, n, :, 1, :], ALU.add).then_inc(s_f1[n], 1)
                pool.wait_ge(s_f1[n], 1)
                pool.wait_ge(s_x1d, 16 * B)
                pool.tensor_tensor(x1[:, NT * n:NT * n + NT, :], x1[:, NT * n:NT * n + NT, :], fin[:, n, :, 0, :], ALU.add).then_inc(s_f2[n], 1)

        @block.scalar
        def _(act):

            def ones_rows(q):
                act.copy(ks[MROW:P, q, :, :].rearrange("p h t -> p (h t)").bitcast(F32),
                         ones_pair[MROW:P, 0:1].to_broadcast([P - MROW, H * T // 2])).then_inc(s_ok, 1)

            act.wait_ge(s_one, 1)
            ones_rows(0)

            def norm(j, n, dst, src, half):
                act.wait_ge(s_coef[j], 4 * n + 4)
                for i in range(2 * half, 2 * half + 2):
                    last = act.activation(dst[:, i, :], src[:, i, :], ACT.Identity, bias=nmr[:, j, i:i + 1], scale=rstd[:, j, i:i + 1])
                if half:
                    last.then_inc(s_norm[j], 1)

            def step(b, pb, has):
                def do(name, k, g):
                    n = b + k if isinstance(k, int) else None
                    if name == "S":
                        slot, i = 4 * b + g, k
                        kb, h = ([(0, j) for j in range(4)] + [(1, j) for j in range(4)] + [(2, 0), (2, 2), (3, 0)])[i]
                        nh = [1, 1, 2, 4][kb]
                        if h == 0:
                            act.wait_ge(s_pv, due(4 * slot - 3 + kb))
                        act.wait_ge(s_s, 11 * slot + i + 1)
                        act.activation(prob_of[kb][:, h:h + nh, :],
                                       pS[:, (g + i) % 2, 0:nh * QN[kb]].rearrange("p (h q) -> p h q", h=nh),
                                       ACT.Exp, scale=SCALE).then_inc(s_e, 1)
                    elif name == "OE":
                        slot = 4 * b + (g - 1)
                        act.wait_ge(s_pv, 4 * slot + 4)
                        act.wait_ge(s_nt, due(slot))
                        act.copy(oT[:, :], pO[:, :]).then_inc(s_oT, 1)
                    elif name == "M":
                        n1, q = 4 * b + (4 + g - 1), (g - 1) % 2
                        act.wait_ge(s_mt, n1 + 1)
                        act.wait_ge(s_mr[q], due(8 * (n1 - q)))
                        act.copy(nmT[q][:, :], pMb[0:3 * G * NT, 0:P]).then_inc(s_nmT, 1)
                    elif name == "X":
                        act.wait_ge(s_xt, n + 1)
                        act.wait_ge(s_vmm, due(n - 1))
                        act.copy(xnT[pb][:, :], pM[:, :]).then_inc(s_xnT, 1)
                    elif name in ("Q", "K"):
                        c = int(name == "K")
                        act.wait_ge(s_qk, 2 * n + c + 1)
                        parts_out, each = [(s_qout, 16), (s_kout, 32)][c]
                        act.wait_ge(parts_out, due(each * n))
                        act.copy(parts[c][:, 0, :], pM[:, :]).then_inc(s_hi, 1)
                    elif name in ("Q2", "K2"):
                        c = int(name == "K2")
                        act.wait_ge(s_res, 2 * n + c + 1)
                        act.copy(parts[c][:, 1, :], resid[:, :]).then_inc(s_mid, 1)
                        if c and isinstance(n, int) and n == 0:
                            ones_rows(1)
                    elif name == "V":
                        q = (pb + 1) % 2
                        act.wait_ge(s_vmm, n + 1)
                        act.wait_ge(s_pv, due(16 * (n - 1)))
                        act.copy(va[q][:, :, :, 0:HD], pM[:, :].rearrange("p (i h d) -> p i h d", i=NT, h=H)).then_inc(s_v, 1)
                    elif name in ("LN1N0", "LN1N1"):
                        act.wait_ge(s_xt, due(n))
                        act.wait_ge(s_xout, due(16 * n))
                        norm(0, n, xn, xin[pb], int(name[4]))
                    elif name in ("LN2N0", "LN2N1"):
                        norm(1, n, z, z, int(name[4]))
                    elif name in ("LN3N0", "LN3N1"):
                        q = (pb + 1) % 2
                        if isinstance(n, int):
                            act.wait_ge(s_sc[q], due(64 * (n - q)))
                        norm(2, n, rows[q][0][:, :, 0:D], x1w, int(name[4]))
                    elif name == "COPY":
                        q = (pb + k) % 2
                        act.wait_ge(s_norm[2], n + 1)
                        act.copy(rows[q][1][:, :, 0:D], rows[q][0][:, :, 0:D]).then_inc(s_row, 1)
                    elif name == "A":
                        act.wait_ge(s_at, n + 1)
                        act.wait_ge(s_pj, due(n))
                        act.copy(aT[:, :], pM[:, :]).then_inc(s_aT, 1)
                    elif name == "T":
                        act.wait_ge(s_tt, n + 1)
                        act.copy(tT[:, :], pM[:, :]).then_inc(s_tT, 1)
                    elif name == "TOP":
                        act.wait_ge(s_lg, LG * n + 3)
                        act.activation(pexp[:, :, :], lsub[:, :, :], ACT.Exp).then_inc(s_le, 1)
                walk(has, do)

            steps(act, step)

            act.wait_ge(s_tb, TB_PAD)
            for e in range(1, E, 2):
                at = act.value_load(pad_at[0:1, e:e + 1], min_val=0, max_val=(e + 1) * ROWS - P)
                act.dma_start(routed[bass.ds(at, P), :], pad_rows[:, :]).then_inc(s_pad, 16)
            act.wait_ge(s_b1, 1)

            def rows_T(t, q):
                act.wait_ge(s_gt, t + 1)
                if not isinstance(t, int) or t >= 2:
                    act.wait_ge(s_h, due(t - 1))
                act.copy(xgT[q % 2][:, :], pM[:, 0:P]).then_inc(s_gT, 1)

            def tile(t, q):
                act.wait_ge(s_h, t + 1)
                if not isinstance(t, int) or t >= 2:
                    act.wait_ge(s_y, due(t - 1))
                for c in range(HC // 2):
                    last = act.activation(hid[q % 2][:, c, :], hidden(c, q), ACT.Relu, bias=w1c[q][:, HID + c:HID + c + 1])
                last.then_inc(s_ha, 1)

            def gate(t, q):
                act.wait_ge(s_yb, t + 1)
                if not isinstance(t, int) or t >= 2:
                    act.wait_ge(s_ys[q % 2], due(8 * (t - q % 2)))
                act.activation(yg[q % 2][:, :], yb[q % 2][:, :], ACT.Identity, scale=ygate[q][:, :]).then_inc(s_yg, 1)

            act.wait_ge(s_tb, TB_END)
            rows_T(0, 0)
            rows_T(1, 1)
            tile(0, 0)
            for t in range(XG):
                rows_T(t + 2, (t + 2) % XG)
                tile(t + 1, (t + 1) % XG)
                gate(t, t)
            with act.Fori(XG, TILES - XG, XG) as t:
                for q in range(XG):
                    rows_T(t + (q + 2), (q + 2) % XG)
                    tile(t + (q + 1), (q + 1) % XG)
                    gate(t + q, q)
            for t in range(TILES - XG, TILES):
                if t + 2 < TILES:
                    rows_T(t + 2, (t + 2) % XG)
                if t + 1 < TILES:
                    tile(t + 1, (t + 1) % XG)
                gate(t, t % XG)

        @block.tensor
        def _(pe):
            last_use = [(s_const, 1)]

            def last_left(s, n):
                before_, last_use[0] = last_use[0], (s, n)
                return before_

            pe.wait_ge(s_const, 1)
            pe.wait_ge(s_w, 16 * 8)
            pe.wait_ge(*last_left(s_b1, 1))
            pe.transpose(pM[:, 0:E * HC], b1row[:, :], ident[0:E * HC, 0:E * HC]).then_inc(s_b1t, 1)
            pe.wait_ge(s_zero, 1)
            pe.wait_ge(s_wperm, 2)

            def turn(src, s):
                for i in range(NT):
                    last = pe.transpose(pM[:, i * P:(i + 1) * P], src(i), ident[:, :])
                last.then_inc(s, 1)

            def step(b, pb, has):
                if has is not None and has(0):
                    last_use[0] = (s_v, b + 1)

                def pv(slot, j, gm, kb, pvp):
                    pe.wait_ge(s_sel, 4 * slot + kb + 1)
                    if kb == 0:
                        pe.wait_ge(s_oT, due(slot))
                    for h in range(G):
                        last = pe.matmul(pO[32 * h:32 * h + HD + 1, kb * P:T], va[pvp][:, kb, G * gm + h, :], prob_of[kb][:, h, :],
                                         start=(kb == 0), stop=(kb == NT - 1), skip_group_check=True)
                    last.then_inc(s_pv, 1)

                def do(name, k, g):
                    n = b + k
                    if name == "S":
                        slot, i = 4 * b + g, k
                        if i == 0:
                            if g == 0 and isinstance(b, int) and b < 2:
                                pe.wait_ge(s_ok, b + 1)
                            pe.wait_ge(s_mr[g % 2], due(8 * (slot - g % 2) + 16))
                        pe.wait_ge(s_e, due(11 * slot + i - 1))
                        kb, h = ([(0, j) for j in range(4)] + [(1, j) for j in range(4)] + [(2, 0), (2, 2), (3, 0)])[i]
                        nh = [1, 1, 2, 4][kb]
                        for j in range(nh):
                            last = pe.matmul(pS[:, (g + i) % 2, j * QN[kb]:(j + 1) * QN[kb]],
                                             ks[:, pb, G * g + h + j, kb * P:(kb + 1) * P],
                                             qs[:, pb, G * g + h + j, kb * P:T], start=True, stop=True)
                        last.then_inc(s_s, 1)
                    elif name == "U":
                        u, slot = k, 4 * b + (4 + g)
                        q, p1 = u % 2, (pb + 1) % 2
                        if u == 0:
                            pe.wait_ge(s_st[g // 2], ST * b + 2 * ST)
                        pe.wait_ge(s_red, due(6 * slot + u - 1))
                        pair, kind = u // 3, u % 3

                        def scores(dst, h, qt, start):
                            pe.matmul(dst, qs[0:MROW, p1, h, qt * P:(qt + 1) * P], ks[0:MROW, p1, h, 0:(qt + 1) * P],
                                      start=start, stop=False, skip_group_check=True)

                        def mask(dst, m):
                            return pe.matmul(dst, identb[:, :], maskneg[:, 0:m, :], start=False, stop=True, skip_group_check=True)

                        for j in range(2):
                            h = G * g + 2 * pair + j
                            if kind == 0:
                                scores(pU[:, q, j, :], h, 3, True)
                                last = mask(pU[:, q, j, 3 * P:4 * P], 1)
                            elif kind == 1:
                                scores(pU[:, q, j, 0:3 * P], h, 2, True)
                                scores(pU[:, q, j, 3 * P:4 * P], h, 0, False)
                                last = mask(pU[:, q, j, 2 * P:4 * P], 2)
                            else:
                                scores(pU[:, q, 0, 2 * j * P:(2 * j + 2) * P], h, 1, j == 0)
                                if j:
                                    last = mask(pU[:, q, 0, :].rearrange("p (h b k) -> p h b k", h=2, b=2)[:, :, 1, :], 2)
                        last.then_inc(s_u, 1)
                    elif name == "PV":
                        if k == 0 and g == 0:
                            pe.wait_ge(s_v, b + 1)
                        pv(4 * b + g, None, g, k, pb)
                    elif name == "PVL":
                        pv(4 * b + (g - 1), None, (g - 1) % 4, k, pb if g else (pb + 1) % 2)
                    elif name == "M":
                        n1, q = 4 * b + (4 + g - 1), (g - 1) % 2
                        left, at = last_left(s_nmT, n1 + 1)
                        at = pe.to_reg(at) if not isinstance(at, int) else at
                        pe.wait_ge(s_spl, held(pe, 4 * n1 + 4))
                        pe.wait_ge(left, at)
                        pe.transpose(pMb[0:3 * G * NT, 0:P], nsplit[q][:, :, :, :].rearrange("p c h i -> p (c h i)"), identb[:, :])\
                            .then_inc(s_mt, 1)
                    elif name == "N":
                        slot = 4 * b + (g - 1)
                        pe.wait_ge(s_oT, slot + 1)
                        pe.wait_ge(*last_left(s_n, slot + 1))
                        turn(lambda i: oT[:, i * P:(i + 1) * P], s_nt)
                    elif name == "X":
                        pe.wait_ge(s_norm[0], n + 1)
                        pe.wait_ge(*last_left(s_xnT, n + 1))
                        turn(lambda i: xn[:, i, :], s_xt)
                    elif name in ("Q", "K"):
                        c = int(name == "K")
                        pe.wait_ge(s_xnT, n + 1)
                        pe.wait_ge(*last_left(s_res, 2 * n + c + 1))
                        pe.matmul(pM[:, :], (wk_p if c else wq_p)[:, :], xnT[pb][:, :], start=True, stop=True).then_inc(s_qk, 1)
                    elif name == "V":
                        pe.wait_ge(*last_left(s_v, n + 1))
                        for i in range(NT):
                            last = pe.matmul(pM[:, i * P:(i + 1) * P], xnT[(pb + 1) % 2][:, i * P:(i + 1) * P], w_raw[:, 2 * D:3 * D], start=True, stop=True)
                        last.then_inc(s_vmm, 1)
                    elif name == "A":
                        q = (pb + 1) % 2
                        pe.wait_ge(s_n, 4 * n + 4)
                        pe.wait_ge(*last_left(s_aT, n + 1))
                        turn(lambda i: on[q][:, i, :], s_at)
                    elif name == "PROJ":
                        pe.wait_ge(s_aT, n + 1)
                        pe.wait_ge(*last_left(s_z, n + 1))
                        for i in range(NT):
                            last = pe.matmul(pM[:, i * P:(i + 1) * P], aT[:, i * P:(i + 1) * P], wp[:, :], start=True, stop=True)
                        last.then_inc(s_pj, 1)
                    elif name == "T":
                        pe.wait_ge(s_norm[2], n + 1)
                        pe.wait_ge(*last_left(s_tT, n + 1))
                        turn(lambda i: rows[(pb + k) % 2][0][:, i, 0:D], s_tt)
                    elif name == "R":
                        pe.wait_ge(s_tT, n + 1)
                        pe.wait_ge(*last_left(s_lg, LG * n + 1))
                        for i in range(NT):
                            last = pe.matmul(pM[:, i * E:(i + 1) * E], tT[:, i * P:(i + 1) * P], wr[:, :], start=True, stop=True)
                        last.then_inc(s_r, 1)
                    elif name == "C":
                        pe.wait_ge(s_lg, LG * n + 11)
                        pe.wait_ge(*last_left(s_cs, CS * n + 2))
                        for i in range(NT):
                            pe.matmul(pM[:, i * E:(i + 1) * E], before[:, :], hotb[:, i, :], start=(i == 0), stop=False, skip_group_check=True)
                            for j in range(i):
                                pe.matmul(pM[:, i * E:(i + 1) * E], onesb[:, :], hotb[:, j, :], start=False, stop=False, skip_group_check=True)
                        for j in range(NT):
                            last = pe.matmul(pM[:, NT * E:(NT + 1) * E], onesb[:, :], hotb[:, j, :], start=False, stop=(j == NT - 1), skip_group_check=True)
                        last.then_inc(s_cp, 1)
                walk(has, do)

            steps(pe, step)

            pe.wait_ge(s_tb, TB_COLS)
            pe.wait_ge(*last_use[0])
            for j in range(2):
                last = pe.matmul(pM[0:1, j * P:(j + 1) * P], tv[:, 4 + j:5 + j], ident[:, :], start=True, stop=True)
            last.then_inc(s_tm, 1)
            pe.wait_ge(s_tb, TB_END)
            pe.wait_ge(s_w1, 16 * 4)
            pe.wait_ge(s_w2, 16 * 5)

            def experts(t):
                word = pe.value_load(table[0:1, 0, t:t + 1] if isinstance(t, int) else table[0:1, 0, bass.ds(t, 1)],
                                     min_val=0, max_val=E ** 4 - 1)
                return [(word // E ** j) % E for j in range(XG)]

            def turn_rows(t, q):
                pe.wait_ge(s_g[q], due(4 * (t - q) + 16))
                pe.wait_ge(s_gT, due(t))
                pe.transpose(pM[:, 0:P], xg[q][:, 0:D], ident[:, :]).then_inc(s_gt, 1)

            def first(t, q):
                pe.wait_ge(s_gT, t + 1)
                pe.wait_ge(s_wc, t + 1)
                if not isinstance(t, int) or t >= 2:
                    pe.wait_ge(s_ha, due(t - 1))
                    pe.wait_ge(s_hv, due(t - 1))
                for c in range(HC):
                    last = pe.matmul(hidden(c, q), w1c[q][:, c * P:(c + 1) * P],
                                     xgT[q % 2][:, :], start=True, stop=True)
                last.then_inc(s_h, 1)

            def second(t, q, e):
                pe.wait_ge(s_ha, t + 1)
                pe.wait_ge(s_hv, t + 1)
                if not isinstance(t, int) or t >= 2:
                    pe.wait_ge(s_yb, due(t - 1))
                for c in range(HC):
                    last = pe.matmul(pS[:, q % 2, 0:D], hid[q % 2][:, c, :], w2s[:, bass.ds(e, 1), c, :].rearrange("p e m -> p (e m)"), start=(c == 0), stop=(c == HC - 1))
                last.then_inc(s_y, 1)

            turn_rows(0, 0)
            first(0, 0)
            turn_rows(1, 1)
            e = experts(0)
            for t in range(XG):
                turn_rows(t + 2, (t + 2) % XG)
                first(t + 1, (t + 1) % XG)
                second(t, t, e[t])
            with pe.Fori(XG, TILES - XG, XG) as t:
                for q in range(XG):
                    turn_rows(t + (q + 2), (q + 2) % XG)
                    first(t + (q + 1), (q + 1) % XG)
                    if q == 0:
                        e = experts(t)
                    second(t + q, q, e[q])
            e = experts(TILES - XG)
            for t in range(TILES - XG, TILES):
                if t + 2 < TILES:
                    turn_rows(t + 2, (t + 2) % XG)
                if t + 1 < TILES:
                    first(t + 1, (t + 1) % XG)
                second(t, t % XG, e[t % XG])

        @block.vector
        def _(dve):
            dve.memset(ones_pair[:, :], ONES_PAIR).then_inc(s_one, 1)
            for tile_ in va:
                dve.memset(tile_[:, :, :, HD:HD + 1], 1.0)
            dve.memset(pO[:, :], 0.0).then_inc(s_zero, 1)
            dve.wait_ge(s_const, 1)

            def zero_k(q):
                dve.memset(ks[64:MROW, q, :, :].rearrange("p h t -> p (h t)").bitcast(F32), 0.0).then_inc(s_zk, 1)

            def prepare():
                dve.wait_ge(s_w, 16 * 8)
                for j, w in enumerate((wq_p, wk_p)):
                    dve.tensor_copy(w[:, :].rearrange("p (g d h) -> p g d h", g=2, d=HD),
                                    w_raw[:, j * D:(j + 1) * D].rearrange("p (g h d) -> p g d h", g=2, h=HH)).then_inc(s_wperm, 1)
                dve.wait_ge(s_b1t, 1)
                dve.tensor_copy(w1s[:, :, HID:HID + HC], pM[:, 0:E * HC].rearrange("p (e c) -> p e c", e=E)).then_inc(s_b1, 1)
                zero_k(0)

            def step(b, pb, has):
                def do(name, k, g):
                    n = b + k
                    if name == "U":
                        u, slot, q = k, 4 * b + (4 + g), g % 2
                        if u == 0:
                            dve.wait_ge(s_spl, due(4 * slot - 4))
                        dve.wait_ge(s_u, 6 * slot + u + 1)
                        pair, kind = u // 3, u % 3
                        hs = slice(2 * pair, 2 * pair + 2)
                        if kind == 0:
                            last = dve.tensor_reduce(nmax[q][:, hs, 3], pU[:, u % 2, :, :], AX.X, ALU.max, negate=True)
                        elif kind == 1:
                            dve.tensor_reduce(nmax[q][:, hs, 2], pU[:, u % 2, :, 0:3 * P], AX.X, ALU.max, negate=True)
                            last = dve.tensor_reduce(nmax[q][:, hs, 0], pU[:, u % 2, :, 3 * P:4 * P], AX.X, ALU.max, negate=True)
                        else:
                            last = dve.tensor_reduce(nmax[q][:, hs, 1], pU[:, u % 2, 0, :].rearrange("p (h k) -> p h k", h=2), AX.X, ALU.max, negate=True)
                        last.then_inc(s_red, 1)
                    elif name == "N":
                        slot, gm, q = 4 * b + (g - 1), (g - 1) % 4, pb if g else (pb + 1) % 2
                        o4 = pM[:, :].rearrange("p (i h c) -> p i h c", i=NT, h=G)
                        dve.wait_ge(s_nt, slot + 1)
                        dve.reciprocal(rsum[:, :, :], o4[:, :, :, HD]).then_inc(s_rs, 1)
                        dve.wait_ge(s_rs, slot + 1)
                        if gm == 0:
                            dve.wait_ge(s_at, due((b if g else b - 1) - 1))
                        dve.tensor_tensor(on[q][:, :, 32 * gm:32 * gm + 32].rearrange("p i (h d) -> p i h d", h=G), o4[:, :, :, 0:HD],
                                          rsum[:, :, :, None].to_broadcast([P, NT, G, HD]), ALU.mult).then_inc(s_n, 1)
                    elif name in ("Q", "K"):
                        c = int(name == "K")
                        dve.wait_ge(s_hi, 2 * n + c + 1)
                        dve.wait_ge(s_lo, 2 * n + c)
                        dve.tensor_tensor(resid[:, :], pM[:, :], parts[c][:, 0, :], ALU.subtract).then_inc(s_res, 1)
                        if c and isinstance(n, int) and n == 0:
                            zero_k(1)
                    elif name in ("LN1S0", "LN1S1", "LN2S0", "LN2S1", "LN3S0", "LN3S1"):
                        j, half = int(name[2]) - 1, int(name[4])
                        if j == 0:
                            src = xin[pb]
                            dve.wait_ge(s_x[pb], due(8 * (n - pb) + 16))
                        elif j == 1:
                            src = z
                            dve.wait_ge(s_z, n + 1)
                        else:
                            src = x1w
                            dve.wait_ge(s_x1, 2 * n + 2)
                        for i in range(2 * half, 2 * half + 2):
                            last = dve.bn_stats(stats[:, j, i, :], src[:, i, :])
                        if not half:
                            return
                        last.then_inc(s_stat[j], 1)
                        dve.wait_ge(s_coef[j], held(dve, 4 * n))
                        dve.wait_ge(s_stat[j], held(dve, n + 1))
                        for i in range(NT):
                            last = dve.bn_aggr(mv[:, j, i, :], stats[:, j, i, :])
                        last.then_inc(s_mv[j], 1)
                        if j == 0 and isinstance(n, int) and n == 0:
                            prepare()
                    elif name == "PROJ":
                        dve.wait_ge(s_pj, n + 1)
                        dve.wait_ge(s_xb, 2 * n + 1)
                        dve.wait_ge(s_x1, due(2 * n))
                        dve.tensor_tensor(z[:, :, :], pM[:, :].rearrange("p (i d) -> p i d", i=NT), xnr[:, :, :], ALU.add).then_inc(s_z, 1)
                    elif name == "X1A" and isinstance(n, int) and n == B - 1:
                        dve.wait_ge(s_norm[1], n + 1)
                        dve.tensor_tensor(z[:, :, :], z[:, :, :], gammab[:, None, :].to_broadcast([P, NT, D]), ALU.mult).then_inc(s_x1, 1)
                    elif name == "X1B" and isinstance(n, int) and n == B - 1:
                        dve.wait_ge(s_x1, 2 * n + 1)
                        dve.wait_ge(s_xb, 2 * n + 2)
                        dve.wait_ge(s_norm[2], n)
                        dve.wait_ge(s_x1d, 16 * n)
                        dve.tensor_tensor(x1w[:, :, :], z[:, :, :], xr[:, :, :], ALU.add).then_inc(s_x1, 1)
                    elif name == "R":
                        a = LG * n
                        dve.wait_ge(s_r, n + 1)
                        dve.tensor_tensor(logit[:, :, :], pM[:, 0:NT * E].rearrange("p (i e) -> p i e", i=NT),
                                          brb[:, None, :].to_broadcast([P, NT, E]), ALU.add).then_inc(s_lg, 1)
                        dve.wait_ge(s_lg, a + 1)
                        dve.tensor_reduce(lmax[:, :], logit[:, :, :], AX.X, ALU.max, negate=True).then_inc(s_lg, 1)
                        dve.wait_ge(s_lg, a + 2)
                        dve.tensor_tensor(lsub[:, :, :], logit[:, :, :], lmax[:, :, None].to_broadcast([P, NT, E]), ALU.add).then_inc(s_lg, 1)
                    elif name == "TOP":
                        a = LG * n
                        dve.wait_ge(s_le, n + 1)
                        dve.tensor_reduce(prob_sum[:, :], pexp[:, :, :], AX.X, ALU.add).then_inc(s_lg, 1)
                        dve.wait_ge(s_lg, a + 4)
                        dve.reciprocal(prec[:, :], prob_sum[:, :]).then_inc(s_lg, 1)
                        dve.wait_ge(s_lg, a + 5)
                        dve.tensor_tensor(prob[:, :, :], pexp[:, :, :], prec[:, :, None].to_broadcast([P, NT, E]), ALU.mult).then_inc(s_lg, 1)
                        dve.wait_ge(s_lg, held(dve, a + 6))
                        for i in range(NT):
                            last = dve.max(top_v[:, i, :], prob[:, i, :])
                        last.then_inc(s_lg, 1)
                        dve.wait_ge(s_lg, held(dve, a + 7))
                        for i in range(NT):
                            last = dve.max_index(top_i[:, i, :], top_v[:, i, :], prob[:, i, :])
                        last.then_inc(s_lg, 1)
                        dve.wait_ge(s_lg, a + 8)
                        dve.tensor_copy(top_f[:, :, :], top_i[:, :, :]).then_inc(s_lg, 1)
                        dve.wait_ge(s_lg, a + 9)
                        for c in range(2):
                            last = dve.tensor_tensor(hot[:, c, :, :], iota_e[:, None, :].to_broadcast([P, NT, E]),
                                                     top_f[:, :, c:c + 1].to_broadcast([P, NT, E]), ALU.is_equal)
                        last.then_inc(s_lg, 1)
                        dve.wait_ge(s_lg, a + 10)
                        dve.tensor_tensor(hotb[:, :, :], hot[:, 0, :, :], hot[:, 1, :, :], ALU.add).then_inc(s_lg, 1)
                    elif name == "C":
                        a, q = CS * n, (pb + k) % 2
                        dve.wait_ge(s_cp, n + 1)
                        dve.tensor_tensor(place[:, :, :], pM[:, 0:NT * E].rearrange("p (i e) -> p i e", i=NT),
                                          base[:, None, :].to_broadcast([P, NT, E]), ALU.add).then_inc(s_cs, 1)
                        dve.wait_ge(s_cs, a + 1)
                        dve.tensor_tensor(base[:, :], pM[:, NT * E:(NT + 1) * E], base[:, :], ALU.add).then_inc(s_cs, 1)
                        dve.wait_ge(s_cs, a + 2)
                        for c in range(2):
                            last = dve.tensor_tensor(picked[:, c, :, :], place[:, :, :], hot[:, c, :, :], ALU.mult)
                        last.then_inc(s_cs, 1)
                        dve.wait_ge(s_cs, a + 3)
                        dve.tensor_reduce(dest_f[:, :, :], picked[:, :, :, :], AX.X, ALU.add).then_inc(s_cs, 1)
                        dve.wait_ge(s_cs, a + 4)
                        if isinstance(n, int):
                            dve.wait_ge(s_sc[q], due(64 * (n - q)))
                        dve.tensor_copy(dest[q][:, :, :], dest_f[:, :, :]).then_inc(s_cs, 1)
                        for c in range(2):
                            dve.tensor_copy(rows[q][c][:, :, D + 1], top_v[:, :, c])
                            last = dve.tensor_scalar(rows[q][c][:, :, D], res_row[:, :], float(c), None, ALU.add)
                        last.then_inc(s_cs, 1)
                        dve.wait_ge(s_cs, a + 6)
                        dve.tensor_scalar(res_row[:, :], res_row[:, :], float(2 * T), None, ALU.add).then_inc(s_cs, 1)
                        dve.wait_ge(s_cs, a + 7)
                walk(has, do)

            steps(dve, step)

            dve.wait_ge(s_cs, CS * B)
            link = [0]

            def chain(ins):
                link[0] += 1
                ins.then_inc(s_tb, 1)
                dve.wait_ge(s_tb, link[0])

            chain(dve.tensor_copy(pad_at[:, :], base[0:1, :]))
            assert link[0] == TB_PAD
            chain(dve.tensor_tensor(cnt[:, :], base[:, :], region[:, :], ALU.subtract))
            chain(dve.tensor_scalar(cnt_i[:, :], cnt[:, :], float(P - 1), None, ALU.add))
            chain(dve.tensor_scalar(nt_i[:, :], cnt_i[:, :], 7, None, ALU.arith_shift_right))
            chain(dve.tensor_copy(nt_f[:, :], nt_i[:, :]))
            chain(dve.tensor_tensor(cum3[:, :, :], upto[:, :, :], nt_f[:, None, :].to_broadcast([P, E, E]), ALU.mult))
            chain(dve.tensor_reduce(cum[:, :], cum3[:, :, :], AX.X, ALU.add))
            chain(dve.tensor_scalar(done[:, :], cum[:, :], tile_no[:, 0:1], None, ALU.is_le))
            chain(dve.tensor_reduce(tv[:, 0:1], done[:, :], AX.X, ALU.add))
            chain(dve.tensor_tensor(skipped[:, :], done[:, :], nt_f[:, :], ALU.mult))
            chain(dve.tensor_reduce(tv[:, 1:2], skipped[:, :], AX.X, ALU.add))
            chain(dve.tensor_tensor(tv[:, 2:3], tile_no[:, :], tv[:, 1:2], ALU.subtract))
            chain(dve.tensor_scalar(tv[:, 3:4], tv[:, 0:1], float(E), float(P), ALU.is_lt, ALU.mult))
            chain(dve.tensor_tensor(tv[:, 2:3], tv[:, 2:3], tv[:, 3:4], ALU.mult))
            chain(dve.tensor_scalar(tv[:, 4:5], tv[:, 0:1], float(E - 1), None, ALU.min))
            chain(dve.scalar_tensor_tensor(out=tv[:, 5:6], in0=tv[:, 0:1], scalar=float(ROWS), in1=tv[:, 2:3], op0=ALU.mult, op1=ALU.add))
            assert link[0] == TB_COLS
            dve.wait_ge(s_tm, 1)
            chain(dve.tensor_copy(table_f[:, :, :], pM[0:1, 0:2 * P].rearrange("p (j t) -> p j t", j=2)))
            for d in (1, 2):
                n = P - d
                chain(dve.scalar_tensor_tensor(out=table_f[:, 0, 0:n], in0=table_f[:, 0, d:P], scalar=float(E ** d),
                                               in1=table_f[:, 0, 0:n], op0=ALU.mult, op1=ALU.add))
            chain(dve.tensor_copy(table[:, :, :], table_f[:, :, :]))
            assert link[0] == TB_END
            dve.wait_ge(s_w2, 16 * 5)
            dve.wait_ge(s_w1, 16 * 4)

            def experts(t):
                word = dve.value_load(table[0:1, 0, t:t + 1] if isinstance(t, int) else table[0:1, 0, bass.ds(t, 1)],
                                      min_val=0, max_val=E ** 4 - 1)
                return [(word // E ** j) % E for j in range(XG)]

            def weights(t, q, e):
                if not isinstance(t, int) or t >= XG:
                    dve.wait_ge(s_ha, due(t - XG + 1))
                    dve.wait_ge(s_hv, due(t - XG + 1))
                    dve.wait_ge(s_yb, due(t - XG + 1))
                dve.tensor_copy(w1c[q][:, :], w1s[:, bass.ds(e, 1), :].rearrange("p e h -> p (e h)")).then_inc(s_wc, 1)
                dve.tensor_copy(b2c[q], b2b[:, bass.ds(e, 1), :].rearrange("p e m -> p (e m)")).then_inc(s_bc, 1)

            def last_columns(t, q):
                dve.wait_ge(s_g[q], due(4 * (t - q) + 16))
                if not isinstance(t, int) or t >= XG:
                    dve.wait_ge(s_ys[q % 2], due(8 * (t - XG - q % 2) + 16))
                    dve.wait_ge(s_yg, due(t - XG + 1))
                dve.tensor_copy(ydest[q][:, :], xg[q][:, D:D + 1])
                dve.tensor_copy(ygate[q][:, :], xg[q][:, D + 1:D + 2]).then_inc(s_yi, 1)

            def act_half(t, q):
                dve.wait_ge(s_h, t + 1)
                if not isinstance(t, int) or t >= 2:
                    dve.wait_ge(s_y, due(t - 1))
                for c in range(HC // 2, HC):
                    last = dve.tensor_scalar(hid[q % 2][:, c, :], hidden(c, q), w1c[q][:, HID + c:HID + c + 1], 0.0, ALU.add, ALU.max)
                last.then_inc(s_hv, 1)

            def bias(t, q):
                dve.wait_ge(s_y, t + 1)
                dve.wait_ge(s_bc, t + 1)
                if not isinstance(t, int) or t >= 2:
                    dve.wait_ge(s_yg, due(t - 1))
                dve.tensor_tensor(yb[q % 2][:, :], pS[:, q % 2, 0:D], b2c[q], ALU.add).then_inc(s_yb, 1)

            e = experts(0)
            for t in range(XG - 1):
                if t == 2:
                    for q in range(2):
                        dve.wait_ge(s_sc[q], 16 * 2 * NT * B // 2)
                weights(t, t, e[t])
            for t in range(2):
                last_columns(t, t)
            act_half(0, 0)
            e = experts(XG - 1)
            for t in range(XG):
                act_half(t + 1, (t + 1) % XG)
                bias(t, t)
                last_columns(t + 2, (t + 2) % XG)
                weights(t + 3, (t + 3) % XG, e[t])
            with dve.Fori(XG, TILES - XG, XG) as t:
                for q in range(XG):
                    act_half(t + (q + 1), (q + 1) % XG)
                    bias(t + q, q)
                    last_columns(t + (q + 2), (q + 2) % XG)
                    if q == 0:
                        e = experts(t + 3)
                    weights(t + (q + 3), (q + 3) % XG, e[q])
            e = experts(TILES - 1)
            for t in range(TILES - XG, TILES):
                if t + 1 < TILES:
                    act_half(t + 1, (t + 1) % XG)
                bias(t, t % XG)
                if t + 2 < TILES:
                    last_columns(t + 2, (t + 2) % XG)
                if t + 3 < TILES:
                    weights(t + 3, (t + 3) % XG, e[t % XG])

            for n in range(B):
                if n in POOL_ADDS:
                    continue
                dve.wait_ge(s_fin[n], 16)
                dve.tensor_tensor(fin[:, n, :, 0, :], fin[:, n, :, 0, :], fin[:, n, :, 1, :], ALU.add).then_inc(s_f1[n], 1)
                dve.wait_ge(s_f1[n], 1)
                dve.wait_ge(s_x1d, 16 * B)
                dve.tensor_tensor(x1[:, NT * n:NT * n + NT, :], x1[:, NT * n:NT * n + NT, :], fin[:, n, :, 0, :], ALU.add).then_inc(s_f2[n], 1)


_INS = ["L0_attn_target", "L0_attn_w_qkv", "L0_attn_w_proj", "L0_attn_b_proj", "L0_attn_ln_gamma", "L0_attn_ln_beta",
        "L0_ffn_Wr", "L0_ffn_br", "L0_ffn_W1", "L0_ffn_b1", "L0_ffn_W2", "L0_ffn_b2"]


def kernel(**inputs):
    import numpy as np
    import concourse.bacc as bacc
    from concourse.bass_utils import run_bass_kernel_spmd

    nc = bacc.Bacc("TRN2", target_bir_lowering=False, num_devices=1)
    arrays, args = {}, []
    for name in _INS:
        a = np.ascontiguousarray(inputs[name])
        arrays[name] = a
        args.append(nc.dram_tensor(name, a.shape, mybir.dt.from_np(a.dtype), kind="ExternalInput").ap())
    shape = inputs["L0_attn_target"].shape
    args.append(nc.dram_tensor("out", shape, F32, kind="ExternalOutput").ap())
    moe_block(nc, *args)
    return run_bass_kernel_spmd(nc, [arrays], core_ids=[0]).results[0]["out"]
```
